# Optimizing a Trainium2 kernel written in Bass

```python
import numpy as np
import jax
import jax.numpy as jnp

def _softmax(x, axis=-1):
    return jax.nn.softmax(x, axis=axis)

def _gelu(x):
    return jax.nn.gelu(x, approximate=True)

def _silu(x):
    return jax.nn.silu(x)

def _sigmoid(x):
    return jax.nn.sigmoid(x)

def _layernorm(x, axis=-1, eps=1e-05):
    m = jnp.mean(x, axis=axis, keepdims=True)
    v = jnp.var(x, axis=axis, keepdims=True)
    return (x - m) / jnp.sqrt(v + eps)

def _scatter_add(tgt, idx, src, axis=0):
    return tgt.at[idx].add(src)

def _segment_sum(src, seg, n):
    return jax.ops.segment_sum(src, seg, n)
kernel_name = 'mk_xattn_seq_d2_seqx_r2_bb009b'

def setup_inputs(seed: int=0):
    np.random.seed(seed)
    _w = jnp.asarray

    def _rec_inputs():
        import jax
        import jax.numpy as jnp
        _rk = jax.random.key(seed)
        x = -0.0002928 + 1 * jax.random.normal(jax.random.fold_in(_rk, 1), (2, 2048, 512), jnp.float32)
        _lenS = 2048 - jax.random.randint(jax.random.fold_in(_rk, 7), (2,), 0, max(1, 2048 // 4) + 1, jnp.int32)
        _lenS2 = 77 - jax.random.randint(jax.random.fold_in(_rk, 8), (2,), 0, max(1, 77 // 4) + 1, jnp.int32)
        _ctx_1024P = jax.random.normal(jax.random.fold_in(_rk, 11), (2, 16, 512), jnp.float32)
        _ctx_1024c = jax.random.dirichlet(jax.random.fold_in(_rk, 511), 0.3 * jnp.ones((16,), jnp.float32), (2, 77))
        _ctx_1024t = jnp.einsum('bsk,bkd->bsd', _ctx_1024c, _ctx_1024P)
        _ctx_1024t = _ctx_1024t * jax.lax.rsqrt(jnp.mean(jnp.square(_ctx_1024t)) + 1e-12) * 0.953939
        ctx_1024 = -1.39393e-06 + 0.999914 * (_ctx_1024t + 0.3 * jax.random.normal(jax.random.fold_in(_rk, 611), (2, 77, 512), jnp.float32))
        _validS = jnp.arange(2048)[None, :] < _lenS[:, None]
        _validS2 = jnp.arange(77)[None, :] < _lenS2[:, None]
        _causal = jnp.tril(jnp.ones((2048, 2048), dtype=bool))
        mask_SxS_ik1 = jnp.where(jnp.broadcast_to(_validS[0:1, :], (2048, 2048)), 1, 0).astype(jnp.int32)
        mask_BxS2_ik0 = jnp.where(jnp.broadcast_to(_validS2[:, :], (2, 77)), 0, 1).astype(jnp.int32)
        return (x, ctx_1024, mask_SxS_ik1, mask_BxS2_ik0)
    x, ctx_1024, mask_SxS_ik1, mask_BxS2_ik0 = _rec_inputs()

    def _L0_xattn_setup():
        import jax, jax.numpy as jnp
        import numpy as np
        D_MODEL = 512
        N_HEAD = 16
        D_FF = 2048
        EPS = 1e-05

        def _linear(x, w, b):
            return jnp.einsum('bli,io->blo', x, w) + b

        def _layernorm(x, g, b):
            mu = jnp.mean(x, -1, keepdims=True)
            var = jnp.mean(jnp.square(x - mu), -1, keepdims=True)
            return (x - mu) * jax.lax.rsqrt(var + EPS) * g + b

        def _attention(q, k, v, mask):
            B, Lq, D = q.shape
            H = N_HEAD
            hd = D // H
            qh = q.reshape(B, Lq, H, hd)
            kh = k.reshape(B, k.shape[1], H, hd)
            vh = v.reshape(B, v.shape[1], H, hd)
            scores = jnp.einsum('bqhd,bkhd->bhqk', qh, kh) / jnp.sqrt(jnp.float32(hd)).astype(q.dtype)
            if mask is not None:
                scores = jnp.where(mask[None, None] != 0, jnp.finfo(scores.dtype).min, scores)
            p = jax.nn.softmax(scores, axis=-1)
            out = jnp.einsum('bhqk,bkhd->bqhd', p, vh).reshape(B, Lq, D)
            return out
        key = jax.random.key(seed)
        ks = jax.random.split(key, 32)
        B, L, S, D, F = (2, 1024, 1024, D_MODEL, D_FF)
        std = 0.02
        inp = {'tgt': jax.random.normal(ks[0], (B, L, D), jnp.float32), 'memory': jax.random.normal(ks[1], (B, S, D), jnp.float32), 'tgt_mask': jnp.triu(jnp.ones((L, L), jnp.int32), k=1)}
        names = ['q', 'k', 'v', 'o', 'cq', 'ck', 'cv', 'co']
        for i, n in enumerate(names):
            inp[n + '_w'] = jax.random.normal(ks[2 + i], (D, D), jnp.float32) * std
            inp[n + '_b'] = jnp.zeros((D,), jnp.float32)
        inp['lin1_w'] = jax.random.normal(ks[12], (D, F), jnp.float32) * std
        inp['lin1_b'] = jnp.zeros((F,), jnp.float32)
        inp['lin2_w'] = jax.random.normal(ks[13], (F, D), jnp.float32) * std
        inp['lin2_b'] = jnp.zeros((D,), jnp.float32)
        for i, n in enumerate(['ln1', 'ln2', 'ln3']):
            inp[n + '_g'] = jnp.ones((D,), jnp.float32)
            inp[n + '_b'] = jnp.zeros((D,), jnp.float32)
        return inp
    _L0_xattn_all = _L0_xattn_setup()
    _L0_xattn_in = {k: v for k, v in _L0_xattn_all.items() if k in ('q_w', 'q_b', 'k_w', 'k_b', 'v_w', 'v_b', 'o_w', 'o_b', 'cq_w', 'cq_b', 'ck_w', 'ck_b', 'cv_w', 'cv_b', 'co_w', 'co_b', 'lin1_w', 'lin1_b', 'lin2_w', 'lin2_b', 'ln1_g', 'ln1_b', 'ln2_g', 'ln2_b', 'ln3_g', 'ln3_b')}
    del _L0_xattn_all

    def _L1_xattn_setup():
        import jax, jax.numpy as jnp
        import numpy as np
        H, D_MODEL, LEN_Q, LEN_K, D_K, D_V = (16, 512, 256, 1024, 64, 64)
        B = 4

        def _layernorm(x, gamma, beta, eps=1e-05):
            mu = jnp.mean(x, axis=-1, keepdims=True)
            var = jnp.mean((x - mu) ** 2, axis=-1, keepdims=True)
            return (x - mu) * jax.lax.rsqrt(var + eps) * gamma + beta
        key = jax.random.key(seed)
        ks = jax.random.split(key, 16)
        s = 0.02
        return {'Q': jax.random.normal(ks[0], (B, LEN_Q, D_MODEL), jnp.float32), 'K': jax.random.normal(ks[1], (B, LEN_K, D_MODEL), jnp.float32), 'V': jax.random.normal(ks[2], (B, LEN_K, D_MODEL), jnp.float32), 'node_num': LEN_Q, 'mask': jax.random.randint(ks[3], (B, LEN_K), 0, 2, jnp.int32), 'Wq': jax.random.normal(ks[4], (D_MODEL, H * D_K), jnp.float32) * s, 'bq': jnp.zeros((H * D_K,), jnp.float32), 'Wk': jax.random.normal(ks[5], (D_MODEL, H * D_K), jnp.float32) * s, 'bk': jnp.zeros((H * D_K,), jnp.float32), 'Wv': jax.random.normal(ks[6], (D_MODEL, H * D_V), jnp.float32) * s, 'bv': jnp.zeros((H * D_V,), jnp.float32), 'Wo': jax.random.normal(ks[7], (H * D_V, D_MODEL), jnp.float32) * s, 'bo': jnp.zeros((D_MODEL,), jnp.float32), 'gamma': jnp.ones((D_MODEL,), jnp.float32), 'beta': jnp.zeros((D_MODEL,), jnp.float32)}
    _L1_xattn_all = _L1_xattn_setup()
    _L1_xattn_in = {k: v for k, v in _L1_xattn_all.items() if k in ('Wq', 'bq', 'Wk', 'bk', 'Wv', 'bv', 'Wo', 'bo', 'gamma', 'beta')}
    del _L1_xattn_all
    return {'x': x, 'ctx_1024': ctx_1024, 'mask_SxS_ik1': mask_SxS_ik1, 'mask_BxS2_ik0': mask_BxS2_ik0, 'L0_xattn_q_w': _L0_xattn_in['q_w'], 'L0_xattn_q_b': _L0_xattn_in['q_b'], 'L0_xattn_k_w': _L0_xattn_in['k_w'], 'L0_xattn_k_b': _L0_xattn_in['k_b'], 'L0_xattn_v_w': _L0_xattn_in['v_w'], 'L0_xattn_v_b': _L0_xattn_in['v_b'], 'L0_xattn_o_w': _L0_xattn_in['o_w'], 'L0_xattn_o_b': _L0_xattn_in['o_b'], 'L0_xattn_cq_w': _L0_xattn_in['cq_w'], 'L0_xattn_cq_b': _L0_xattn_in['cq_b'], 'L0_xattn_ck_w': _L0_xattn_in['ck_w'], 'L0_xattn_ck_b': _L0_xattn_in['ck_b'], 'L0_xattn_cv_w': _L0_xattn_in['cv_w'], 'L0_xattn_cv_b': _L0_xattn_in['cv_b'], 'L0_xattn_co_w': _L0_xattn_in['co_w'], 'L0_xattn_co_b': _L0_xattn_in['co_b'], 'L0_xattn_lin1_w': _L0_xattn_in['lin1_w'], 'L0_xattn_lin1_b': _L0_xattn_in['lin1_b'], 'L0_xattn_lin2_w': _L0_xattn_in['lin2_w'], 'L0_xattn_lin2_b': _L0_xattn_in['lin2_b'], 'L0_xattn_ln1_g': _L0_xattn_in['ln1_g'], 'L0_xattn_ln1_b': _L0_xattn_in['ln1_b'], 'L0_xattn_ln2_g': _L0_xattn_in['ln2_g'], 'L0_xattn_ln2_b': _L0_xattn_in['ln2_b'], 'L0_xattn_ln3_g': _L0_xattn_in['ln3_g'], 'L0_xattn_ln3_b': _L0_xattn_in['ln3_b'], 'L1_xattn_Wq': _L1_xattn_in['Wq'], 'L1_xattn_bq': _L1_xattn_in['bq'], 'L1_xattn_Wk': _L1_xattn_in['Wk'], 'L1_xattn_bk': _L1_xattn_in['bk'], 'L1_xattn_Wv': _L1_xattn_in['Wv'], 'L1_xattn_bv': _L1_xattn_in['bv'], 'L1_xattn_Wo': _L1_xattn_in['Wo'], 'L1_xattn_bo': _L1_xattn_in['bo'], 'L1_xattn_gamma': _L1_xattn_in['gamma'], 'L1_xattn_beta': _L1_xattn_in['beta']}

def reference(x, ctx_1024, mask_SxS_ik1, mask_BxS2_ik0, L0_xattn_q_w, L0_xattn_q_b, L0_xattn_k_w, L0_xattn_k_b, L0_xattn_v_w, L0_xattn_v_b, L0_xattn_o_w, L0_xattn_o_b, L0_xattn_cq_w, L0_xattn_cq_b, L0_xattn_ck_w, L0_xattn_ck_b, L0_xattn_cv_w, L0_xattn_cv_b, L0_xattn_co_w, L0_xattn_co_b, L0_xattn_lin1_w, L0_xattn_lin1_b, L0_xattn_lin2_w, L0_xattn_lin2_b, L0_xattn_ln1_g, L0_xattn_ln1_b, L0_xattn_ln2_g, L0_xattn_ln2_b, L0_xattn_ln3_g, L0_xattn_ln3_b, L1_xattn_Wq, L1_xattn_bq, L1_xattn_Wk, L1_xattn_bk, L1_xattn_Wv, L1_xattn_bv, L1_xattn_Wo, L1_xattn_bo, L1_xattn_gamma, L1_xattn_beta):
    import jax
    import jax.numpy as jnp

    def _L0_xattn_ref(tgt, memory, tgt_mask, q_w, q_b, k_w, k_b, v_w, v_b, o_w, o_b, cq_w, cq_b, ck_w, ck_b, cv_w, cv_b, co_w, co_b, lin1_w, lin1_b, lin2_w, lin2_b, ln1_g, ln1_b, ln2_g, ln2_b, ln3_g, ln3_b):
        import jax, jax.numpy as jnp
        import numpy as np
        D_MODEL = 512
        N_HEAD = 16
        D_FF = 2048
        EPS = 1e-05

        def _linear(x, w, b):
            return jnp.einsum('bli,io->blo', x, w) + b

        def _layernorm(x, g, b):
            mu = jnp.mean(x, -1, keepdims=True)
            var = jnp.mean(jnp.square(x - mu), -1, keepdims=True)
            return (x - mu) * jax.lax.rsqrt(var + EPS) * g + b

        def _attention(q, k, v, mask):
            B, Lq, D = q.shape
            H = N_HEAD
            hd = D // H
            qh = q.reshape(B, Lq, H, hd)
            kh = k.reshape(B, k.shape[1], H, hd)
            vh = v.reshape(B, v.shape[1], H, hd)
            scores = jnp.einsum('bqhd,bkhd->bhqk', qh, kh) / jnp.sqrt(jnp.float32(hd)).astype(q.dtype)
            if mask is not None:
                scores = jnp.where(mask[None, None] != 0, jnp.finfo(scores.dtype).min, scores)
            p = jax.nn.softmax(scores, axis=-1)
            out = jnp.einsum('bhqk,bkhd->bqhd', p, vh).reshape(B, Lq, D)
            return out
        q = _linear(tgt, q_w, q_b)
        k = _linear(tgt, k_w, k_b)
        v = _linear(tgt, v_w, v_b)
        tgt2 = _linear(_attention(q, k, v, tgt_mask), o_w, o_b)
        x = _layernorm(tgt + tgt2, ln1_g, ln1_b)
        q = _linear(x, cq_w, cq_b)
        k = _linear(memory, ck_w, ck_b)
        v = _linear(memory, cv_w, cv_b)
        tgt2 = _linear(_attention(q, k, v, None), co_w, co_b)
        x = _layernorm(x + tgt2, ln2_g, ln2_b)
        tgt2 = _linear(jax.nn.relu(_linear(x, lin1_w, lin1_b)), lin2_w, lin2_b)
        x = _layernorm(x + tgt2, ln3_g, ln3_b)
        return x

    def _L1_xattn_ref(Q, K, V, node_num, mask, Wq, bq, Wk, bk, Wv, bv, Wo, bo, gamma, beta):
        import jax, jax.numpy as jnp
        import numpy as np
        H, D_MODEL, LEN_Q, LEN_K, D_K, D_V = (16, 512, 256, 1024, 64, 64)
        B = 4

        def _layernorm(x, gamma, beta, eps=1e-05):
            mu = jnp.mean(x, axis=-1, keepdims=True)
            var = jnp.mean((x - mu) ** 2, axis=-1, keepdims=True)
            return (x - mu) * jax.lax.rsqrt(var + eps) * gamma + beta
        b, lq, _ = Q.shape
        lk = K.shape[1]
        q = (Q @ Wq + bq).reshape(b, lq, H, D_K)
        k = (K @ Wk + bk).reshape(b, lk, H, D_K)
        v = (V @ Wv + bv).reshape(b, lk, H, D_V)
        scores = jnp.einsum('bqhd,bkhd->bhqk', q, k) / jnp.sqrt(jnp.float32(D_K))
        scores = jnp.where(mask[:, None, None, :] == 0, -jnp.inf, scores)
        alpha = jax.nn.softmax(scores, axis=-1)
        out = jnp.einsum('bhqk,bkhd->bqhd', alpha, v).reshape(b, lq, H * D_V)
        out = out @ Wo + bo + Q
        return _layernorm(out, gamma, beta)
    x = _L0_xattn_ref(x, ctx_1024, mask_SxS_ik1, L0_xattn_q_w, L0_xattn_q_b, L0_xattn_k_w, L0_xattn_k_b, L0_xattn_v_w, L0_xattn_v_b, L0_xattn_o_w, L0_xattn_o_b, L0_xattn_cq_w, L0_xattn_cq_b, L0_xattn_ck_w, L0_xattn_ck_b, L0_xattn_cv_w, L0_xattn_cv_b, L0_xattn_co_w, L0_xattn_co_b, L0_xattn_lin1_w, L0_xattn_lin1_b, L0_xattn_lin2_w, L0_xattn_lin2_b, L0_xattn_ln1_g, L0_xattn_ln1_b, L0_xattn_ln2_g, L0_xattn_ln2_b, L0_xattn_ln3_g, L0_xattn_ln3_b)
    x = _L1_xattn_ref(x, ctx_1024, ctx_1024, 2048, mask_BxS2_ik0, L1_xattn_Wq, L1_xattn_bq, L1_xattn_Wk, L1_xattn_bk, L1_xattn_Wv, L1_xattn_bv, L1_xattn_Wo, L1_xattn_bo, L1_xattn_gamma, L1_xattn_beta)
    return x

_drawn_inputs = setup_inputs


def setup_inputs(seed=0):
    import zlib

    import numpy as np

    out = dict(_drawn_inputs(seed))
    spreads = {'L0_xattn_q_b': (0.0, 0.8),
     'L0_xattn_k_b': (0.0, 0.8),
     'L0_xattn_v_b': (0.0, 0.1),
     'L0_xattn_o_b': (0.0, 0.1),
     'L0_xattn_cq_b': (0.0, 0.8),
     'L0_xattn_ck_b': (0.0, 0.8),
     'L0_xattn_cv_b': (0.0, 0.1),
     'L0_xattn_co_b': (0.0, 0.1),
     'L0_xattn_lin1_b': (0.0, 0.1),
     'L0_xattn_lin2_b': (0.0, 0.1),
     'L0_xattn_ln1_g': (1.0, 0.2),
     'L0_xattn_ln1_b': (0.0, 0.1),
     'L0_xattn_ln2_g': (1.0, 0.2),
     'L0_xattn_ln2_b': (0.0, 0.1),
     'L0_xattn_ln3_g': (1.0, 0.2),
     'L0_xattn_ln3_b': (0.0, 0.1),
     'L1_xattn_bq': (0.0, 0.8),
     'L1_xattn_bk': (0.0, 0.8),
     'L1_xattn_bv': (0.0, 0.1),
     'L1_xattn_bo': (0.0, 0.1),
     'L1_xattn_gamma': (1.0, 0.2),
     'L1_xattn_beta': (0.0, 0.1)}
    factors = {'L0_xattn_q_w': 8.0,
     'L0_xattn_k_w': 8.0,
     'L0_xattn_v_w': 5.61,
     'L0_xattn_cq_w': 7.135,
     'L0_xattn_ck_w': 6.853}
    for name, (base, spread) in spreads.items():
        noise = np.random.default_rng([zlib.crc32(name.encode()), seed]).standard_normal(out[name].shape)
        drawn = base * np.exp(spread * noise) if base else spread * noise
        out[name] = jnp.asarray(drawn.astype(out[name].dtype))
    for name, factor in factors.items():
        out[name] = (out[name] * factor).astype(out[name].dtype)
    return out
```

```python
from contextlib import ExitStack

import concourse.bass as bass
from concourse import mybir

F32 = mybir.dt.float32
F32R = mybir.dt.float32r
BF16 = mybir.dt.bfloat16
I32 = mybir.dt.int32
ALU = mybir.AluOpType
ACT = mybir.ActivationFunctionType
AX = mybir.AxisListType

P = 128
B, S, D = 2, 2048, 512
TOK = B * S
KC = D // P
H0, HD0 = 16, 32
H1, HD1 = 16, 64
CTX = 77
FF = 2048
EPS = 1e-5
BIG = 2.0 ** 126
BANK = 512
KEYS = 512


class Count:

    def __init__(self, sem, step=1, ahead=0):
        self.sem, self.step, self.ahead, self.start = sem, step, ahead, step * ahead

    def done(self, n):
        return n * self.step + self.step * (self.ahead + 1)

    def room(self, n, ring):
        assert ring <= self.ahead
        return n * self.step + self.step * (self.ahead + 1 - ring)


class Banks:

    def __init__(self, psum, ready, read, names):
        self.psum, self.ready, self.read, self.names = psum, ready, read, names
        self.at = {name: n for n, name in enumerate(names)}
        self.per_bank = [len(range(b, len(names), 8)) for b in range(8)]
        assert len(self.at) == len(names) >= 8

    def bank(self, name):
        return self.psum[:, self.at[name] % 8, :]

    def read_of(self, name):
        return self.read[self.at[name] % 8]

    def free(self, rnd, name):
        n = self.at[name]
        return rnd * self.per_bank[n % 8] + (n // 8 + 1)

    def drained(self, rnd, name):
        n = self.at[name]
        return rnd * self.per_bank[n % 8] + (n // 8 + 2)

    def made(self, rnd, name):
        return rnd * len(self.names) + (len(self.names) + self.at[name] + 1)

    def made_before(self, rnd, name):
        return rnd * len(self.names) + (self.at[name] + 1)


def product(pe, out, w, x, first, last):
    pe.matmul(out, w[1], x[0], start=first, stop=False)
    pe.matmul(out, w[0], x[1], start=False, stop=False)
    return pe.matmul(out, w[0], x[0], start=False, stop=last)


class Stage:

    def __init__(self, nc, ctx, name):
        self.nc, self.ctx, self.name, self.sems = nc, ctx, name, []
        ctx.callback(self.clear)

    def clear(self):
        with self.nc.Block() as block:

            @block.gpsimd
            def _(pool):
                self.nc.clear_and_free_semaphores(self.sems)

    def sb(self, name, shape, dt=F32):
        return self.ctx.enter_context(self.nc.sbuf_tensor(f"{self.name}_{name}", shape, dt))

    def halves(self, name, shape):
        return [self.sb(f"{name}_{h}", shape, F32R) for h in ("hi", "lo")]

    def sem(self, name):
        self.sems.append(self.nc.alloc_semaphore(f"{self.name}_{name}"))
        return self.sems[-1]

    def count(self, name, step=1, ahead=0):
        return Count(self.sem(name), step, ahead)

    def banks(self, psum, names):
        return Banks(psum, self.sem("ready"), [self.sem(f"read{b}") for b in range(8)], names)


def rows_of(m):
    return m.rearrange("(c p) n -> p c n", p=P)


def tokens_of(m, first, tiles):
    return m[bass.ds(first, tiles * P), :].rearrange("(t p) n -> p t n", p=P)


def split_weights(nc, name, jobs):
    shape = list(jobs[0][0].shape)
    with ExitStack() as ctx:
        st = Stage(nc, ctx, name)
        raw = [st.sb(f"raw{s}", shape) for s in range(2)]
        loaded = [st.count(f"raw{s}_loaded", 16) for s in range(2)]
        hi_done, split = st.count("raw_hi"), st.count("raw_split")
        with nc.Block() as block:

            @block.sync
            def _(sp):
                for n, (src, _, _) in enumerate(jobs):
                    if n >= 2:
                        sp.wait_ge(split.sem, split.done(n - 2))
                    sp.dma_start(raw[n % 2][:, :, :], src).then_inc(loaded[n % 2].sem, 16)

            @block.scalar
            def _(act):
                for n, (_, hi, _) in enumerate(jobs):
                    act.wait_ge(loaded[n % 2].sem, loaded[n % 2].done(n // 2))
                    act.activation(hi, raw[n % 2][:, :, :], ACT.Copy).then_inc(hi_done.sem, 1)

            @block.vector
            def _(dve):
                for n, (_, hi, lo) in enumerate(jobs):
                    dve.wait_ge(hi_done.sem, hi_done.done(n))
                    dve.tensor_tensor(lo, raw[n % 2][:, :, :], hi.bitcast(F32), ALU.subtract).then_inc(split.sem, 1)
                dve.wait_ge(split.sem, split.done(len(jobs) - 1))


def make_constants(nc, ctx):
    st = Stage(nc, ctx, "const")
    ident, half, ones = st.sb("ident", [P, P]), st.sb("minus_half", [P, 1]), st.sb("ones", [P, P])
    made = st.sem("made")
    with nc.Block() as block:

        @block.gpsimd
        def _(pool):
            pool.memset(ident[:, :], 0.0).then_inc(made, 1)
            pool.memset(half[:, :], -0.5).then_inc(made, 1)
            pool.memset(ones[:, :], 1.0).then_inc(made, 1)
            pool.wait_ge(made, 3)
            pool.affine_select(out=ident[:, :], in_=ident[:, :], compare_op=ALU.not_equal, fill=1.0,
                               base=0, pattern=[[-1, P]], channel_multiplier=1).then_inc(made, 1)
            pool.wait_ge(made, 4)

    return ident, half, ones


class Tail:

    def __init__(self, st, tiles, residual, out, bias, gain, shift, minus_half):
        assert tiles % 2 == 0
        self.tiles, self.residual, self.out, self.half = tiles, residual, out, minus_half
        self.rows_dram = (bias, gain, shift)
        self.rows = [st.sb(f"row_{n}", [P, D]) for n in ("bias", "gain", "shift")]
        self.res = [st.sb(f"residual{s}", [P, D]) for s in range(2)]
        self.sum = [st.sb(f"sum{s}", [P, D]) for s in range(2)]
        self.y = [st.sb(f"normed{s}", [P, D]) for s in range(2)]
        self.stats = [st.sb(f"stats{s}", [P, 6]) for s in range(2)]
        self.mean_var = [st.sb(f"mean_var{s}", [P, 2]) for s in range(2)]
        self.var_eps = [st.sb(f"var_eps{s}", [P, 1]) for s in range(2)]
        self.rstd = [st.sb(f"rstd{s}", [P, 1]) for s in range(2)]
        self.rows_in = st.count("rows_in", 16)
        self.passed = st.sem("waits_passed")
        self.res_in = [st.count(f"residual_in{s}", 16) for s in range(2)]
        self.biased = st.count("residual_biased")
        self.stats_done = st.count("stats_done")
        self.var_done = st.count("variance_done", ahead=2)
        self.eps_added = st.count("eps_added")
        self.rstd_done = st.count("rstd_done")
        self.normed = st.count("normed")
        self.gained = st.count("gained", ahead=2)
        self.finished = st.count("finished")
        self.stored = [st.count(f"stored{s}", 16, 1) for s in range(2)]

    def tile(self, rnd, t):
        return rnd * self.tiles + t, rnd * (self.tiles // 2) + t // 2, t % 2

    def load_rows(self, sp):
        for row, src in zip(self.rows, self.rows_dram):
            sp.dma_start(row[:, :], src.partition_broadcast(P)).then_inc(self.rows_in.sem, 16)

    def load(self, sp, rnd, t):
        n, k, s = self.tile(rnd, t)
        sp.wait_ge(self.var_done.sem, self.var_done.room(n, 2))
        sp.dma_start(self.res[s][:, :], self.residual[bass.ds(n * P, P), :]).then_inc(self.res_in[s].sem, 16)

    def start_dve(self, dve):
        dve.sem_inc(self.var_done.sem, self.var_done.start)

    def store(self, sp, rnd, t):
        n, k, s = self.tile(rnd, t)
        sp.wait_ge(self.finished.sem, self.finished.done(n))
        sp.dma_start(self.out[bass.ds(n * P, P), :], self.y[s][:, :]).then_inc(self.stored[s].sem, 16)

    def run_sync(self, sp, rounds, load_x):
        for c in self.stored:
            sp.sem_inc(c.sem, c.start)
        self.load_rows(sp)
        load_x(0)
        for t in range(2):
            self.load(sp, 0, t)
        with sp.Fori(0, rounds - 1) as r:
            load_x(r + 1)
            for t in range(self.tiles):
                self.load(sp, r, t + 2)
                self.store(sp, r, t)
        for t in range(self.tiles):
            if t + 2 < self.tiles:
                self.load(sp, rounds - 1, t + 2)
            self.store(sp, rounds - 1, t)
        for c in self.stored:
            sp.wait_ge(c.sem, c.done(rounds * (self.tiles // 2) - 1))

    def start_pool(self, pool):
        pool.sem_inc(self.gained.sem, self.gained.start)
        pool.wait_ge(self.rows_in.sem, self.rows_in.done(2))

    def pool_bias(self, pool, rnd, t):
        n, k, s = self.tile(rnd, t)
        pool.wait_ge(self.res_in[s].sem, self.res_in[s].done(k))
        pool.tensor_tensor(self.res[s][:, :], self.res[s][:, :], self.rows[0][:, :], ALU.add).then_inc(self.biased.sem, 1)

    def dve_sum(self, dve, rnd, t, banks, name):
        n, k, s = self.tile(rnd, t)
        dve.wait_ge(self.biased.sem, self.biased.done(n))
        dve.wait_ge(self.gained.sem, self.gained.room(n, 2))
        dve.wait_ge(banks.ready, banks.made(rnd, name))
        dve.tensor_tensor(self.sum[s][:, :], banks.bank(name), self.res[s][:, :], ALU.add).then_inc(banks.read_of(name), 1)
        dve.wait_ge(banks.read_of(name), banks.drained(rnd, name))
        dve.bn_stats(self.stats[s][:, :], self.sum[s][:, :]).then_inc(self.stats_done.sem, 1)
        dve.wait_ge(self.stats_done.sem, self.stats_done.done(n))
        dve.sem_inc(self.passed, 1)
        dve.bn_aggr(self.mean_var[s][:, :], self.stats[s][:, :]).then_inc(self.var_done.sem, 1)

    def pool_rstd(self, pool, rnd, t):
        n, k, s = self.tile(rnd, t)
        pool.wait_ge(self.var_done.sem, self.var_done.done(n))
        pool.sem_inc(self.passed, 1)
        pool.tensor_scalar(self.var_eps[s][:, :], self.mean_var[s][:, 1:2], EPS, None, ALU.add).then_inc(self.eps_added.sem, 1)
        pool.wait_ge(self.eps_added.sem, self.eps_added.done(n))
        pool.tensor_tensor(self.rstd[s][:, :], self.var_eps[s][:, :], self.half[:, :], ALU.pow).then_inc(self.rstd_done.sem, 1)

    def dve_norm(self, dve, rnd, t):
        n, k, s = self.tile(rnd, t)
        dve.wait_ge(self.rstd_done.sem, self.rstd_done.done(n))
        dve.tensor_scalar(self.sum[s][:, :], self.sum[s][:, :], self.mean_var[s][:, 0:1],
                                         self.rstd[s][:, :], ALU.subtract, ALU.mult).then_inc(self.normed.sem, 1)

    def pool_finish(self, pool, rnd, t):
        n, k, s = self.tile(rnd, t)
        pool.wait_ge(self.normed.sem, self.normed.done(n))
        pool.wait_ge(self.stored[s].sem, self.stored[s].room(k, 1))
        pool.tensor_tensor(self.y[s][:, :], self.sum[s][:, :], self.rows[1][:, :], ALU.mult).then_inc(self.gained.sem, 1)
        pool.wait_ge(self.gained.sem, self.gained.done(n))
        pool.tensor_tensor(self.y[s][:, :], self.y[s][:, :], self.rows[2][:, :], ALU.add).then_inc(self.finished.sem, 1)




def project(nc, psum, ident, x, mask, weights, biases, halves, v_dram, bias_dram, open_max):
    T = 4
    CH = T * P
    BR = S // CH
    ROUNDS = B * BR
    MT = S // P // ROUNDS
    with ExitStack() as ctx:
        st = Stage(nc, ctx, "project")
        w = [st.halves(f"w{n}", [P, KC, D]) for n in "qkv"]
        split_weights(nc, "project_w", [
            (rows_of(m)[:, j:j + 2, :], h[0][:, j:j + 2, :], h[1][:, j:j + 2, :])
            for m, h in zip(weights, w) for j in range(0, KC, 2)])
        bcol = [st.sb(f"b{n}", [P, KC]) for n in "qk"]
        brow = st.sb("bv", [P, D])
        xn = st.sb("x", [P, T, D])
        xt = st.halves("xt", [P, KC, CH])
        out = [st.halves(n, [P, KC, CH]) for n in "qk"]
        vo = st.sb("v", [P, T, H0, HD0 + 1])
        mi = [st.sb(f"mask{j}", [P, S], I32) for j in range(MT)]
        mb = [st.sb(f"bias{j}", [P, S], BF16) for j in range(MT)]

        banks = st.banks(psum, [f"xt{c}" for c in range(KC)] + [f"{n}{o}" for n in "qk" for o in range(KC)]
                         + [f"v{t}" for t in range(T)])
        biases_in = st.count("biases_in", 16)
        ones_set = st.count("ones_set")
        x_in = st.count("x_in", 16)
        mask_in = [st.count(f"mask_in{j}", 16) for j in range(MT)]
        xt_hi = st.count("xt_hi")
        out_hi = st.count("qk_hi")
        bias_made = st.count("bias_made", ahead=MT)
        open_made = st.count("open_made", ahead=MT)
        halves_out = [st.count(f"{n}_stored", 32, 1) for n in "qk"]
        v_out = st.count("v_stored", 16, 1)
        bias_out = [st.count(f"bias_stored{j}", 16, 1) for j in range(MT)]

        def rounds(eng, one):
            with eng.Fori(0, ROUNDS) as r:
                one(r)

        with nc.Block() as block:

            @block.sync
            def _(sp):
                for t, src in zip(bcol, biases[:2]):
                    sp.dma_start(t[:, :], src.rearrange("(c p) -> p c", p=P), allow_slow_non_contiguous=True).then_inc(biases_in.sem, 16)
                sp.dma_start(brow[:, :], biases[2].partition_broadcast(P)).then_inc(biases_in.sem, 16)

                def load(r):
                    sp.wait_ge(banks.ready, banks.made_before(r, f"xt{KC - 1}"))
                    sp.dma_start(xn[:, :, :], tokens_of(x, r * CH, T)).then_inc(x_in.sem, 16)
                    for m in range(MT):
                        sp.wait_ge(bias_made.sem, bias_made.room(r * MT + m, MT))
                        sp.dma_start(mi[m][:, :], mask[bass.ds((r * MT + m) * P, P), :]).then_inc(mask_in[m].sem, 16)

                def store(r):
                    for m in range(MT):
                        sp.wait_ge(bias_made.sem, bias_made.done(r * MT + m))
                        sp.dma_start(bias_dram[bass.ds((r * MT + m) * P, P), :], mb[m][:, :]).then_inc(bias_out[m].sem, 16)
                    for m, n in enumerate("qk"):
                        for o in range(KC):
                            sp.wait_ge(banks.read_of(f"{n}{o}"), banks.drained(r, f"{n}{o}"))
                        for h in range(2):
                            dst = halves[m][h].rearrange("(c p) s -> p c s", p=P)[
                                :, bass.ds(r // BR * KC, KC), bass.ds(r % BR * CH, CH)]
                            sp.dma_start(dst, out[m][h][:, :, :].bitcast(F32)).then_inc(halves_out[m].sem, 16)
                    for t in range(T):
                        sp.wait_ge(banks.read_of(f"v{t}"), banks.drained(r, f"v{t}"))
                    sp.dma_start(tokens_of(v_dram, r * CH, T),
                                          vo[:, :, :, :].rearrange("p t h d -> p t (h d)")).then_inc(v_out.sem, 16)

                stores = (*halves_out, v_out, *bias_out)
                for c in stores:
                    sp.sem_inc(c.sem, c.start)
                load(0)
                with sp.Fori(0, ROUNDS - 1) as r:
                    load(r + 1)
                    store(r)
                store(ROUNDS - 1)
                for c in stores:
                    sp.wait_ge(c.sem, c.done(ROUNDS - 1))

            @block.tensor
            def _(pe):
                pe.sem_inc(banks.ready, len(banks.names))
                for sem in banks.read:
                    pe.sem_inc(sem, 1)

                def one(r):
                    pe.wait_ge(x_in.sem, x_in.done(r))
                    for c in range(KC):
                        pe.wait_ge(banks.read_of(f"xt{c}"), banks.free(r, f"xt{c}"))
                        for t in range(T):
                            last = pe.transpose(banks.bank(f"xt{c}")[:, t * P:(t + 1) * P],
                                                xn[:, t, c * P:(c + 1) * P], ident[:, :])
                        last.then_inc(banks.ready, 1)
                    for m, n in enumerate("qk"):
                        for o in range(KC):
                            pe.wait_ge(banks.read_of(f"{n}{o}"), banks.free(r, f"{n}{o}"))
                            for c in range(KC):
                                if m == 0 and o == 0:
                                    pe.wait_ge(banks.read_of(f"xt{c}"), banks.drained(r, f"xt{c}"))
                                last = product(pe, banks.bank(f"{n}{o}"),
                                               [h[:, c, o * P:(o + 1) * P] for h in w[m]],
                                               [h[:, c, :] for h in xt], c == 0, c == KC - 1)
                            last.then_inc(banks.ready, 1)
                    for t in range(T):
                        pe.wait_ge(banks.read_of(f"v{t}"), banks.free(r, f"v{t}"))
                        for c in range(KC):
                            last = product(pe, banks.bank(f"v{t}"), [h[:, c, t * P:(t + 1) * P] for h in xt],
                                           [h[:, c, :] for h in w[2]], c == 0, c == KC - 1)
                        last.then_inc(banks.ready, 1)

                rounds(pe, one)

            @block.scalar
            def _(act):
                act.wait_ge(biases_in.sem, biases_in.done(2))

                def one(r):
                    for c in range(KC):
                        act.wait_ge(banks.ready, banks.made(r, f"xt{c}"))
                        act.wait_ge(banks.ready, banks.made_before(r, f"v{T - 1}"))
                        act.activation(xt[0][:, c, :], banks.bank(f"xt{c}"), ACT.Copy).then_inc(xt_hi.sem, 1)
                    for m, n in enumerate("qk"):
                        act.wait_ge(halves_out[m].sem, halves_out[m].room(r, 1))
                        for o in range(KC):
                            act.wait_ge(banks.ready, banks.made(r, f"{n}{o}"))
                            act.activation(out[m][0][:, o, :], banks.bank(f"{n}{o}"), ACT.Identity,
                                                     bias=bcol[m][:, o:o + 1]).then_inc(out_hi.sem, 1)

                rounds(act, one)

            @block.vector
            def _(dve):
                dve.sem_inc(bias_made.sem, bias_made.start)
                dve.sem_inc(open_made.sem, open_made.start)
                dve.memset(vo[:, :, :, HD0:], 1.0).then_inc(ones_set.sem, 1)
                dve.wait_ge(ones_set.sem, ones_set.done(0))
                dve.wait_ge(biases_in.sem, biases_in.done(2))

                def one(r):
                    for c in range(KC):
                        dve.wait_ge(xt_hi.sem, xt_hi.done(r * KC + c))
                        dve.tensor_tensor(xt[1][:, c, :], banks.bank(f"xt{c}"),
                                                        xt[0][:, c, :].bitcast(F32), ALU.subtract).then_inc(banks.read_of(f"xt{c}"), 1)
                    for m in range(MT):
                        dve.wait_ge(mask_in[m].sem, mask_in[m].done(r))
                        dve.wait_ge(bias_out[m].sem, bias_out[m].room(r, 1))
                        dve.wait_ge(open_made.sem, open_made.room(r * MT + m, MT))
                        dve.tensor_scalar(mb[m][:, :], mi[m][:, :], 0.0, -BIG,
                                                       ALU.not_equal, ALU.mult).then_inc(bias_made.sem, 1)
                    for m, n in enumerate("qk"):
                        dve.wait_ge(halves_out[m].sem, halves_out[m].room(r, 1))
                        for o in range(KC):
                            dve.wait_ge(out_hi.sem, out_hi.done(r * 2 * KC + (m * KC + o)))
                            dve.scalar_tensor_tensor(
                                out[m][1][:, o, :], banks.bank(f"{n}{o}"), bcol[m][:, o:o + 1],
                                out[m][0][:, o, :].bitcast(F32), ALU.add, ALU.subtract).then_inc(banks.read_of(f"{n}{o}"), 1)
                        if m < MT:
                            dve.wait_ge(bias_made.sem, bias_made.done(r * MT + m))
                            dve.tensor_reduce(
                                open_max[:, bass.ds(r * MT + m, 1), :].rearrange("p o k -> p (o k)"),
                                mb[m][:, :].rearrange("p (k s) -> p k s", s=KEYS), AX.X, ALU.max).then_inc(open_made.sem, 1)
                    dve.wait_ge(v_out.sem, v_out.room(r, 1))
                    for t in range(T):
                        dve.wait_ge(banks.ready, banks.made(r, f"v{t}"))
                        dve.tensor_tensor(
                            vo[:, t, :, 0:HD0], banks.bank(f"v{t}").rearrange("p (h d) -> p h d", d=HD0),
                            brow[:, :].rearrange("p (h d) -> p h d", d=HD0), ALU.add).then_inc(banks.read_of(f"v{t}"), 1)

                rounds(dve, one)




def choose_window(nc, psum, ones, open_max, choice):
    NB, NT = S // KEYS, S // P
    with ExitStack() as ctx:
        st = Stage(nc, ctx, "choose")
        is_open = st.sb("is_open", [P, NT * NB])
        rows = st.sb("rows", [P, NB])
        full, empty, which = st.sb("full", [P, NB]), st.sb("empty", [P, NB]), st.sb("which", [P, NB])
        votes, res = st.sb("votes", [P, NB]), st.sb("res", [P, 2])
        place = st.sb("place", [P, NB])
        yes = st.sb("yes", [P, 2])
        step, counted = st.sem("step"), st.sem("counted")
        with nc.Block() as block:

            @block.vector
            def _(dve):
                n = 0

                def link(ins):
                    nonlocal n
                    n += 1
                    ins.then_inc(step, 1)
                    dve.wait_ge(step, n)

                link(dve.tensor_scalar(is_open[:, :], open_max[:, :, :].rearrange("p t k -> p (t k)"), 0.0, None,
                                       ALU.is_equal))
                for k in range(NB):
                    link(dve.memset(place[:, k:k + 1], float(k)))
                dve.wait_ge(counted, 1)
                link(dve.tensor_reduce(rows[:, :], psum[:, 0, 0:NT * NB].rearrange("p (t k) -> p k t", k=NB),
                                       AX.X, ALU.add))
                link(dve.tensor_scalar(full[:, :], rows[:, :], float(S), None, ALU.is_equal))
                link(dve.tensor_scalar(empty[:, :], rows[:, :], 0.0, None, ALU.is_equal))
                link(dve.scalar_tensor_tensor(votes[:, :], full[:, :], float(NB), empty[:, :], ALU.mult, ALU.add))
                link(dve.tensor_reduce(res[:, 0:1], votes[:, :], AX.X, ALU.add))
                link(dve.tensor_scalar(yes[:, 0:1], res[:, 0:1], float(2 * NB - 1), None, ALU.is_equal))
                link(dve.tensor_tensor(which[:, :], full[:, :], place[:, :], ALU.mult))
                link(dve.tensor_reduce(res[:, 1:2], which[:, :], AX.X, ALU.add))
                link(dve.tensor_tensor(yes[:, 1:2], res[:, 1:2], yes[:, 0:1], ALU.mult))
                link(dve.tensor_copy(choice[:, :], yes[0:1, :]))

            @block.tensor
            def _(pe):
                pe.wait_ge(step, 1)
                pe.matmul(psum[:, 0, 0:NT * NB], ones[:, :], is_open[:, :], start=True, stop=True).then_inc(counted, 1)


def attend(nc, psum, ident, halves, v_dram, bias_dram, att_dram, blocks, first):
    NK = blocks * KEYS
    G = 4
    NT = S // P
    TG = G // blocks
    HU = 2 if blocks == 1 else 1
    KT = KEYS // P
    PER_HEAD = NT * blocks
    N = HU * PER_HEAD
    ROUNDS = B * H0 // HU
    HV = HD0 + 1
    AHEAD, WARM = 7, 3
    SCALE = float(HD0) ** -0.5
    TOFS, OOFS = 4, 6
    with ExitStack() as ctx:
        st = Stage(nc, ctx, f"attend{blocks}")
        bias = st.sb("bias", [P, NT, NK], BF16)
        v = st.sb("v", [P, NK // P, B, H0 * HV])
        kst = [st.sb(f"k{u}", [P, NK], F32R) for u in range(HU)]
        qst = [st.sb(f"q{u}", [P, S], F32R) for u in range(HU)]
        pr = st.sb("weights", [P, 8, KEYS])
        pt = st.sb("weights_t", [P, 4, KEYS])
        mx = st.sb("max", [P, 2, G])
        gmx = st.sb("group_max", [P, 2])
        neg = st.sb("neg_max", [P, 2, G])
        rs = st.sb("inverse_sum", [P, 2, TG])
        ao = [st.sb(f"out{u}", [P, NT, HD0]) for u in range(HU)]

        fixed_in = st.count("bias_v_in", 16)
        passed = st.sem("waits_passed")
        kq_in = [st.count(f"kq_in{u}", 16 * 8) for u in range(HU)]
        scored = st.count("scored", ahead=N)
        masked = st.count("masked", ahead=4)
        group_max = st.count("group_max_done")
        shifted = st.count("shift_done")
        exped = st.count("exp_done")
        turned = st.count("transposed", ahead=8)
        moved = st.count("transposed_moved", ahead=2)
        summed = st.count("summed", ahead=4)
        inverted = st.count("inverted")
        normed = st.count("normed", ahead=2)
        stored = [st.count(f"stored{u}", 16, 1) for u in range(HU)]

        def place(n):
            m = n % PER_HEAD
            return n // PER_HEAD, m // blocks, m % blocks

        with nc.Block() as block:

            @block.sync
            def _(sp):
                sp.dma_start(bias[:, :, :], bias_dram[:, bass.ds(first * KEYS, NK)].rearrange(
                    "(t p) s -> p t s", p=P)).then_inc(fixed_in.sem, 16)
                for b in range(B):
                    sp.dma_start(v[:, :, b, :], v_dram[bass.ds(first * KEYS + b * S, NK), :].rearrange(
                        "(t p) n -> p t n", p=P)).then_inc(fixed_in.sem, 16)

                def load(i, u):
                    row = (i * HU + u) * HD0
                    sp.wait_ge(scored.sem, scored.room(i * N + ((u + 1) * PER_HEAD - 1), N))
                    for part in range(4):
                        rows = slice(part * HD0, (part + 1) * HD0)
                        sp.dma_start(kst[u][rows, :].bitcast(F32), halves[1][part % 2][
                            bass.ds(row, HD0), bass.ds(first * KEYS, NK)]).then_inc(kq_in[u].sem, 16)
                        sp.dma_start(qst[u][rows, :].bitcast(F32), halves[0][part // 2][
                            bass.ds(row, HD0), :]).then_inc(kq_in[u].sem, 16)

                def store(i, u):
                    sp.wait_ge(normed.sem, normed.done(i * (N // G) + ((u + 1) * PER_HEAD // G - 1)))
                    sp.dma_start(
                        att_dram[bass.ds(i * HU + u, 1), :, :].rearrange("o (t p) d -> p (o t) d", p=P),
                        ao[u][:, :, :]).then_inc(stored[u].sem, 16)

                for u in range(HU):
                    load(0, u)
                with sp.Fori(0, ROUNDS - 1) as i:
                    for u in range(HU):
                        load(i + 1, u)
                        store(i, u)
                for u in range(HU):
                    store(ROUNDS - 1, u)
                for c in stored:
                    sp.wait_ge(c.sem, c.done(ROUNDS - 1))

            @block.tensor
            def _(pe):
                pe.sem_inc(scored.sem, scored.start)
                pe.sem_inc(turned.sem, turned.start)
                pe.sem_inc(summed.sem, summed.start)
                pe.wait_ge(fixed_in.sem, fixed_in.done(B))

                def score(i, n):
                    u, qt, kb = place(n)
                    if n % PER_HEAD == 0:
                        pe.wait_ge(kq_in[u].sem, kq_in[u].done(i))
                    pe.wait_ge(masked.sem, masked.room(i * N + n, 4))
                    pe.matmul(psum[:, n % 4, :], qst[u][:, qt * P:(qt + 1) * P],
                                        kst[u][:, kb * KEYS:(kb + 1) * KEYS], start=True, stop=True).then_inc(scored.sem, 1)

                def turn(i, n):
                    pe.wait_ge(exped.sem, exped.done(i * N + n))
                    pe.wait_ge(moved.sem, moved.room(i * N + n, 2))
                    for c in range(KT):
                        last = pe.transpose(psum[:, TOFS + n % 2, c * P:(c + 1) * P],
                                            pr[:, n % 8, c * P:(c + 1) * P], ident[:, :])
                    last.then_inc(turned.sem, 1)

                def weigh(i, n):
                    u, qt, kb = place(n)
                    j = n % G
                    if j == 0:
                        pe.wait_ge(normed.sem, normed.room(i * (N // G) + n // G, 2))
                    pe.wait_ge(moved.sem, moved.done(i * N + n))
                    o = (j if blocks == 1 else 0) * HV
                    for c in range(KT):
                        first_one = c == 0 and (blocks == 1 or kb == 0)
                        last_one = c == KT - 1 and (blocks == 1 or kb == blocks - 1)
                        last = pe.matmul(psum[:, OOFS + n // G % 2, o:o + HV], pt[:, n % 4, c * P:(c + 1) * P],
                                         v[:, kb * KT + c, :, :].rearrange("p b n -> p (b n)")[
                                             :, bass.ds((i * HU + u) * HV, HV)],
                                         start=first_one, stop=last_one)
                    last.then_inc(summed.sem, 1)

                def one(i, more):
                    for n in range(N):
                        if n + AHEAD < N or more:
                            score(i + (n + AHEAD) // N, (n + AHEAD) % N)
                        if n + 1 < N or more:
                            turn(i + (n + 1) // N, (n + 1) % N)
                        weigh(i, n)

                for n in range(AHEAD):
                    score(0, n)
                turn(0, 0)
                with pe.Fori(0, ROUNDS - 1) as i:
                    one(i, True)
                one(ROUNDS - 1, False)

            @block.scalar
            def _(act):
                act.sem_inc(moved.sem, moved.start)

                def exp(i, n):
                    j = n % G
                    act.wait_ge(shifted.sem, shifted.done(i * (N // G) + n // G))
                    bias_of = neg[:, n // G % 2, j:j + 1] if blocks == 1 else neg[:, n // G % 2, 0:1]
                    act.activation(pr[:, n % 8, :], pr[:, n % 8, :], ACT.Exp, bias=bias_of, scale=SCALE).then_inc(exped.sem, 1)

                def move(i, n):
                    act.wait_ge(turned.sem, turned.done(i * N + n))
                    act.wait_ge(summed.sem, summed.room(i * N + n, 4))
                    act.activation(pt[:, n % 4, :], psum[:, TOFS + n % 2, :], ACT.Copy).then_inc(moved.sem, 1)

                def one(i, more):
                    for n in range(N):
                        move(i, n)
                        if n + WARM < N or more:
                            exp(i + (n + WARM) // N, (n + WARM) % N)

                for n in range(WARM):
                    exp(0, n)
                with act.Fori(0, ROUNDS - 1) as i:
                    one(i, True)
                one(ROUNDS - 1, False)

            @block.gpsimd
            def _(pool):
                for c in stored:
                    pool.sem_inc(c.sem, c.start)

            @block.vector
            def _(dve):
                dve.sem_inc(masked.sem, masked.start)
                dve.sem_inc(normed.sem, normed.start)
                dve.wait_ge(fixed_in.sem, fixed_in.done(B))

                def mask(i, n):
                    u, qt, kb = place(n)
                    dve.wait_ge(scored.sem, scored.done(i * N + n))
                    dve.wait_ge(turned.sem, turned.room(i * N + n, 8))
                    dve.sem_inc(passed, 1)
                    dve.tensor_tensor_reduce(
                        pr[:, n % 8, :], psum[:, n % 4, :], bias[:, qt, kb * KEYS:(kb + 1) * KEYS], 1.0,
                        -3.0e38, ALU.add, ALU.max, mx[:, n // G % 2, n % G:n % G + 1]).then_inc(masked.sem, 1)
                    if n % G == G - 1:
                        g, p = i * (N // G) + n // G, n // G % 2
                        dve.wait_ge(masked.sem, masked.done(i * N + n))
                        if blocks == 1:
                            dve.tensor_scalar(neg[:, p, :], mx[:, p, :], -SCALE, None, ALU.mult).then_inc(shifted.sem, 1)
                        else:
                            dve.tensor_reduce(gmx[:, p:p + 1], mx[:, p, :], AX.X, ALU.max).then_inc(group_max.sem, 1)
                            dve.wait_ge(group_max.sem, group_max.done(g))
                            dve.tensor_scalar(neg[:, p, 0:1], gmx[:, p:p + 1], -SCALE, None, ALU.mult).then_inc(shifted.sem, 1)

                def norm(i, n):
                    u, qt, kb = place(n)
                    p, first_tile = n // G % 2, qt - (TG - 1)
                    res = psum[:, OOFS + p, 0:TG * HV].rearrange("p (t d) -> p t d", d=HV)
                    dve.wait_ge(summed.sem, summed.done(i * N + n))
                    dve.reciprocal(rs[:, p, :], res[:, :, HD0:].rearrange("p t d -> p (t d)")).then_inc(inverted.sem, 1)
                    dve.wait_ge(inverted.sem, inverted.done(i * (N // G) + n // G))
                    if first_tile == 0:
                        dve.wait_ge(stored[u].sem, stored[u].room(i, 1))
                    dve.tensor_tensor(
                        ao[u][:, first_tile:first_tile + TG, :], res[:, :, 0:HD0],
                        rs[:, p, :].unsqueeze(2).to_broadcast([P, TG, HD0]), ALU.mult).then_inc(normed.sem, 1)

                def one(i, more):
                    for n in range(N):
                        if n + AHEAD < N or more:
                            mask(i + (n + AHEAD) // N, (n + AHEAD) % N)
                        if n % G == G - 1:
                            norm(i, n)

                for n in range(AHEAD):
                    mask(0, n)
                with dve.Fori(0, ROUNDS - 1) as i:
                    one(i, True)
                one(ROUNDS - 1, False)




def join(nc, psum, consts, att_dram, x, out, weight, bias, gain, shift):
    ident, half = consts
    T = 4
    ROUNDS = TOK // (T * P)
    with ExitStack() as ctx:
        st = Stage(nc, ctx, "join")
        w = st.halves("w", [P, KC, D])
        split_weights(nc, "join_w", [(rows_of(weight)[:, j:j + 2, :], w[0][:, j:j + 2, :], w[1][:, j:j + 2, :])
                                     for j in range(0, KC, 2)])
        an = st.sb("att", [P, T, D])
        at = [st.halves(f"att_t{s}", [P, KC, P]) for s in range(2)]
        tail = Tail(st, T, x, out, bias, gain, shift, half)
        banks = st.banks(psum, ["t0", "t1", "y0", "t2", "y1", "t3", "y2", "y3"])
        a_in = st.count("att_in", 16 * T)
        at_hi = st.count("att_t_hi")
        with nc.Block() as block:

            @block.sync
            def _(sp):
                RB = ROUNDS // B

                def load(r):
                    sp.wait_ge(banks.ready, banks.made_before(r, f"t{T - 1}"))
                    for t in range(T):
                        src = att_dram[bass.ds(r // RB * H0, H0), bass.ds(r % RB * (T * P) + t * P, P), :]
                        sp.dma_start(an[:, t, :].rearrange("p (h d) -> p h d", d=HD0),
                                     src.rearrange("h p d -> p h d")).then_inc(a_in.sem, 16)

                tail.run_sync(sp, ROUNDS, load)

            @block.tensor
            def _(pe):
                pe.sem_inc(banks.ready, len(banks.names))
                for sem in banks.read:
                    pe.sem_inc(sem, 1)
                with pe.Fori(0, ROUNDS) as r:
                    pe.wait_ge(a_in.sem, a_in.done(r))
                    for name in banks.names:
                        t = int(name[1])
                        pe.wait_ge(banks.read_of(name), banks.free(r, name))
                        if name[0] == "t":
                            for c in range(KC):
                                last = pe.transpose(banks.bank(name)[:, c * P:(c + 1) * P],
                                                    an[:, t, c * P:(c + 1) * P], ident[:, :])
                        else:
                            pe.wait_ge(banks.read_of(f"t{t}"), banks.drained(r, f"t{t}"))
                            for c in range(KC):
                                last = product(pe, banks.bank(name), [h[:, c, :] for h in at[t % 2]],
                                               [h[:, c, :] for h in w], c == 0, c == KC - 1)
                        last.then_inc(banks.ready, 1)

            @block.scalar
            def _(act):
                with act.Fori(0, ROUNDS) as r:
                    for t in range(T):
                        act.wait_ge(banks.ready, banks.made(r, f"t{t}"))
                        if t >= 2:
                            act.wait_ge(banks.ready, banks.made(r, f"y{t - 2}"))
                        else:
                            act.wait_ge(banks.ready, banks.made_before(r, f"y{t + 2}"))
                        act.activation(at[t % 2][0][:, :, :].rearrange("p c q -> p (c q)"),
                                                banks.bank(f"t{t}"), ACT.Copy).then_inc(at_hi.sem, 1)

            @block.vector
            def _(dve):
                tail.start_dve(dve)

                def low(r, t):
                    dve.wait_ge(at_hi.sem, at_hi.done(r * T + t))
                    dve.tensor_tensor(
                        at[t % 2][1][:, :, :].rearrange("p c q -> p (c q)"), banks.bank(f"t{t}"),
                        at[t % 2][0][:, :, :].rearrange("p c q -> p (c q)").bitcast(F32), ALU.subtract).then_inc(banks.read_of(f"t{t}"), 1)

                with dve.Fori(0, ROUNDS) as r:
                    low(r, 0)
                    for t in range(T):
                        if t + 1 < T:
                            low(r, t + 1)
                        tail.dve_sum(dve, r, t, banks, f"y{t}")
                        if t > 0:
                            tail.dve_norm(dve, r, t - 1)
                    tail.dve_norm(dve, r, T - 1)

            @block.gpsimd
            def _(pool):
                tail.start_pool(pool)
                with pool.Fori(0, ROUNDS) as r:
                    for t in range(T):
                        tail.pool_bias(pool, r, t)
                        if t > 0:
                            tail.pool_finish(pool, r, t - 1)
                        tail.pool_rstd(pool, r, t)
                    tail.pool_finish(pool, r, T - 1)




def cross(nc, psum, consts, name, heads, hd, x, context, ctx_mask, wq, bq, wk, bk, wv, bv, wo, bo, gain, shift,
          out):
    ident, half = consts
    T = 2
    CH = T * P
    ROUNDS = TOK // CH
    BR = ROUNDS // B
    W = heads * hd
    NG = W // P
    HG = P // hd
    SB, HB = 4, heads // 4
    HV = hd + 1
    OB = 2 if HV * 8 <= BANK else 4
    HO = heads // OB
    AB = W // BANK
    SCALE = float(hd) ** -0.5
    masked = ctx_mask is not None
    with ExitStack() as ctx:
        st = Stage(nc, ctx, name)
        w1, w2 = st.halves("wq", [P, KC, W]), st.halves("wo", [P, NG, D])
        bqc = st.sb("bq", [P, NG])
        kd = st.halves("k", [P, B * NG, HG * CTX])
        vc = st.sb("v", [CTX, B * heads, HV])
        mrow = st.sb("mask_row", [P, B, CTX])
        cross_context(nc, psum, ident, name, heads, hd, context, ctx_mask, wk, bk, wv, bv, kd, vc, mrow)
        split_weights(nc, f"{name}_w", [
            *((rows_of(wq)[:, j:j + 1, :], w1[0][:, j:j + 1, :], w1[1][:, j:j + 1, :])
              for j in range(KC))])
        split_weights(nc, f"{name}_u", [
            *((rows_of(wo)[:, j:j + 2, :], w2[0][:, j:j + 2, :], w2[1][:, j:j + 2, :])
              for j in range(0, NG, 2))])

        xn = st.sb("x", [P, T, D])
        xt = st.halves("xt", [P, KC, CH])
        qt = st.halves("q", [P, NG, CH])
        sc = [st.sb(f"scores{t}", [P, heads, CTX]) for t in range(T)]
        mx = [st.sb(f"max{t}", [P, heads]) for t in range(T)]
        pt = [st.sb(f"weights_t{t}", [CTX, heads, P]) for t in range(T)]
        rs = [st.sb(f"inverse{t}", [P, heads]) for t in range(T)]
        ao = [st.sb(f"att{t}", [P, W]) for t in range(T)]
        at = [st.halves(f"att_t{t}", [P, NG, P]) for t in range(T)]
        tail = Tail(st, T, x, out, bo, gain, shift, half)

        names = [f"x{t}" for t in range(T)] + [f"q{o}" for o in range(NG)]
        names += [f"s{t}{g}" for t in range(T) for g in range(SB)]
        names += [f"p{t}{g}" for t in range(T) for g in range(4)]
        names += [f"o{t}{g}" for t in range(T) for g in range(OB)]
        names += [f"a{t}{g}" for t in range(T) for g in range(AB)] + [f"y{t}" for t in range(T)]
        banks = st.banks(psum, names)
        fixed_in = st.count("bq_in", 16)
        x_in = st.count("x_in", 16)
        xt_hi, q_hi, at_hi = st.count("xt_hi"), st.count("q_hi"), st.count("att_t_hi")
        maxed, shifted, exped = (st.count(n) for n in ("scores_max", "scores_shifted", "exp_done"))
        inverted = st.count("inverted")

        def rounds(eng, one):
            with eng.Fori(0, ROUNDS) as r:
                one(r, r // BR)

        with nc.Block() as block:

            @block.sync
            def _(sp):
                sp.dma_start(bqc[:, :], bq.rearrange("(c p) -> p c", p=P), allow_slow_non_contiguous=True).then_inc(fixed_in.sem, 16)

                def load(r):
                    sp.wait_ge(banks.ready, banks.made_before(r, f"x{T - 1}"))
                    sp.dma_start(xn[:, :, :], tokens_of(x, r * CH, T)).then_inc(x_in.sem, 16)

                tail.run_sync(sp, ROUNDS, load)

            @block.tensor
            def _(pe):
                pe.sem_inc(banks.ready, len(banks.names))
                for sem in banks.read:
                    pe.sem_inc(sem, 1)

                def one(r, b):
                    pe.wait_ge(x_in.sem, x_in.done(r))
                    for t in range(T):
                        pe.wait_ge(banks.read_of(f"x{t}"), banks.free(r, f"x{t}"))
                        for c in range(KC):
                            last = pe.transpose(banks.bank(f"x{t}")[:, c * P:(c + 1) * P],
                                                xn[:, t, c * P:(c + 1) * P], ident[:, :])
                        last.then_inc(banks.ready, 1)
                    for t in range(T):
                        pe.wait_ge(banks.read_of(f"x{t}"), banks.drained(r, f"x{t}"))
                    for o in range(NG):
                        pe.wait_ge(banks.read_of(f"q{o}"), banks.free(r, f"q{o}"))
                        for c in range(KC):
                            last = product(pe, banks.bank(f"q{o}")[:, 0:CH], [h[:, c, o * P:(o + 1) * P] for h in w1],
                                           [h[:, c, :] for h in xt], c == 0, c == KC - 1)
                        last.then_inc(banks.ready, 1)
                    GB = NG // SB
                    for t in range(T):
                        for g in range(SB):
                            pe.wait_ge(banks.read_of(f"s{t}{g}"), banks.free(r, f"s{t}{g}"))
                            for m in range(GB):
                                o = g * GB + m
                                if t == 0:
                                    pe.wait_ge(banks.read_of(f"q{o}"), banks.drained(r, f"q{o}"))
                                last = product(pe, banks.bank(f"s{t}{g}")[:, m * HG * CTX:(m + 1) * HG * CTX],
                                               [h[:, o, t * P:(t + 1) * P] for h in qt],
                                               [h[:, bass.ds(b * NG + o, 1), :].rearrange("p o n -> p (o n)")
                                                for h in kd], True, True)
                            last.then_inc(banks.ready, 1)
                    for t in range(T):
                        for g in range(4):
                            pe.wait_ge(banks.read_of(f"p{t}{g}"), banks.free(r, f"p{t}{g}"))
                            pe.wait_ge(exped.sem, exped.done(r * (T * SB) + (t * SB + g)))
                            for h in range(4):
                                last = pe.transpose(banks.bank(f"p{t}{g}")[0:CTX, h * P:(h + 1) * P],
                                                    sc[t][:, g * 4 + h, :], ident[:, :])
                            last.then_inc(banks.ready, 1)
                    for t in range(T):
                        for g in range(OB):
                            pe.wait_ge(banks.read_of(f"o{t}{g}"), banks.free(r, f"o{t}{g}"))
                            for q in range(4):
                                if q * 4 < (g + 1) * HO and g * HO < (q + 1) * 4:
                                    pe.wait_ge(banks.read_of(f"p{t}{q}"), banks.drained(r, f"p{t}{q}"))
                            for h in range(HO):
                                last = pe.matmul(banks.bank(f"o{t}{g}")[:, h * HV:(h + 1) * HV],
                                                 pt[t][:, g * HO + h, :],
                                                 vc[:, bass.ds(b * heads + (g * HO + h), 1), :].rearrange(
                                                     "p o n -> p (o n)"), start=True, stop=True)
                            last.then_inc(banks.ready, 1)
                    for t in range(T):
                        for g in range(AB):
                            pe.wait_ge(banks.read_of(f"a{t}{g}"), banks.free(r, f"a{t}{g}"))
                            for q in range(g * (OB // AB), (g + 1) * (OB // AB)):
                                pe.wait_ge(banks.read_of(f"o{t}{q}"), banks.drained(r, f"o{t}{q}"))
                            for c in range(4):
                                o = g * 4 + c
                                last = pe.transpose(banks.bank(f"a{t}{g}")[:, c * P:(c + 1) * P],
                                                    ao[t][:, o * P:(o + 1) * P], ident[:, :])
                            last.then_inc(banks.ready, 1)
                    for t in range(T):
                        pe.wait_ge(banks.read_of(f"y{t}"), banks.free(r, f"y{t}"))
                        for g in range(AB):
                            pe.wait_ge(banks.read_of(f"a{t}{g}"), banks.drained(r, f"a{t}{g}"))
                            for c in range(4 * g, 4 * g + 4):
                                last = product(pe, banks.bank(f"y{t}"), [h[:, c, :] for h in at[t]],
                                               [h[:, c, :] for h in w2], c == 0, c == NG - 1)
                        last.then_inc(banks.ready, 1)

                rounds(pe, one)

            @block.scalar
            def _(act):
                act.wait_ge(fixed_in.sem, fixed_in.done(0))

                def one(r, b):
                    for t in range(T):
                        act.wait_ge(banks.ready, banks.made(r, f"x{t}"))
                        act.activation(xt[0][:, :, t * P:(t + 1) * P],
                                                banks.bank(f"x{t}").rearrange("p (c q) -> p c q", q=P), ACT.Copy).then_inc(xt_hi.sem, 1)
                    for o in range(NG):
                        act.wait_ge(banks.ready, banks.made(r, f"q{o}"))
                        act.activation(qt[0][:, o, :], banks.bank(f"q{o}")[:, 0:CH], ACT.Identity,
                                               bias=bqc[:, o:o + 1]).then_inc(q_hi.sem, 1)
                    for t in range(T):
                        for g in range(SB):
                            part = sc[t][:, g * HB:(g + 1) * HB, :].rearrange("p h k -> p (h k)")
                            if masked:
                                act.wait_ge(shifted.sem, shifted.done(r * (T * SB) + (t * SB + g)))
                            else:
                                act.wait_ge(banks.read_of(f"s{t}{g}"), banks.drained(r, f"s{t}{g}"))
                            act.activation(part, part, ACT.Exp, scale=SCALE).then_inc(exped.sem, 1)
                    for t in range(T):
                        for g in range(4):
                            act.wait_ge(banks.ready, banks.made(r, f"p{t}{g}"))
                            act.activation(
                                pt[t][:, 4 * g:4 * g + 4, :].rearrange("p h q -> p (h q)"),
                                banks.bank(f"p{t}{g}")[0:CTX, :], ACT.Copy).then_inc(banks.read_of(f"p{t}{g}"), 1)
                    for t in range(T):
                        for g in range(AB):
                            act.wait_ge(banks.ready, banks.made(r, f"a{t}{g}"))
                            act.activation(
                                at[t][0][:, 4 * g:4 * g + 4, :].rearrange("p c q -> p (c q)"),
                                banks.bank(f"a{t}{g}"), ACT.Copy).then_inc(at_hi.sem, 1)

                rounds(act, one)

            @block.vector
            def _(dve):
                tail.start_dve(dve)

                def one(r, b):
                    for t in range(T):
                        dve.wait_ge(xt_hi.sem, xt_hi.done(r * T + t))
                        dve.tensor_tensor(
                            xt[1][:, :, t * P:(t + 1) * P], banks.bank(f"x{t}").rearrange("p (c q) -> p c q", q=P),
                            xt[0][:, :, t * P:(t + 1) * P].bitcast(F32), ALU.subtract).then_inc(banks.read_of(f"x{t}"), 1)
                    for o in range(NG):
                        dve.wait_ge(q_hi.sem, q_hi.done(r * NG + o))
                        dve.scalar_tensor_tensor(
                            qt[1][:, o, :], banks.bank(f"q{o}")[:, 0:CH], bqc[:, o:o + 1],
                            qt[0][:, o, :].bitcast(F32), ALU.add, ALU.subtract).then_inc(banks.read_of(f"q{o}"), 1)
                    for t in range(T):
                        for g in range(SB):
                            n = r * (T * SB) + (t * SB + g)
                            res = banks.bank(f"s{t}{g}")[:, 0:HB * CTX].rearrange("p (h k) -> p h k", k=CTX)
                            part = sc[t][:, g * HB:(g + 1) * HB, :]
                            top = mx[t][:, g * HB:(g + 1) * HB]
                            dve.wait_ge(banks.ready, banks.made(r, f"s{t}{g}"))
                            if masked:
                                dve.tensor_tensor(
                                    part, res, mrow[:, bass.ds(b, 1), :].to_broadcast([P, HB, CTX]), ALU.add).then_inc(banks.read_of(f"s{t}{g}"), 1)
                                dve.wait_ge(banks.read_of(f"s{t}{g}"), banks.drained(r, f"s{t}{g}"))
                                dve.tensor_reduce(top, part, AX.X, ALU.max).then_inc(maxed.sem, 1)
                                dve.wait_ge(maxed.sem, maxed.done(n))
                                dve.tensor_tensor(part, part, top.unsqueeze(2).to_broadcast(
                                    [P, HB, CTX]), ALU.subtract).then_inc(shifted.sem, 1)
                            else:
                                dve.tensor_reduce(top, res, AX.X, ALU.max).then_inc(maxed.sem, 1)
                                dve.wait_ge(maxed.sem, maxed.done(n))
                                dve.tensor_tensor(part, res, top.unsqueeze(2).to_broadcast(
                                    [P, HB, CTX]), ALU.subtract).then_inc(banks.read_of(f"s{t}{g}"), 1)
                    for t in range(T):
                        for g in range(OB):
                            n = r * (T * OB) + (t * OB + g)
                            res = banks.bank(f"o{t}{g}")[:, 0:HO * HV].rearrange("p (h d) -> p h d", d=HV)
                            inv = rs[t][:, g * HO:(g + 1) * HO]
                            dve.wait_ge(banks.ready, banks.made(r, f"o{t}{g}"))
                            dve.reciprocal(inv, res[:, :, hd:].rearrange("p h d -> p (h d)")).then_inc(inverted.sem, 1)
                            dve.wait_ge(inverted.sem, inverted.done(n))
                            dve.tensor_tensor(
                                ao[t][:, g * HO * hd:(g + 1) * HO * hd].rearrange("p (h d) -> p h d", d=hd),
                                res[:, :, 0:hd], inv.unsqueeze(2).to_broadcast([P, HO, hd]), ALU.mult).then_inc(banks.read_of(f"o{t}{g}"), 1)
                    for t in range(T):
                        for g in range(AB):
                            dve.wait_ge(at_hi.sem, at_hi.done(r * (T * AB) + (t * AB + g)))
                            dve.tensor_tensor(
                                at[t][1][:, 4 * g:4 * g + 4, :].rearrange("p c q -> p (c q)"),
                                banks.bank(f"a{t}{g}"),
                                at[t][0][:, 4 * g:4 * g + 4, :].rearrange("p c q -> p (c q)").bitcast(F32),
                                ALU.subtract).then_inc(banks.read_of(f"a{t}{g}"), 1)
                    for t in range(T):
                        tail.dve_sum(dve, r, t, banks, f"y{t}")
                    for t in range(T):
                        tail.dve_norm(dve, r, t)

                rounds(dve, one)

            @block.gpsimd
            def _(pool):
                tail.start_pool(pool)

                def one(r, b):
                    for t in range(T):
                        tail.pool_bias(pool, r, t)
                    for t in range(T):
                        tail.pool_rstd(pool, r, t)
                    for t in range(T):
                        tail.pool_finish(pool, r, t)

                rounds(pool, one)


def cross_context(nc, psum, ident, name, heads, hd, context, ctx_mask, wk, bk, wv, bv, kd, vc, mrow):
    W = heads * hd
    NG, HG = W // P, P // hd
    VB = W // BANK
    with ExitStack() as ctx:
        st = Stage(nc, ctx, f"{name}_context")
        wks, wvs = st.sb("wk", [P, KC, W]), st.sb("wv", [P, KC, W])
        bkc, bvr = st.sb("bk", [P, NG]), st.sb("bv", [CTX, W])
        cn = st.sb("c", [CTX, B, D])
        ct = st.sb("ct", [P, KC, B, CTX])
        mi = st.sb("mask", [P, B, CTX], I32)
        loaded, zeroed = st.sem("loaded"), st.sem("zeroed")
        made, read, hi_done, built = st.sem("made"), st.sem("read"), st.sem("hi_done"), st.sem("built")
        loads = [(wks[:, :, :], rows_of(wk)), (wvs[:, :, :], rows_of(wv)),
                 (bkc[:, :], bk.rearrange("(c p) -> p c", p=P)), (bvr[:, :], bv.partition_broadcast(CTX)),
                 (cn[:, :, :], context.rearrange("b s d -> s b d"))]
        if ctx_mask is not None:
            loads.append((mi[:, :, :], ctx_mask.partition_broadcast(P)))
        with nc.Block() as block:

            @block.sync
            def _(sp):
                for dst, src in loads:
                    sp.dma_start(dst, src, allow_slow_non_contiguous=True).then_inc(loaded, 16)

            @block.gpsimd
            def _(pool):
                for h in kd:
                    pool.memset(h[:, :, :].bitcast(F32), 0.0).then_inc(zeroed, 1)
                pool.memset(vc[:, :, hd:], 1.0).then_inc(zeroed, 1)
                pool.wait_ge(zeroed, 3)

            @block.tensor
            def _(pe):
                pe.wait_ge(loaded, 16 * len(loads))
                for b in range(B):
                    for c in range(KC):
                        last = pe.transpose(psum[:, b, c * CTX:(c + 1) * CTX], cn[:, b, c * P:(c + 1) * P],
                                            ident[0:CTX, 0:CTX])
                    last.then_inc(made, 1)
                pe.wait_ge(read, B)
                for o in range(NG):
                    if o >= 2:
                        pe.wait_ge(built, (o - 1) * B * HG)
                    for c in range(KC):
                        last = pe.matmul(psum[:, 2 + o % 2, 0:B * CTX], wks[:, c, o * P:(o + 1) * P],
                                         ct[:, c, :, :].rearrange("p b s -> p (b s)"), start=c == 0,
                                         stop=c == KC - 1)
                    last.then_inc(made, 1)
                for b in range(B):
                    for g in range(VB):
                        for c in range(KC):
                            last = pe.matmul(psum[0:CTX, 4 + b * VB + g, :], ct[:, c, b, :],
                                             wvs[:, c, g * BANK:(g + 1) * BANK], start=c == 0, stop=c == KC - 1)
                        last.then_inc(made, 1)

            @block.scalar
            def _(act):
                act.wait_ge(zeroed, 3)
                act.wait_ge(loaded, 16 * len(loads))
                for o in range(NG):
                    act.wait_ge(made, B + o + 1)
                    for b in range(B):
                        for h in range(HG):
                            rows = slice(h * hd, (h + 1) * hd)
                            act.activation(kd[0][rows, b * NG + o, h * CTX:(h + 1) * CTX],
                                           psum[rows, 2 + o % 2, b * CTX:(b + 1) * CTX], ACT.Identity,
                                           bias=bkc[rows, o:o + 1]).then_inc(hi_done, 1)

            @block.vector
            def _(dve):
                dve.wait_ge(zeroed, 3)
                dve.wait_ge(loaded, 16 * len(loads))
                for b in range(B):
                    dve.wait_ge(made, b + 1)
                    dve.tensor_copy(ct[:, :, b, :], psum[:, b, 0:KC * CTX].rearrange(
                        "p (c s) -> p c s", s=CTX)).then_inc(read, 1)
                n = 0
                for o in range(NG):
                    dve.wait_ge(hi_done, (o + 1) * B * HG)
                    for b in range(B):
                        for h in range(HG):
                            rows = slice(h * hd, (h + 1) * hd)
                            n += 1
                            dst = kd[1][rows, b * NG + o, h * CTX:(h + 1) * CTX]
                            dve.scalar_tensor_tensor(
                                dst, psum[rows, 2 + o % 2, b * CTX:(b + 1) * CTX], bkc[rows, o:o + 1],
                                kd[0][rows, b * NG + o, h * CTX:(h + 1) * CTX].bitcast(F32),
                                ALU.add, ALU.subtract).then_inc(built, 1)
                k = B
                for b in range(B):
                    for g in range(VB):
                        dve.wait_ge(made, B + NG + b * VB + g + 1)
                        hb = BANK // hd
                        dve.tensor_tensor(
                            vc[:, b * heads + g * hb:b * heads + (g + 1) * hb, 0:hd],
                            psum[0:CTX, 4 + b * VB + g, :].rearrange("p (h d) -> p h d", d=hd),
                            bvr[:, g * BANK:(g + 1) * BANK].rearrange("p (h d) -> p h d", d=hd),
                            ALU.add).then_inc(read, 1)
                        k += 1
                if ctx_mask is not None:
                    dve.tensor_scalar(mrow[:, :, :], mi[:, :, :], 0.0, -BIG, ALU.is_equal, ALU.mult).then_inc(read, 1)
                    k += 1
                dve.wait_ge(read, k)
                dve.wait_ge(built, n)




def feed(nc, psum, consts, x, w1, b1, w2, b2, gain, shift, out):
    ident, half = consts
    T = 2
    CH = T * P
    ROUNDS = TOK // CH
    NF = FF // P
    NR = 4
    with ExitStack() as ctx:
        st = Stage(nc, ctx, "feed")
        wa, wb = st.halves("w1", [P, KC, FF]), st.halves("w2", [P, NF, D])
        split_weights(nc, "feed_w1", [(rows_of(w1)[:, j:j + 1, :], wa[0][:, j:j + 1, :], wa[1][:, j:j + 1, :])
                                      for j in range(KC)])
        split_weights(nc, "feed_w2", [(rows_of(w2)[:, j:j + 4, :], wb[0][:, j:j + 4, :], wb[1][:, j:j + 4, :])
                                      for j in range(0, NF, 4)])
        b1c = st.sb("b1", [P, NF])
        xn = st.sb("x", [P, T, D])
        xt = st.halves("xt", [P, KC, CH])
        hf = st.sb("hidden", [P, NR, CH])
        ht = st.halves("ht", [P, NF, CH])
        tail = Tail(st, T, x, out, b2, gain, shift, half)
        banks = st.banks(psum, [f"x{t}" for t in range(T)] + [f"h{o}" for o in range(NF)]
                         + [f"y{t}" for t in range(T)])
        b1_in, x_in, xt_hi = st.count("b1_in", 16), st.count("x_in", 16), st.count("xt_hi")
        h_hi, h_split = st.count("hidden_hi"), st.count("hidden_split", ahead=NR)
        with nc.Block() as block:

            @block.sync
            def _(sp):
                sp.dma_start(b1c[:, :], b1.rearrange("(c p) -> p c", p=P), allow_slow_non_contiguous=True).then_inc(b1_in.sem, 16)

                def load(r):
                    sp.wait_ge(banks.ready, banks.made_before(r, f"x{T - 1}"))
                    sp.dma_start(xn[:, :, :], tokens_of(x, r * CH, T)).then_inc(x_in.sem, 16)

                tail.run_sync(sp, ROUNDS, load)

            @block.tensor
            def _(pe):
                pe.sem_inc(banks.ready, len(banks.names))
                for sem in banks.read:
                    pe.sem_inc(sem, 1)
                with pe.Fori(0, ROUNDS) as r:
                    pe.wait_ge(x_in.sem, x_in.done(r))
                    for t in range(T):
                        pe.wait_ge(banks.read_of(f"x{t}"), banks.free(r, f"x{t}"))
                        for c in range(KC):
                            last = pe.transpose(banks.bank(f"x{t}")[:, c * P:(c + 1) * P],
                                                xn[:, t, c * P:(c + 1) * P], ident[:, :])
                        last.then_inc(banks.ready, 1)
                    for t in range(T):
                        pe.wait_ge(banks.read_of(f"x{t}"), banks.drained(r, f"x{t}"))
                    for o in range(NF):
                        pe.wait_ge(banks.read_of(f"h{o}"), banks.free(r, f"h{o}"))
                        for c in range(KC):
                            last = product(pe, banks.bank(f"h{o}")[:, 0:CH], [h[:, c, o * P:(o + 1) * P] for h in wa],
                                           [h[:, c, :] for h in xt], c == 0, c == KC - 1)
                        last.then_inc(banks.ready, 1)
                    for t in range(T):
                        pe.wait_ge(banks.read_of(f"y{t}"), banks.free(r, f"y{t}"))
                        for o in range(NF):
                            if t == 0:
                                pe.wait_ge(h_split.sem, h_split.done(r * NF + o))
                            last = product(pe, banks.bank(f"y{t}"), [h[:, o, t * P:(t + 1) * P] for h in ht],
                                           [h[:, o, :] for h in wb], o == 0, o == NF - 1)
                        last.then_inc(banks.ready, 1)

            @block.scalar
            def _(act):
                act.wait_ge(b1_in.sem, b1_in.done(0))
                with act.Fori(0, ROUNDS) as r:
                    for t in range(T):
                        act.wait_ge(banks.ready, banks.made(r, f"x{t}"))
                        act.activation(xt[0][:, :, t * P:(t + 1) * P],
                                                banks.bank(f"x{t}").rearrange("p (c q) -> p c q", q=P), ACT.Copy).then_inc(xt_hi.sem, 1)
                    for o in range(NF):
                        act.wait_ge(banks.ready, banks.made(r, f"h{o}"))
                        act.wait_ge(h_split.sem, h_split.room(r * NF + o, NR))
                        act.activation(hf[:, o % NR, :], banks.bank(f"h{o}")[:, 0:CH], ACT.Relu,
                                                     bias=b1c[:, o:o + 1]).then_inc(banks.read_of(f"h{o}"), 1)

            @block.vector
            def _(dve):
                tail.start_dve(dve)
                dve.sem_inc(h_split.sem, h_split.start)
                with dve.Fori(0, ROUNDS) as r:
                    for t in range(T):
                        dve.wait_ge(xt_hi.sem, xt_hi.done(r * T + t))
                        dve.tensor_tensor(
                            xt[1][:, :, t * P:(t + 1) * P], banks.bank(f"x{t}").rearrange("p (c q) -> p c q", q=P),
                            xt[0][:, :, t * P:(t + 1) * P].bitcast(F32), ALU.subtract).then_inc(banks.read_of(f"x{t}"), 1)
                    dve.wait_ge(banks.ready, banks.made_before(r, f"y{T - 1}"))
                    for o in range(NF):
                        dve.wait_ge(banks.read_of(f"h{o}"), banks.drained(r, f"h{o}"))
                        dve.tensor_copy(ht[0][:, o, :], hf[:, o % NR, :]).then_inc(h_hi.sem, 1)
                        dve.wait_ge(h_hi.sem, h_hi.done(r * NF + o))
                        dve.tensor_tensor(ht[1][:, o, :], hf[:, o % NR, :], ht[0][:, o, :].bitcast(F32),
                                                     ALU.subtract).then_inc(h_split.sem, 1)
                    for t in range(T):
                        tail.dve_sum(dve, r, t, banks, f"y{t}")
                        tail.dve_norm(dve, r, t)

            @block.gpsimd
            def _(pool):
                tail.start_pool(pool)
                with pool.Fori(0, ROUNDS) as r:
                    for t in range(T):
                        tail.pool_bias(pool, r, t)
                        tail.pool_rstd(pool, r, t)
                        tail.pool_finish(pool, r, t)




def build(nc, a, out):
    def scratch(name, shape, dt=F32):
        return nc.dram_tensor(name, shape, dt, kind="Internal").ap()

    halves = [scratch(f"{n}_halves", (2, B * D, S)) for n in "qk"]
    v_dram = scratch("v_ones", (TOK, H0 * (HD0 + 1)))
    bias_dram = scratch("mask_bias", (S, S), BF16)
    att_dram = scratch("attention", (B * H0, S, HD0))
    x1, x2, x3 = (scratch(f"x_{n}", (TOK, D)) for n in ("joined", "crossed", "fed"))
    x = a["x"].rearrange("b s d -> (b s) d")
    layer = {k[9:]: v for k, v in a.items() if k.startswith("L0_xattn_")}
    second = {k[9:]: v for k, v in a.items() if k.startswith("L1_xattn_")}

    with ExitStack() as ctx:
        psum = ctx.enter_context(nc.psum_tensor("psum", [P, 8, BANK], F32))
        ident, half, ones = make_constants(nc, ctx)
        consts = (ident, half)
        with ExitStack() as inner:
            st = Stage(nc, inner, "window")
            open_max = st.sb("open_max", [P, S // P, S // KEYS])
            choice = st.sb("choice", [1, 2], I32)
            project(nc, psum, ident, x, a["mask_SxS_ik1"], [layer[f"{n}_w"] for n in "qkv"],
                    [layer[f"{n}_b"] for n in "qkv"], halves, v_dram, bias_dram, open_max)
            choose_window(nc, psum, ones, open_max, choice)
            one_block = nc.values_load(choice[:, 0:1], min_val=0, max_val=1)
            block = nc.values_load(choice[:, 1:2], min_val=0, max_val=S // KEYS - 1)
            with nc.If(one_block):
                attend(nc, psum, ident, halves, v_dram, bias_dram, att_dram, 1, block)
            with nc.Else():
                attend(nc, psum, ident, halves, v_dram, bias_dram, att_dram, S // KEYS, 0)
        join(nc, psum, consts, att_dram, x, x1, layer["o_w"], layer["o_b"], layer["ln1_g"], layer["ln1_b"])
        cross(nc, psum, consts, "cross", H0, HD0, x1, a["ctx_1024"], None, layer["cq_w"], layer["cq_b"],
              layer["ck_w"], layer["ck_b"], layer["cv_w"], layer["cv_b"], layer["co_w"], layer["co_b"],
              layer["ln2_g"], layer["ln2_b"], x2)
        feed(nc, psum, consts, x2, layer["lin1_w"], layer["lin1_b"], layer["lin2_w"], layer["lin2_b"],
             layer["ln3_g"], layer["ln3_b"], x3)
        cross(nc, psum, consts, "second", H1, HD1, x3, a["ctx_1024"], a["mask_BxS2_ik0"], second["Wq"],
              second["bq"], second["Wk"], second["bk"], second["Wv"], second["bv"], second["Wo"], second["bo"],
              second["gamma"], second["beta"], out)


def kernel(**inputs):
    import numpy as np
    import concourse.bacc as bacc
    from concourse.bass_utils import run_bass_kernel_spmd

    nc = bacc.Bacc("TRN2", target_bir_lowering=False, num_devices=1)
    arrays = {f"in_{name}": np.ascontiguousarray(a) for name, a in inputs.items()}
    given = {name: nc.dram_tensor(f"in_{name}", arrays[f"in_{name}"].shape,
                                  mybir.dt.from_np(arrays[f"in_{name}"].dtype), kind="ExternalInput").ap()
             for name in inputs}
    out = nc.dram_tensor("out", (B, S, D), F32, kind="ExternalOutput").ap()
    build(nc, given, out.rearrange("b s d -> (b s) d"))
    result = run_bass_kernel_spmd(nc, [arrays], core_ids=[0])
    return result.results[0]["out"]
```

```python
from contextlib import ExitStack

import concourse.bass as bass
from concourse import mybir

F32 = mybir.dt.float32
F32R = mybir.dt.float32r
BF16 = mybir.dt.bfloat16
I32 = mybir.dt.int32
ALU = mybir.AluOpType
ACT = mybir.ActivationFunctionType
AX = mybir.AxisListType

P = 128
B, S, D = 2, 2048, 512
TOK = B * S
KC = D // P
H0, HD0 = 16, 32
H1, HD1 = 16, 64
CTX = 77
FF = 2048
EPS = 1e-5
BIG = 2.0 ** 126
BANK = 512
KEYS = 512


class Count:

    def __init__(self, sem, step=1, ahead=0):
        self.sem, self.step, self.ahead, self.start = sem, step, ahead, step * ahead

    def done(self, n):
        return n * self.step + self.step * (self.ahead + 1)

    def room(self, n, ring):
        assert ring <= self.ahead
        return n * self.step + self.step * (self.ahead + 1 - ring)


class Banks:

    def __init__(self, psum, ready, read, names):
        self.psum, self.ready, self.read, self.names = psum, ready, read, names
        self.at = {name: n for n, name in enumerate(names)}
        self.per_bank = [len(range(b, len(names), 8)) for b in range(8)]
        assert len(self.at) == len(names) >= 8

    def bank(self, name):
        return self.psum[:, self.at[name] % 8, :]

    def read_of(self, name):
        return self.read[self.at[name] % 8]

    def free(self, rnd, name):
        n = self.at[name]
        return rnd * self.per_bank[n % 8] + (n // 8 + 1)

    def drained(self, rnd, name):
        n = self.at[name]
        return rnd * self.per_bank[n % 8] + (n // 8 + 2)

    def made(self, rnd, name):
        return rnd * len(self.names) + (len(self.names) + self.at[name] + 1)

    def made_before(self, rnd, name):
        return rnd * len(self.names) + (self.at[name] + 1)


def product(pe, out, w, x, first, last):
    pe.matmul(out, w[1], x[0], start=first, stop=False)
    pe.matmul(out, w[0], x[1], start=False, stop=False)
    return pe.matmul(out, w[0], x[0], start=False, stop=last)


class Stage:

    def __init__(self, nc, ctx, name):
        self.nc, self.ctx, self.name, self.sems = nc, ctx, name, []
        ctx.push(self.clear)

    def clear(self, failed, *_):
        if failed:
            return
        with self.nc.Block() as block:

            @block.gpsimd
            def _(pool):
                self.nc.clear_and_free_semaphores(self.sems)

    def sb(self, name, shape, dt=F32):
        return self.ctx.enter_context(self.nc.sbuf_tensor(f"{self.name}_{name}", shape, dt))

    def halves(self, name, shape):
        return [self.sb(f"{name}_{h}", shape, F32R) for h in ("hi", "lo")]

    def sem(self, name):
        self.sems.append(self.nc.alloc_semaphore(f"{self.name}_{name}"))
        return self.sems[-1]

    def count(self, name, step=1, ahead=0):
        return Count(self.sem(name), step, ahead)

    def banks(self, psum, names):
        return Banks(psum, self.sem("ready"), [self.sem(f"read{b}") for b in range(8)], names)


def rows_of(m):
    return m.rearrange("(c p) n -> p c n", p=P)


def tokens_of(m, first, tiles):
    return m[bass.ds(first, tiles * P), :].rearrange("(t p) n -> p t n", p=P)


def split_weights(nc, name, jobs):
    shape = list(jobs[0][0].shape)
    with ExitStack() as ctx:
        st = Stage(nc, ctx, name)
        raw = [st.sb(f"raw{s}", shape) for s in range(2)]
        loaded = [st.count(f"raw{s}_loaded", 16) for s in range(2)]
        hi_done, split = st.count("raw_hi"), st.count("raw_split")
        with nc.Block() as block:

            @block.sync
            def _(sp):
                for n, (src, _, _) in enumerate(jobs):
                    if n >= 2:
                        sp.wait_ge(split.sem, split.done(n - 2))
                    sp.dma_start(raw[n % 2][:, :, :], src).then_inc(loaded[n % 2].sem, 16)

            @block.scalar
            def _(act):
                for n, (_, hi, _) in enumerate(jobs):
                    act.wait_ge(loaded[n % 2].sem, loaded[n % 2].done(n // 2))
                    act.activation(hi, raw[n % 2][:, :, :], ACT.Copy).then_inc(hi_done.sem, 1)

            @block.vector
            def _(dve):
                for n, (_, hi, lo) in enumerate(jobs):
                    dve.wait_ge(hi_done.sem, hi_done.done(n))
                    dve.tensor_tensor(lo, raw[n % 2][:, :, :], hi.bitcast(F32), ALU.subtract).then_inc(split.sem, 1)
                dve.wait_ge(split.sem, split.done(len(jobs) - 1))


def make_constants(nc, ctx):
    st = Stage(nc, ctx, "const")
    ident, half, ones = st.sb("ident", [P, P]), st.sb("minus_half", [P, 1]), st.sb("ones", [P, P])
    made = st.sem("made")
    with nc.Block() as block:

        @block.gpsimd
        def _(pool):
            pool.memset(ident[:, :], 0.0).then_inc(made, 1)
            pool.memset(half[:, :], -0.5).then_inc(made, 1)
            pool.memset(ones[:, :], 1.0).then_inc(made, 1)
            pool.wait_ge(made, 3)
            pool.affine_select(out=ident[:, :], in_=ident[:, :], compare_op=ALU.not_equal, fill=1.0,
                               base=0, pattern=[[-1, P]], channel_multiplier=1).then_inc(made, 1)
            pool.wait_ge(made, 4)

    return ident, half, ones


class Tail:

    def __init__(self, st, tiles, residual, out, bias, gain, shift, minus_half):
        assert tiles % 2 == 0
        self.tiles, self.residual, self.out, self.half = tiles, residual, out, minus_half
        self.rows_dram = (bias, gain, shift)
        self.rows = [st.sb(f"row_{n}", [P, D]) for n in ("bias", "gain", "shift")]
        self.res = [st.sb(f"residual{s}", [P, D]) for s in range(2)]
        self.sum = [st.sb(f"sum{s}", [P, D]) for s in range(2)]
        self.y = [st.sb(f"normed{s}", [P, D]) for s in range(2)]
        self.stats = [st.sb(f"stats{s}", [P, 6]) for s in range(2)]
        self.mean_var = [st.sb(f"mean_var{s}", [P, 2]) for s in range(2)]
        self.var_eps = [st.sb(f"var_eps{s}", [P, 1]) for s in range(2)]
        self.rstd = [st.sb(f"rstd{s}", [P, 1]) for s in range(2)]
        self.rows_in = st.count("rows_in", 16)
        self.passed = st.sem("waits_passed")
        self.res_in = [st.count(f"residual_in{s}", 16) for s in range(2)]
        self.biased = st.count("residual_biased")
        self.stats_done = st.count("stats_done")
        self.var_done = st.count("variance_done", ahead=2)
        self.eps_added = st.count("eps_added")
        self.rstd_done = st.count("rstd_done")
        self.normed = st.count("normed")
        self.gained = st.count("gained", ahead=2)
        self.finished = st.count("finished")
        self.stored = [st.count(f"stored{s}", 16, 1) for s in range(2)]

    def tile(self, rnd, t):
        return rnd * self.tiles + t, rnd * (self.tiles // 2) + t // 2, t % 2

    def load_rows(self, sp):
        for row, src in zip(self.rows, self.rows_dram):
            sp.dma_start(row[:, :], src.partition_broadcast(P)).then_inc(self.rows_in.sem, 16)

    def load(self, sp, rnd, t):
        n, k, s = self.tile(rnd, t)
        sp.wait_ge(self.var_done.sem, self.var_done.room(n, 2))
        sp.dma_start(self.res[s][:, :], self.residual[bass.ds(n * P, P), :]).then_inc(self.res_in[s].sem, 16)

    def start_dve(self, dve):
        dve.sem_inc(self.var_done.sem, self.var_done.start)

    def store(self, sp, rnd, t):
        n, k, s = self.tile(rnd, t)
        sp.wait_ge(self.finished.sem, self.finished.done(n))
        sp.dma_start(self.out[bass.ds(n * P, P), :], self.y[s][:, :]).then_inc(self.stored[s].sem, 16)

    def run_sync(self, sp, rounds, load_x, parts=1):
        def part(rnd, p, last):
            if not (last and p == parts - 1):
                load_x(rnd * parts + (p + 1))
            for t in range(p * self.tiles // parts, (p + 1) * self.tiles // parts):
                if not (last and t + 2 >= self.tiles):
                    self.load(sp, rnd, t + 2)
                self.store(sp, rnd, t)

        for c in self.stored:
            sp.sem_inc(c.sem, c.start)
        self.load_rows(sp)
        load_x(0)
        for t in range(2):
            self.load(sp, 0, t)
        with sp.Fori(0, rounds - 1) as r:
            for p in range(parts):
                part(r, p, False)
        for p in range(parts):
            part(rounds - 1, p, True)
        for c in self.stored:
            sp.wait_ge(c.sem, c.done(rounds * (self.tiles // 2) - 1))

    def start_pool(self, pool):
        pool.sem_inc(self.gained.sem, self.gained.start)
        pool.wait_ge(self.rows_in.sem, self.rows_in.done(2))

    def pool_bias(self, pool, rnd, t):
        n, k, s = self.tile(rnd, t)
        pool.wait_ge(self.res_in[s].sem, self.res_in[s].done(k))
        pool.tensor_tensor(self.res[s][:, :], self.res[s][:, :], self.rows[0][:, :], ALU.add).then_inc(self.biased.sem, 1)

    def dve_sum(self, dve, rnd, t, banks, name):
        n, k, s = self.tile(rnd, t)
        dve.wait_ge(self.biased.sem, self.biased.done(n))
        dve.wait_ge(self.gained.sem, self.gained.room(n, 2))
        dve.wait_ge(banks.ready, banks.made(rnd, name))
        dve.tensor_tensor(self.sum[s][:, :], banks.bank(name), self.res[s][:, :], ALU.add).then_inc(banks.read_of(name), 1)
        dve.wait_ge(banks.read_of(name), banks.drained(rnd, name))
        dve.bn_stats(self.stats[s][:, :], self.sum[s][:, :]).then_inc(self.stats_done.sem, 1)
        dve.wait_ge(self.stats_done.sem, self.stats_done.done(n))
        dve.sem_inc(self.passed, 1)
        dve.bn_aggr(self.mean_var[s][:, :], self.stats[s][:, :]).then_inc(self.var_done.sem, 1)

    def pool_rstd(self, pool, rnd, t):
        n, k, s = self.tile(rnd, t)
        pool.wait_ge(self.var_done.sem, self.var_done.done(n))
        pool.sem_inc(self.passed, 1)
        pool.tensor_scalar(self.var_eps[s][:, :], self.mean_var[s][:, 1:2], EPS, None, ALU.add).then_inc(self.eps_added.sem, 1)
        pool.wait_ge(self.eps_added.sem, self.eps_added.done(n))
        pool.tensor_tensor(self.rstd[s][:, :], self.var_eps[s][:, :], self.half[:, :], ALU.pow).then_inc(self.rstd_done.sem, 1)

    def dve_norm(self, dve, rnd, t):
        n, k, s = self.tile(rnd, t)
        dve.wait_ge(self.rstd_done.sem, self.rstd_done.done(n))
        dve.tensor_scalar(self.sum[s][:, :], self.sum[s][:, :], self.mean_var[s][:, 0:1], self.rstd[s][:, :],
                          ALU.subtract, ALU.mult).then_inc(self.normed.sem, 1)

    def pool_finish(self, pool, rnd, t):
        n, k, s = self.tile(rnd, t)
        pool.wait_ge(self.normed.sem, self.normed.done(n))
        pool.wait_ge(self.stored[s].sem, self.stored[s].room(k, 1))
        pool.tensor_tensor(self.y[s][:, :], self.sum[s][:, :], self.rows[1][:, :], ALU.mult).then_inc(self.gained.sem, 1)
        pool.wait_ge(self.gained.sem, self.gained.done(n))
        pool.tensor_tensor(self.y[s][:, :], self.y[s][:, :], self.rows[2][:, :], ALU.add).then_inc(self.finished.sem, 1)




def project(nc, psum, ident, x, mask, weights, biases, halves, v_dram, bias_dram, open_max):
    T = 4
    CH = T * P
    BR = S // CH
    ROUNDS = B * BR
    MT = S // P // ROUNDS
    with ExitStack() as ctx:
        st = Stage(nc, ctx, "project")
        w = [st.halves(f"w{n}", [P, KC, D]) for n in "qkv"]
        split_weights(nc, "project_w", [
            (rows_of(m)[:, j:j + 2, :], h[0][:, j:j + 2, :], h[1][:, j:j + 2, :])
            for m, h in zip(weights, w) for j in range(0, KC, 2)])
        bcol = [st.sb(f"b{n}", [P, KC]) for n in "qk"]
        brow = st.sb("bv", [P, D])
        xn = st.sb("x", [P, T, D])
        xt = st.halves("xt", [P, KC, CH])
        out = [st.halves(n, [P, KC, CH]) for n in "qk"]
        vo = st.sb("v", [P, T, H0, HD0 + 1])
        mi = [st.sb(f"mask{j}", [P, S], I32) for j in range(MT)]
        mb = [st.sb(f"bias{j}", [P, S], BF16) for j in range(MT)]

        banks = st.banks(psum, [f"xt{c}" for c in range(KC)] + [f"{n}{o}" for n in "qk" for o in range(KC)]
                         + [f"v{t}" for t in range(T)])
        biases_in = st.count("biases_in", 16)
        ones_set = st.count("ones_set")
        x_in = st.count("x_in", 16)
        mask_in = [st.count(f"mask_in{j}", 16) for j in range(MT)]
        xt_hi = st.count("xt_hi")
        out_hi = st.count("qk_hi")
        bias_made = st.count("bias_made", ahead=MT)
        open_made = st.count("open_made", ahead=MT)
        halves_out = [st.count(f"{n}_stored", 32, 1) for n in "qk"]
        v_out = st.count("v_stored", 16, 1)
        bias_out = [st.count(f"bias_stored{j}", 16, 1) for j in range(MT)]

        def rounds(eng, one):
            with eng.Fori(0, ROUNDS) as r:
                one(r)

        with nc.Block() as block:

            @block.sync
            def _(sp):
                for t, src in zip(bcol, biases[:2]):
                    sp.dma_start(t[:, :], src.rearrange("(c p) -> p c", p=P), allow_slow_non_contiguous=True).then_inc(biases_in.sem, 16)
                sp.dma_start(brow[:, :], biases[2].partition_broadcast(P)).then_inc(biases_in.sem, 16)

                def load(r):
                    sp.wait_ge(banks.ready, banks.made_before(r, f"xt{KC - 1}"))
                    sp.dma_start(xn[:, :, :], tokens_of(x, r * CH, T)).then_inc(x_in.sem, 16)
                    for m in range(MT):
                        sp.wait_ge(bias_made.sem, bias_made.room(r * MT + m, MT))
                        sp.dma_start(mi[m][:, :], mask[bass.ds((r * MT + m) * P, P), :]).then_inc(mask_in[m].sem, 16)

                def store(r):
                    for m in range(MT):
                        sp.wait_ge(bias_made.sem, bias_made.done(r * MT + m))
                        sp.dma_start(bias_dram[bass.ds((r * MT + m) * P, P), :], mb[m][:, :]).then_inc(bias_out[m].sem, 16)
                    for m, n in enumerate("qk"):
                        for o in range(KC):
                            sp.wait_ge(banks.read_of(f"{n}{o}"), banks.drained(r, f"{n}{o}"))
                        for h in range(2):
                            dst = halves[m][h].rearrange("(c p) s -> p c s", p=P)[
                                :, bass.ds(r // BR * KC, KC), bass.ds(r % BR * CH, CH)]
                            sp.dma_start(dst, out[m][h][:, :, :].bitcast(F32)).then_inc(halves_out[m].sem, 16)
                    for t in range(T):
                        sp.wait_ge(banks.read_of(f"v{t}"), banks.drained(r, f"v{t}"))
                    sp.dma_start(tokens_of(v_dram, r * CH, T),
                                          vo[:, :, :, :].rearrange("p t h d -> p t (h d)")).then_inc(v_out.sem, 16)

                stores = (*halves_out, v_out, *bias_out)
                for c in stores:
                    sp.sem_inc(c.sem, c.start)
                load(0)
                with sp.Fori(0, ROUNDS - 1) as r:
                    load(r + 1)
                    store(r)
                store(ROUNDS - 1)
                for c in stores:
                    sp.wait_ge(c.sem, c.done(ROUNDS - 1))

            @block.tensor
            def _(pe):
                pe.sem_inc(banks.ready, len(banks.names))
                for sem in banks.read:
                    pe.sem_inc(sem, 1)

                def one(r):
                    pe.wait_ge(x_in.sem, x_in.done(r))
                    for c in range(KC):
                        pe.wait_ge(banks.read_of(f"xt{c}"), banks.free(r, f"xt{c}"))
                        for t in range(T):
                            last = pe.transpose(banks.bank(f"xt{c}")[:, t * P:(t + 1) * P],
                                                xn[:, t, c * P:(c + 1) * P], ident[:, :])
                        last.then_inc(banks.ready, 1)
                    for m, n in enumerate("qk"):
                        for o in range(KC):
                            pe.wait_ge(banks.read_of(f"{n}{o}"), banks.free(r, f"{n}{o}"))
                            for c in range(KC):
                                if m == 0 and o == 0:
                                    pe.wait_ge(banks.read_of(f"xt{c}"), banks.drained(r, f"xt{c}"))
                                last = product(pe, banks.bank(f"{n}{o}"),
                                               [h[:, c, o * P:(o + 1) * P] for h in w[m]],
                                               [h[:, c, :] for h in xt], c == 0, c == KC - 1)
                            last.then_inc(banks.ready, 1)
                    for t in range(T):
                        pe.wait_ge(banks.read_of(f"v{t}"), banks.free(r, f"v{t}"))
                        for c in range(KC):
                            last = product(pe, banks.bank(f"v{t}"), [h[:, c, t * P:(t + 1) * P] for h in xt],
                                           [h[:, c, :] for h in w[2]], c == 0, c == KC - 1)
                        last.then_inc(banks.ready, 1)

                rounds(pe, one)

            @block.scalar
            def _(act):
                act.wait_ge(biases_in.sem, biases_in.done(2))

                def one(r):
                    for c in range(KC):
                        act.wait_ge(banks.ready, banks.made(r, f"xt{c}"))
                        act.wait_ge(banks.ready, banks.made_before(r, f"v{T - 1}"))
                        act.activation(xt[0][:, c, :], banks.bank(f"xt{c}"), ACT.Copy).then_inc(xt_hi.sem, 1)
                    for m, n in enumerate("qk"):
                        act.wait_ge(halves_out[m].sem, halves_out[m].room(r, 1))
                        for o in range(KC):
                            act.wait_ge(banks.ready, banks.made(r, f"{n}{o}"))
                            act.activation(out[m][0][:, o, :], banks.bank(f"{n}{o}"), ACT.Identity,
                                                     bias=bcol[m][:, o:o + 1]).then_inc(out_hi.sem, 1)

                rounds(act, one)

            @block.vector
            def _(dve):
                dve.sem_inc(bias_made.sem, bias_made.start)
                dve.sem_inc(open_made.sem, open_made.start)
                dve.memset(vo[:, :, :, HD0:], 1.0).then_inc(ones_set.sem, 1)
                dve.wait_ge(ones_set.sem, ones_set.done(0))
                dve.wait_ge(biases_in.sem, biases_in.done(2))

                def one(r):
                    for c in range(KC):
                        dve.wait_ge(xt_hi.sem, xt_hi.done(r * KC + c))
                        dve.tensor_tensor(xt[1][:, c, :], banks.bank(f"xt{c}"),
                                                        xt[0][:, c, :].bitcast(F32), ALU.subtract).then_inc(banks.read_of(f"xt{c}"), 1)
                    for m in range(MT):
                        dve.wait_ge(mask_in[m].sem, mask_in[m].done(r))
                        dve.wait_ge(bias_out[m].sem, bias_out[m].room(r, 1))
                        dve.wait_ge(open_made.sem, open_made.room(r * MT + m, MT))
                        dve.tensor_scalar(mb[m][:, :], mi[m][:, :], 0.0, -BIG,
                                                       ALU.not_equal, ALU.mult).then_inc(bias_made.sem, 1)
                    for m, n in enumerate("qk"):
                        dve.wait_ge(halves_out[m].sem, halves_out[m].room(r, 1))
                        for o in range(KC):
                            dve.wait_ge(out_hi.sem, out_hi.done(r * 2 * KC + (m * KC + o)))
                            dve.scalar_tensor_tensor(
                                out[m][1][:, o, :], banks.bank(f"{n}{o}"), bcol[m][:, o:o + 1],
                                out[m][0][:, o, :].bitcast(F32), ALU.add, ALU.subtract).then_inc(banks.read_of(f"{n}{o}"), 1)
                        if m < MT:
                            dve.wait_ge(bias_made.sem, bias_made.done(r * MT + m))
                            dve.tensor_reduce(
                                open_max[:, bass.ds(r * MT + m, 1), :].rearrange("p o k -> p (o k)"),
                                mb[m][:, :].rearrange("p (k s) -> p k s", s=KEYS), AX.X, ALU.max).then_inc(open_made.sem, 1)
                    dve.wait_ge(v_out.sem, v_out.room(r, 1))
                    for t in range(T):
                        dve.wait_ge(banks.ready, banks.made(r, f"v{t}"))
                        dve.tensor_tensor(
                            vo[:, t, :, 0:HD0], banks.bank(f"v{t}").rearrange("p (h d) -> p h d", d=HD0),
                            brow[:, :].rearrange("p (h d) -> p h d", d=HD0), ALU.add).then_inc(banks.read_of(f"v{t}"), 1)

                rounds(dve, one)




def choose_window(nc, psum, ones, open_max, choice):
    NB, NT = S // KEYS, S // P
    with ExitStack() as ctx:
        st = Stage(nc, ctx, "choose")
        is_open = st.sb("is_open", [P, NT * NB])
        rows = st.sb("rows", [P, NB])
        full, empty, which = st.sb("full", [P, NB]), st.sb("empty", [P, NB]), st.sb("which", [P, NB])
        votes, res = st.sb("votes", [P, NB]), st.sb("res", [P, 2])
        place = st.sb("place", [P, NB])
        yes = st.sb("yes", [P, 2])
        step, counted = st.sem("step"), st.sem("counted")
        with nc.Block() as block:

            @block.vector
            def _(dve):
                n = 0

                def link(ins):
                    nonlocal n
                    n += 1
                    ins.then_inc(step, 1)
                    dve.wait_ge(step, n)

                link(dve.tensor_scalar(is_open[:, :], open_max[:, :, :].rearrange("p t k -> p (t k)"), 0.0, None,
                                       ALU.is_equal))
                for k in range(NB):
                    link(dve.memset(place[:, k:k + 1], float(k)))
                dve.wait_ge(counted, 1)
                link(dve.tensor_reduce(rows[:, :], psum[:, 0, 0:NT * NB].rearrange("p (t k) -> p k t", k=NB),
                                       AX.X, ALU.add))
                link(dve.tensor_scalar(full[:, :], rows[:, :], float(S), None, ALU.is_equal))
                link(dve.tensor_scalar(empty[:, :], rows[:, :], 0.0, None, ALU.is_equal))
                link(dve.scalar_tensor_tensor(votes[:, :], full[:, :], float(NB), empty[:, :], ALU.mult, ALU.add))
                link(dve.tensor_reduce(res[:, 0:1], votes[:, :], AX.X, ALU.add))
                link(dve.tensor_scalar(yes[:, 0:1], res[:, 0:1], float(2 * NB - 1), None, ALU.is_equal))
                link(dve.tensor_tensor(which[:, :], full[:, :], place[:, :], ALU.mult))
                link(dve.tensor_reduce(res[:, 1:2], which[:, :], AX.X, ALU.add))
                link(dve.tensor_tensor(yes[:, 1:2], res[:, 1:2], yes[:, 0:1], ALU.mult))
                link(dve.tensor_copy(choice[:, :], yes[0:1, :]))

            @block.tensor
            def _(pe):
                pe.wait_ge(step, 1)
                pe.matmul(psum[:, 0, 0:NT * NB], ones[:, :], is_open[:, :], start=True, stop=True).then_inc(counted, 1)


def attend(nc, psum, ident, halves, v_dram, bias_dram, att_dram, sums_dram, blocks, first):
    NK = blocks * KEYS
    G = 4
    NT = S // P
    TG = G // blocks
    HU = 2 if blocks == 1 else 1
    KT = KEYS // P
    U = G * HU
    SETS = 2 if blocks == 1 else 1
    NS = HU * NT * blocks
    N = SETS * NS
    WS, HEADS = NS // U, SETS * HU
    ROUNDS = B * H0 // HEADS
    HV = HD0 + 1
    PLACES = 16 if blocks == 1 else 8
    QW = TG * P
    MV = 2 * HD0
    SCORE, EXP, TURN = (17, 12, 9) if blocks == 1 else (10, 6, 5)
    assert N % PLACES == 0 and N // G % 4 == 0 and N // U % 2 == 0
    SCALE = float(HD0) ** -0.5
    TOFS, OOFS = 4, 6
    with ExitStack() as ctx:
        st = Stage(nc, ctx, f"attend{blocks}")
        bias = st.sb("bias", [P, NT, NK], BF16)
        v = st.sb("v", [P, NK // P, B, H0 * HV])
        kst, qst = ([[st.sb(f"{n}{m}{u}", [P, width], F32R) for u in range(HU)] for m in range(SETS)]
                    for n, width in (("k", NK), ("q", S)))
        pr = st.sb("weights", [P, PLACES, KEYS])
        pt = [[st.sb(f"weights_t{s}{u}", [P, G, KEYS]) for u in range(HU)] for s in range(2)]
        mx = st.sb("max", [P, 4, G])
        gmx = st.sb("group_max", [P, 4])
        neg = st.sb("neg_max", [P, 4, G])
        vh = [[st.sb(f"v_of_head{m}{u}", [P, NK // P, MV]) for u in range(HU)] for m in range(SETS)]
        ao = [st.sb(f"out{m}", [HU * MV, S]) for m in range(SETS)]

        fixed_in = st.count("bias_v_in", 16)
        passed = st.sem("waits_passed")
        kq_in = [st.count(f"kq_in{m}", 16 * 8 * HU) for m in range(SETS)]
        scored = st.count("scored", ahead=N)
        masked = st.count("masked", ahead=4)
        group_max = st.count("group_max_done")
        shifted = st.count("shift_done")
        exped = st.count("exp_done")
        turned = st.count("transposed", ahead=PLACES)
        moved = st.count("transposed_moved", ahead=2)
        summed = st.count("summed", ahead=max(2 * G, N // U * G))
        ones_set = st.count("ones_set")
        v_here = [st.count(f"v_of_head{m}", HU) for m in range(SETS)]
        taken = st.count("sums_taken", ahead=2)
        stored = [st.count(f"stored{m}", 32 * HU, 1) for m in range(SETS)]

        def place(n):
            m, k = n // NS, n % NS
            return (m, k % U // G, k // U * G + k % G, 0) if blocks == 1 else (m, 0, k // G, k % G)

        with nc.Block() as block:

            @block.sync
            def _(sp):
                sp.dma_start(bias[:, :, :], bias_dram[:, bass.ds(first * KEYS, NK)].rearrange(
                    "(t p) s -> p t s", p=P)).then_inc(fixed_in.sem, 16)
                for b in range(B):
                    sp.dma_start(v[:, :, b, :], v_dram[bass.ds(first * KEYS + b * S, NK), :].rearrange(
                        "(t p) n -> p t n", p=P)).then_inc(fixed_in.sem, 16)

                def load(i, m):
                    sp.wait_ge(scored.sem, scored.room(i * N + ((m + 1) * NS - 1), N))
                    for u in range(HU):
                        row = i * (HEADS * HD0) + (m * HU + u) * HD0
                        for part in range(4):
                            rows = slice(part * HD0, (part + 1) * HD0)
                            sp.dma_start(kst[m][u][rows, :].bitcast(F32), halves[1][part % 2][
                                bass.ds(row, HD0), bass.ds(first * KEYS, NK)]).then_inc(kq_in[m].sem, 16)
                            sp.dma_start(qst[m][u][rows, :].bitcast(F32), halves[0][part // 2][
                                bass.ds(row, HD0), :]).then_inc(kq_in[m].sem, 16)

                def store(i, m):
                    sp.wait_ge(taken.sem, taken.done(i * (N // U) + ((m + 1) * WS - 1)))
                    for u in range(HU):
                        head = i * HEADS + (m * HU + u)
                        sp.dma_start(att_dram[bass.ds(head * HD0, HD0), :],
                                     ao[m][u * MV:u * MV + HD0, :]).then_inc(stored[m].sem, 16)
                        sp.dma_start(sums_dram[bass.ds(head, 1), :],
                                     ao[m][u * MV + HD0:u * MV + HD0 + 1, :]).then_inc(stored[m].sem, 16)

                for m in range(SETS):
                    load(0, m)
                with sp.Fori(0, ROUNDS - 1) as i:
                    for m in range(SETS):
                        load(i + 1, m)
                        store(i, m)
                for m in range(SETS):
                    store(ROUNDS - 1, m)
                for m in range(SETS):
                    sp.wait_ge(stored[m].sem, stored[m].done(ROUNDS - 1))

            @block.tensor
            def _(pe):
                pe.sem_inc(scored.sem, scored.start)
                pe.sem_inc(turned.sem, turned.start)
                pe.sem_inc(summed.sem, summed.start)
                pe.wait_ge(fixed_in.sem, fixed_in.done(B))

                def score(i, n):
                    m, u, qt, kb = place(n)
                    if n % NS == 0:
                        pe.wait_ge(kq_in[m].sem, kq_in[m].done(i))
                    pe.wait_ge(masked.sem, masked.room(i * N + n, 4))
                    pe.matmul(psum[:, n % 4, :], qst[m][u][:, qt * P:(qt + 1) * P],
                                        kst[m][u][:, kb * KEYS:(kb + 1) * KEYS], start=True, stop=True).then_inc(scored.sem, 1)

                def turn(i, n):
                    pe.wait_ge(exped.sem, exped.done(i * N + n))
                    pe.wait_ge(moved.sem, moved.room(i * N + n, 2))
                    for c in range(KT):
                        last = pe.transpose(psum[:, TOFS + n % 2, c * P:(c + 1) * P],
                                            pr[:, n % PLACES, c * P:(c + 1) * P], ident[:, :])
                    last.then_inc(turned.sem, 1)

                def weigh(i, n):
                    w, k, m = n // U, n % U, n // NS
                    if n % NS == 0:
                        pe.wait_ge(v_here[m].sem, v_here[m].done(i))
                    if k == 0:
                        pe.wait_ge(moved.sem, moved.done(i * N + n + (U - 1)))
                        pe.wait_ge(taken.sem, taken.room(i * (N // U) + w, 2))
                    if k % HU:
                        return
                    j = k // HU
                    tiles = 1 if blocks == 1 else KT
                    for c in range(tiles):
                        for u in range(HU):
                            last = pe.matmul(psum[u * MV:(u + 1) * MV, OOFS + w % 2, 0:QW],
                                             vh[m][u][:, j * tiles + c, :], pt[w % 2][u][:, j, c * P:c * P + QW],
                                             start=j == 0 and c == 0, stop=j == G - 1 and c == tiles - 1)
                    last.then_inc(summed.sem, 1)

                def one(i, more):
                    for n in range(N):
                        if n + SCORE < N or more:
                            score(i + (n + SCORE) // N, (n + SCORE) % N)
                        if n + TURN < N or more:
                            turn(i + (n + TURN) // N, (n + TURN) % N)
                        weigh(i, n)

                for n in range(SCORE):
                    score(0, n)
                for n in range(TURN):
                    turn(0, n)
                with pe.Fori(0, ROUNDS - 1) as i:
                    one(i, True)
                one(ROUNDS - 1, False)

            @block.scalar
            def _(act):
                act.sem_inc(moved.sem, moved.start)

                def exp(i, n):
                    j = n % G
                    act.wait_ge(shifted.sem, shifted.done(i * (N // G) + n // G))
                    bias_of = neg[:, n // G % 4, j:j + 1] if blocks == 1 else neg[:, n // G % 4, 0:1]
                    act.activation(pr[:, n % PLACES, :], pr[:, n % PLACES, :], ACT.Exp, bias=bias_of,
                                   scale=SCALE).then_inc(exped.sem, 1)

                def move(i, n):
                    j, w, u = n % G, n // U, n % U // G
                    act.wait_ge(turned.sem, turned.done(i * N + n))
                    act.wait_ge(summed.sem, summed.room(i * (N // U * G) + (w * G + (G - 1)), 2 * G))
                    res = psum[:, TOFS + n % 2, :]
                    if blocks == 1:
                        act.activation(pt[w % 2][u][:, :, j * P:(j + 1) * P], res.rearrange("p (c q) -> p c q", q=P),
                                       ACT.Copy).then_inc(moved.sem, 1)
                    else:
                        act.activation(pt[w % 2][u][:, j, :], res, ACT.Copy).then_inc(moved.sem, 1)

                def one(i, more):
                    for n in range(N):
                        if n + TURN < N or more:
                            move(i + (n + TURN) // N, (n + TURN) % N)
                        if n + EXP < N or more:
                            exp(i + (n + EXP) // N, (n + EXP) % N)

                for n in range(EXP):
                    exp(0, n)
                for n in range(TURN):
                    move(0, n)
                with act.Fori(0, ROUNDS - 1) as i:
                    one(i, True)
                one(ROUNDS - 1, False)

            @block.gpsimd
            def _(pool):
                for m in range(SETS):
                    pool.sem_inc(stored[m].sem, stored[m].start)
                    for u in range(HU):
                        pool.memset(vh[m][u][:, :, HD0:], 1.0).then_inc(ones_set.sem, 1)
                pool.wait_ge(ones_set.sem, ones_set.done(HEADS - 1))
                pool.wait_ge(fixed_in.sem, fixed_in.done(B))
                with pool.Fori(0, ROUNDS) as i:
                    for m in range(SETS):
                        pool.wait_ge(summed.sem, summed.room(i * (N // U * G) + ((m + 1) * WS * G - 1), N // U * G))
                        pool.sem_inc(passed, 1)
                        for u in range(HU):
                            pool.tensor_copy(vh[m][u][:, :, 0:HD0], v[:, :, :, :].rearrange("p t b n -> p t (b n)")[
                                :, :, bass.ds(i * (HEADS * HV) + (m * HU + u) * HV, HD0)]).then_inc(v_here[m].sem, 1)

            @block.vector
            def _(dve):
                dve.sem_inc(masked.sem, masked.start)
                dve.sem_inc(taken.sem, taken.start)
                dve.wait_ge(fixed_in.sem, fixed_in.done(B))

                def mask(i, n):
                    _, _, qt, kb = place(n)
                    dve.wait_ge(scored.sem, scored.done(i * N + n))
                    dve.wait_ge(turned.sem, turned.room(i * N + n, PLACES))
                    dve.sem_inc(passed, 1)
                    dve.tensor_tensor_reduce(
                        pr[:, n % PLACES, :], psum[:, n % 4, :], bias[:, qt, kb * KEYS:(kb + 1) * KEYS], 1.0,
                        -3.0e38, ALU.add, ALU.max, mx[:, n // G % 4, n % G:n % G + 1]).then_inc(masked.sem, 1)
                    if n % G == G - 1:
                        g, p = i * (N // G) + n // G, n // G % 4
                        dve.wait_ge(masked.sem, masked.done(i * N + n))
                        if blocks == 1:
                            dve.tensor_scalar(neg[:, p, :], mx[:, p, :], -SCALE, None, ALU.mult).then_inc(shifted.sem, 1)
                        else:
                            dve.tensor_reduce(gmx[:, p:p + 1], mx[:, p, :], AX.X, ALU.max).then_inc(group_max.sem, 1)
                            dve.wait_ge(group_max.sem, group_max.done(g))
                            dve.tensor_scalar(neg[:, p, 0:1], gmx[:, p:p + 1], -SCALE, None, ALU.mult).then_inc(shifted.sem, 1)

                def take(i, n):
                    w, m = n // U, n // NS
                    if w % WS == 0:
                        dve.wait_ge(stored[m].sem, stored[m].room(i, 1))
                    dve.wait_ge(summed.sem, summed.done(i * (N // U * G) + (w * G + (G - 1))))
                    dve.tensor_copy(ao[m][:, w % WS * QW:(w % WS + 1) * QW], psum[0:HU * MV, OOFS + w % 2, 0:QW]).then_inc(
                        taken.sem, 1)

                def one(i, more):
                    for n in range(N):
                        if n + SCORE < N or more:
                            mask(i + (n + SCORE) // N, (n + SCORE) % N)
                        if n % U == U - 1:
                            take(i, n)

                for n in range(SCORE):
                    mask(0, n)
                with dve.Fori(0, ROUNDS - 1) as i:
                    one(i, True)
                one(ROUNDS - 1, False)




def invert_sums(nc, sums_dram, inverse_dram):
    with ExitStack() as ctx:
        st = Stage(nc, ctx, "invert")
        rows = st.sb("sums", [P, B * H0 * S // P])
        moved, inverted = st.count("moved", 16), st.count("inverted")

        def flat(m):
            return m.rearrange("h (c q) -> (h c) q", q=B * H0 * S // P)

        with nc.Block() as block:

            @block.sync
            def _(sp):
                sp.dma_start(rows[:, :], flat(sums_dram)).then_inc(moved.sem, 16)
                sp.wait_ge(inverted.sem, inverted.done(0))
                sp.dma_start(flat(inverse_dram), rows[:, :]).then_inc(moved.sem, 16)
                sp.wait_ge(moved.sem, moved.done(1))

            @block.vector
            def _(dve):
                dve.wait_ge(moved.sem, moved.done(0))
                dve.reciprocal(rows[:, :], rows[:, :]).then_inc(inverted.sem, 1)


def join(nc, psum, consts, att_dram, inverse_dram, x, out, weight, bias, gain, shift):
    ident, half = consts
    T = 4
    CH = T * P
    ROUNDS = TOK // CH
    HT = P // HD0
    with ExitStack() as ctx:
        st = Stage(nc, ctx, "join")
        w = st.halves("w", [P, KC, D])
        split_weights(nc, "join_w", [(rows_of(weight)[:, j:j + 2, :], w[0][:, j:j + 2, :], w[1][:, j:j + 2, :])
                                     for j in range(0, KC, 2)])
        raw, inv = st.sb("att", [P, KC, CH]), st.sb("inverse", [P, KC, CH])
        quo = st.sb("quotient", [P, KC, CH])
        at = [st.halves(f"att_t{s}", [P, KC, CH]) for s in range(2)]
        tail = Tail(st, 2 * T, x, out, bias, gain, shift, half)
        banks = st.banks(psum, [f"y{u}{t}" for u in range(2) for t in range(T)])
        a_in = st.count("att_in", 16 * (1 + HT))
        divided = st.count("divided", ahead=KC)
        at_hi = st.count("att_t_hi", ahead=KC)
        split = st.count("att_t_split", ahead=1)
        with nc.Block() as block:

            @block.sync
            def _(sp):
                RB = ROUNDS // B

                def load(r):
                    sp.wait_ge(divided.sem, divided.room(r * KC + (KC - 1), KC))
                    cols = bass.ds(r % RB * CH, CH)
                    sp.dma_start(raw[:, :, :], att_dram.rearrange("(c p) q -> p c q", p=P)[
                        :, bass.ds(r // RB * KC, KC), cols]).then_inc(a_in.sem, 16)
                    for h in range(HT):
                        sp.dma_start(inv[h * HD0:(h + 1) * HD0, :, :], inverse_dram.rearrange(
                            "(c h) q -> h c q", h=HT)[h, bass.ds(r // RB * KC, KC), cols].partition_broadcast(
                                HD0)).then_inc(a_in.sem, 16)

                tail.run_sync(sp, ROUNDS // 2, load, parts=2)

            @block.tensor
            def _(pe):
                pe.sem_inc(banks.ready, len(banks.names))
                for sem in banks.read:
                    pe.sem_inc(sem, 1)
                with pe.Fori(0, ROUNDS // 2) as k:
                    for u in range(2):
                        for t in range(T):
                            pe.wait_ge(banks.read_of(f"y{u}{t}"), banks.free(k, f"y{u}{t}"))
                            for c in range(KC):
                                if t == 0:
                                    pe.wait_ge(split.sem, split.done(k * 2 * KC + (u * KC + c)))
                                last = product(pe, banks.bank(f"y{u}{t}"),
                                               [h[:, c, t * P:(t + 1) * P] for h in at[u]],
                                               [h[:, c, :] for h in w], c == 0, c == KC - 1)
                            last.then_inc(banks.ready, 1)

            @block.scalar
            def _(act):
                act.sem_inc(at_hi.sem, at_hi.start)
                with act.Fori(0, ROUNDS // 2) as k:
                    for u in range(2):
                        act.wait_ge(banks.ready, banks.made_before(k, f"y{u}{T - 1}"))
                        for c in range(KC):
                            act.wait_ge(divided.sem, divided.done(k * 2 * KC + (u * KC + c)))
                            act.activation(at[u][0][:, c, :], quo[:, c, :], ACT.Copy).then_inc(at_hi.sem, 1)

            @block.vector
            def _(dve):
                tail.start_dve(dve)
                dve.sem_inc(divided.sem, divided.start)
                dve.sem_inc(split.sem, split.start)

                def ready(k, u):
                    dve.wait_ge(a_in.sem, a_in.done(k * 2 + u))
                    for c in range(KC):
                        n = k * 2 * KC + (u * KC + c)
                        dve.wait_ge(at_hi.sem, at_hi.room(n, KC))
                        if c == 0:
                            dve.wait_ge(split.sem, split.done(n - 1))
                        dve.tensor_tensor(quo[:, c, :], raw[:, c, :], inv[:, c, :], ALU.mult).then_inc(divided.sem, 1)
                    for c in range(KC):
                        n = k * 2 * KC + (u * KC + c)
                        dve.wait_ge(at_hi.sem, at_hi.done(n))
                        dve.tensor_tensor(at[u][1][:, c, :], quo[:, c, :], at[u][0][:, c, :].bitcast(F32),
                                          ALU.subtract).then_inc(split.sem, 1)

                def tails(k, u):
                    for t in range(T):
                        tail.dve_sum(dve, k, u * T + t, banks, f"y{u}{t}")
                        if t > 0:
                            tail.dve_norm(dve, k, u * T + t - 1)
                    tail.dve_norm(dve, k, u * T + T - 1)

                ready(0, 0)
                with dve.Fori(0, ROUNDS // 2 - 1) as k:
                    ready(k, 1)
                    tails(k, 0)
                    ready(k + 1, 0)
                    tails(k, 1)
                ready(ROUNDS // 2 - 1, 1)
                tails(ROUNDS // 2 - 1, 0)
                tails(ROUNDS // 2 - 1, 1)

            @block.gpsimd
            def _(pool):
                tail.start_pool(pool)
                with pool.Fori(0, ROUNDS // 2) as k:
                    for t in range(2 * T):
                        tail.pool_bias(pool, k, t)
                        if t > 0:
                            tail.pool_finish(pool, k, t - 1)
                        tail.pool_rstd(pool, k, t)
                    tail.pool_finish(pool, k, 2 * T - 1)




def cross(nc, psum, consts, name, heads, hd, x, context, ctx_mask, wq, bq, wk, bk, wv, bv, wo, bo, gain, shift,
          out):
    ident, half = consts
    T = 2
    CH = T * P
    ROUNDS = TOK // CH
    BR = ROUNDS // B
    W = heads * hd
    NG = W // P
    HG = P // hd
    SB, HB = 4, heads // 4
    HV = hd + 1
    OB = 2 if HV * 8 <= BANK else 4
    HO = heads // OB
    AB = W // BANK
    SCALE = float(hd) ** -0.5
    masked = ctx_mask is not None
    with ExitStack() as ctx:
        st = Stage(nc, ctx, name)
        w1, w2 = st.halves("wq", [P, KC, W]), st.halves("wo", [P, NG, D])
        bqc = st.sb("bq", [P, NG])
        kd = st.halves("k", [P, B * NG, HG * CTX])
        vc = st.sb("v", [CTX, B * heads, HV])
        mrow = st.sb("mask_row", [P, B, CTX])
        cross_context(nc, psum, ident, name, heads, hd, context, ctx_mask, wk, bk, wv, bv, kd, vc, mrow)
        split_weights(nc, f"{name}_w", [
            *((rows_of(wq)[:, j:j + 1, :], w1[0][:, j:j + 1, :], w1[1][:, j:j + 1, :])
              for j in range(KC))])
        split_weights(nc, f"{name}_u", [
            *((rows_of(wo)[:, j:j + 2, :], w2[0][:, j:j + 2, :], w2[1][:, j:j + 2, :])
              for j in range(0, NG, 2))])

        xn = st.sb("x", [P, T, D])
        xt = st.halves("xt", [P, KC, CH])
        qt = st.halves("q", [P, NG, CH])
        sc = [st.sb(f"scores{t}", [P, heads, CTX]) for t in range(T)]
        mx = [st.sb(f"max{t}", [P, heads]) for t in range(T)]
        pt = [st.sb(f"weights_t{t}", [CTX, heads, P]) for t in range(T)]
        rs = [st.sb(f"inverse{t}", [P, heads]) for t in range(T)]
        ao = [st.sb(f"att{t}", [P, W]) for t in range(T)]
        at = [st.halves(f"att_t{t}", [P, NG, P]) for t in range(T)]
        tail = Tail(st, T, x, out, bo, gain, shift, half)

        names = [f"x{t}" for t in range(T)] + [f"q{o}" for o in range(NG)]
        names += [f"s{t}{g}" for t in range(T) for g in range(SB)]
        names += [f"p{t}{g}" for t in range(T) for g in range(4)]
        names += [f"o{t}{g}" for t in range(T) for g in range(OB)]
        names += [f"a{t}{g}" for t in range(T) for g in range(AB)] + [f"y{t}" for t in range(T)]
        banks = st.banks(psum, names)
        fixed_in = st.count("bq_in", 16)
        x_in = st.count("x_in", 16)
        xt_hi, q_hi, at_hi = st.count("xt_hi"), st.count("q_hi"), st.count("att_t_hi")
        maxed, shifted, exped = (st.count(n) for n in ("scores_max", "scores_shifted", "exp_done"))
        inverted = st.count("inverted")

        def rounds(eng, one):
            with eng.Fori(0, ROUNDS) as r:
                one(r, r // BR)

        with nc.Block() as block:

            @block.sync
            def _(sp):
                sp.dma_start(bqc[:, :], bq.rearrange("(c p) -> p c", p=P), allow_slow_non_contiguous=True).then_inc(fixed_in.sem, 16)

                def load(r):
                    sp.wait_ge(banks.ready, banks.made_before(r, f"x{T - 1}"))
                    sp.dma_start(xn[:, :, :], tokens_of(x, r * CH, T)).then_inc(x_in.sem, 16)

                tail.run_sync(sp, ROUNDS, load)

            @block.tensor
            def _(pe):
                pe.sem_inc(banks.ready, len(banks.names))
                for sem in banks.read:
                    pe.sem_inc(sem, 1)

                def one(r, b):
                    pe.wait_ge(x_in.sem, x_in.done(r))
                    for t in range(T):
                        pe.wait_ge(banks.read_of(f"x{t}"), banks.free(r, f"x{t}"))
                        for c in range(KC):
                            last = pe.transpose(banks.bank(f"x{t}")[:, c * P:(c + 1) * P],
                                                xn[:, t, c * P:(c + 1) * P], ident[:, :])
                        last.then_inc(banks.ready, 1)
                    for t in range(T):
                        pe.wait_ge(banks.read_of(f"x{t}"), banks.drained(r, f"x{t}"))
                    for o in range(NG):
                        pe.wait_ge(banks.read_of(f"q{o}"), banks.free(r, f"q{o}"))
                        for c in range(KC):
                            last = product(pe, banks.bank(f"q{o}")[:, 0:CH], [h[:, c, o * P:(o + 1) * P] for h in w1],
                                           [h[:, c, :] for h in xt], c == 0, c == KC - 1)
                        last.then_inc(banks.ready, 1)
                    GB = NG // SB
                    for t in range(T):
                        for g in range(SB):
                            pe.wait_ge(banks.read_of(f"s{t}{g}"), banks.free(r, f"s{t}{g}"))
                            for m in range(GB):
                                o = g * GB + m
                                if t == 0:
                                    pe.wait_ge(banks.read_of(f"q{o}"), banks.drained(r, f"q{o}"))
                                last = product(pe, banks.bank(f"s{t}{g}")[:, m * HG * CTX:(m + 1) * HG * CTX],
                                               [h[:, o, t * P:(t + 1) * P] for h in qt],
                                               [h[:, bass.ds(b * NG + o, 1), :].rearrange("p o n -> p (o n)")
                                                for h in kd], True, True)
                            last.then_inc(banks.ready, 1)
                    for t in range(T):
                        for g in range(4):
                            pe.wait_ge(banks.read_of(f"p{t}{g}"), banks.free(r, f"p{t}{g}"))
                            pe.wait_ge(exped.sem, exped.done(r * (T * SB) + (t * SB + g)))
                            for h in range(4):
                                last = pe.transpose(banks.bank(f"p{t}{g}")[0:CTX, h * P:(h + 1) * P],
                                                    sc[t][:, g * 4 + h, :], ident[:, :])
                            last.then_inc(banks.ready, 1)
                    for t in range(T):
                        for g in range(OB):
                            pe.wait_ge(banks.read_of(f"o{t}{g}"), banks.free(r, f"o{t}{g}"))
                            for q in range(4):
                                if q * 4 < (g + 1) * HO and g * HO < (q + 1) * 4:
                                    pe.wait_ge(banks.read_of(f"p{t}{q}"), banks.drained(r, f"p{t}{q}"))
                            for h in range(HO):
                                last = pe.matmul(banks.bank(f"o{t}{g}")[:, h * HV:(h + 1) * HV],
                                                 pt[t][:, g * HO + h, :],
                                                 vc[:, bass.ds(b * heads + (g * HO + h), 1), :].rearrange(
                                                     "p o n -> p (o n)"), start=True, stop=True)
                            last.then_inc(banks.ready, 1)
                    for t in range(T):
                        for g in range(AB):
                            pe.wait_ge(banks.read_of(f"a{t}{g}"), banks.free(r, f"a{t}{g}"))
                            for q in range(g * (OB // AB), (g + 1) * (OB // AB)):
                                pe.wait_ge(banks.read_of(f"o{t}{q}"), banks.drained(r, f"o{t}{q}"))
                            for c in range(4):
                                o = g * 4 + c
                                last = pe.transpose(banks.bank(f"a{t}{g}")[:, c * P:(c + 1) * P],
                                                    ao[t][:, o * P:(o + 1) * P], ident[:, :])
                            last.then_inc(banks.ready, 1)
                    for t in range(T):
                        pe.wait_ge(banks.read_of(f"y{t}"), banks.free(r, f"y{t}"))
                        for g in range(AB):
                            pe.wait_ge(banks.read_of(f"a{t}{g}"), banks.drained(r, f"a{t}{g}"))
                            for c in range(4 * g, 4 * g + 4):
                                last = product(pe, banks.bank(f"y{t}"), [h[:, c, :] for h in at[t]],
                                               [h[:, c, :] for h in w2], c == 0, c == NG - 1)
                        last.then_inc(banks.ready, 1)

                rounds(pe, one)

            @block.scalar
            def _(act):
                act.wait_ge(fixed_in.sem, fixed_in.done(0))

                def one(r, b):
                    for t in range(T):
                        act.wait_ge(banks.ready, banks.made(r, f"x{t}"))
                        act.activation(xt[0][:, :, t * P:(t + 1) * P],
                                                banks.bank(f"x{t}").rearrange("p (c q) -> p c q", q=P), ACT.Copy).then_inc(xt_hi.sem, 1)
                    for o in range(NG):
                        act.wait_ge(banks.ready, banks.made(r, f"q{o}"))
                        act.activation(qt[0][:, o, :], banks.bank(f"q{o}")[:, 0:CH], ACT.Identity,
                                               bias=bqc[:, o:o + 1]).then_inc(q_hi.sem, 1)
                    for t in range(T):
                        for g in range(SB):
                            part = sc[t][:, g * HB:(g + 1) * HB, :].rearrange("p h k -> p (h k)")
                            if masked:
                                act.wait_ge(shifted.sem, shifted.done(r * (T * SB) + (t * SB + g)))
                            else:
                                act.wait_ge(banks.read_of(f"s{t}{g}"), banks.drained(r, f"s{t}{g}"))
                            act.activation(part, part, ACT.Exp, scale=SCALE).then_inc(exped.sem, 1)
                    for t in range(T):
                        for g in range(4):
                            act.wait_ge(banks.ready, banks.made(r, f"p{t}{g}"))
                            act.activation(
                                pt[t][:, 4 * g:4 * g + 4, :].rearrange("p h q -> p (h q)"),
                                banks.bank(f"p{t}{g}")[0:CTX, :], ACT.Copy).then_inc(banks.read_of(f"p{t}{g}"), 1)
                    for t in range(T):
                        for g in range(AB):
                            act.wait_ge(banks.ready, banks.made(r, f"a{t}{g}"))
                            act.activation(
                                at[t][0][:, 4 * g:4 * g + 4, :].rearrange("p c q -> p (c q)"),
                                banks.bank(f"a{t}{g}"), ACT.Copy).then_inc(at_hi.sem, 1)

                rounds(act, one)

            @block.vector
            def _(dve):
                tail.start_dve(dve)

                def one(r, b):
                    for t in range(T):
                        dve.wait_ge(xt_hi.sem, xt_hi.done(r * T + t))
                        dve.tensor_tensor(
                            xt[1][:, :, t * P:(t + 1) * P], banks.bank(f"x{t}").rearrange("p (c q) -> p c q", q=P),
                            xt[0][:, :, t * P:(t + 1) * P].bitcast(F32), ALU.subtract).then_inc(banks.read_of(f"x{t}"), 1)
                    for o in range(NG):
                        dve.wait_ge(q_hi.sem, q_hi.done(r * NG + o))
                        dve.scalar_tensor_tensor(
                            qt[1][:, o, :], banks.bank(f"q{o}")[:, 0:CH], bqc[:, o:o + 1],
                            qt[0][:, o, :].bitcast(F32), ALU.add, ALU.subtract).then_inc(banks.read_of(f"q{o}"), 1)
                    for t in range(T):
                        for g in range(SB):
                            n = r * (T * SB) + (t * SB + g)
                            res = banks.bank(f"s{t}{g}")[:, 0:HB * CTX].rearrange("p (h k) -> p h k", k=CTX)
                            part = sc[t][:, g * HB:(g + 1) * HB, :]
                            top = mx[t][:, g * HB:(g + 1) * HB]
                            dve.wait_ge(banks.ready, banks.made(r, f"s{t}{g}"))
                            if masked:
                                dve.tensor_tensor(
                                    part, res, mrow[:, bass.ds(b, 1), :].to_broadcast([P, HB, CTX]), ALU.add).then_inc(banks.read_of(f"s{t}{g}"), 1)
                                dve.wait_ge(banks.read_of(f"s{t}{g}"), banks.drained(r, f"s{t}{g}"))
                                dve.tensor_reduce(top, part, AX.X, ALU.max).then_inc(maxed.sem, 1)
                                dve.wait_ge(maxed.sem, maxed.done(n))
                                dve.tensor_tensor(part, part, top.unsqueeze(2).to_broadcast(
                                    [P, HB, CTX]), ALU.subtract).then_inc(shifted.sem, 1)
                            else:
                                dve.tensor_reduce(top, res, AX.X, ALU.max).then_inc(maxed.sem, 1)
                                dve.wait_ge(maxed.sem, maxed.done(n))
                                dve.tensor_tensor(part, res, top.unsqueeze(2).to_broadcast(
                                    [P, HB, CTX]), ALU.subtract).then_inc(banks.read_of(f"s{t}{g}"), 1)
                    for t in range(T):
                        for g in range(OB):
                            n = r * (T * OB) + (t * OB + g)
                            res = banks.bank(f"o{t}{g}")[:, 0:HO * HV].rearrange("p (h d) -> p h d", d=HV)
                            inv = rs[t][:, g * HO:(g + 1) * HO]
                            dve.wait_ge(banks.ready, banks.made(r, f"o{t}{g}"))
                            dve.reciprocal(inv, res[:, :, hd:].rearrange("p h d -> p (h d)")).then_inc(inverted.sem, 1)
                            dve.wait_ge(inverted.sem, inverted.done(n))
                            dve.tensor_tensor(
                                ao[t][:, g * HO * hd:(g + 1) * HO * hd].rearrange("p (h d) -> p h d", d=hd),
                                res[:, :, 0:hd], inv.unsqueeze(2).to_broadcast([P, HO, hd]), ALU.mult).then_inc(banks.read_of(f"o{t}{g}"), 1)
                    for t in range(T):
                        for g in range(AB):
                            dve.wait_ge(at_hi.sem, at_hi.done(r * (T * AB) + (t * AB + g)))
                            dve.tensor_tensor(
                                at[t][1][:, 4 * g:4 * g + 4, :].rearrange("p c q -> p (c q)"),
                                banks.bank(f"a{t}{g}"),
                                at[t][0][:, 4 * g:4 * g + 4, :].rearrange("p c q -> p (c q)").bitcast(F32),
                                ALU.subtract).then_inc(banks.read_of(f"a{t}{g}"), 1)
                    for t in range(T):
                        tail.dve_sum(dve, r, t, banks, f"y{t}")
                    for t in range(T):
                        tail.dve_norm(dve, r, t)

                rounds(dve, one)

            @block.gpsimd
            def _(pool):
                tail.start_pool(pool)

                def one(r, b):
                    for t in range(T):
                        tail.pool_bias(pool, r, t)
                    for t in range(T):
                        tail.pool_rstd(pool, r, t)
                    for t in range(T):
                        tail.pool_finish(pool, r, t)

                rounds(pool, one)


def cross_context(nc, psum, ident, name, heads, hd, context, ctx_mask, wk, bk, wv, bv, kd, vc, mrow):
    W = heads * hd
    NG, HG = W // P, P // hd
    VB = W // BANK
    with ExitStack() as ctx:
        st = Stage(nc, ctx, f"{name}_context")
        wks, wvs = st.sb("wk", [P, KC, W]), st.sb("wv", [P, KC, W])
        bkc, bvr = st.sb("bk", [P, NG]), st.sb("bv", [CTX, W])
        cn = st.sb("c", [CTX, B, D])
        ct = st.sb("ct", [P, KC, B, CTX])
        mi = st.sb("mask", [P, B, CTX], I32)
        loaded, zeroed = st.sem("loaded"), st.sem("zeroed")
        made, read, hi_done, built = st.sem("made"), st.sem("read"), st.sem("hi_done"), st.sem("built")
        loads = [(wks[:, :, :], rows_of(wk)), (wvs[:, :, :], rows_of(wv)),
                 (bkc[:, :], bk.rearrange("(c p) -> p c", p=P)), (bvr[:, :], bv.partition_broadcast(CTX)),
                 (cn[:, :, :], context.rearrange("b s d -> s b d"))]
        if ctx_mask is not None:
            loads.append((mi[:, :, :], ctx_mask.partition_broadcast(P)))
        with nc.Block() as block:

            @block.sync
            def _(sp):
                for dst, src in loads:
                    sp.dma_start(dst, src, allow_slow_non_contiguous=True).then_inc(loaded, 16)

            @block.gpsimd
            def _(pool):
                for h in kd:
                    pool.memset(h[:, :, :].bitcast(F32), 0.0).then_inc(zeroed, 1)
                pool.memset(vc[:, :, hd:], 1.0).then_inc(zeroed, 1)
                pool.wait_ge(zeroed, 3)

            @block.tensor
            def _(pe):
                pe.wait_ge(loaded, 16 * len(loads))
                for b in range(B):
                    for c in range(KC):
                        last = pe.transpose(psum[:, b, c * CTX:(c + 1) * CTX], cn[:, b, c * P:(c + 1) * P],
                                            ident[0:CTX, 0:CTX])
                    last.then_inc(made, 1)
                pe.wait_ge(read, B)
                for o in range(NG):
                    if o >= 2:
                        pe.wait_ge(built, (o - 1) * B * HG)
                    for c in range(KC):
                        last = pe.matmul(psum[:, 2 + o % 2, 0:B * CTX], wks[:, c, o * P:(o + 1) * P],
                                         ct[:, c, :, :].rearrange("p b s -> p (b s)"), start=c == 0,
                                         stop=c == KC - 1)
                    last.then_inc(made, 1)
                for b in range(B):
                    for g in range(VB):
                        for c in range(KC):
                            last = pe.matmul(psum[0:CTX, 4 + b * VB + g, :], ct[:, c, b, :],
                                             wvs[:, c, g * BANK:(g + 1) * BANK], start=c == 0, stop=c == KC - 1)
                        last.then_inc(made, 1)

            @block.scalar
            def _(act):
                act.wait_ge(zeroed, 3)
                act.wait_ge(loaded, 16 * len(loads))
                for o in range(NG):
                    act.wait_ge(made, B + o + 1)
                    for b in range(B):
                        for h in range(HG):
                            rows = slice(h * hd, (h + 1) * hd)
                            act.activation(kd[0][rows, b * NG + o, h * CTX:(h + 1) * CTX],
                                           psum[rows, 2 + o % 2, b * CTX:(b + 1) * CTX], ACT.Identity,
                                           bias=bkc[rows, o:o + 1]).then_inc(hi_done, 1)

            @block.vector
            def _(dve):
                dve.wait_ge(zeroed, 3)
                dve.wait_ge(loaded, 16 * len(loads))
                for b in range(B):
                    dve.wait_ge(made, b + 1)
                    dve.tensor_copy(ct[:, :, b, :], psum[:, b, 0:KC * CTX].rearrange(
                        "p (c s) -> p c s", s=CTX)).then_inc(read, 1)
                n = 0
                for o in range(NG):
                    dve.wait_ge(hi_done, (o + 1) * B * HG)
                    for b in range(B):
                        for h in range(HG):
                            rows = slice(h * hd, (h + 1) * hd)
                            n += 1
                            dst = kd[1][rows, b * NG + o, h * CTX:(h + 1) * CTX]
                            dve.scalar_tensor_tensor(
                                dst, psum[rows, 2 + o % 2, b * CTX:(b + 1) * CTX], bkc[rows, o:o + 1],
                                kd[0][rows, b * NG + o, h * CTX:(h + 1) * CTX].bitcast(F32),
                                ALU.add, ALU.subtract).then_inc(built, 1)
                k = B
                for b in range(B):
                    for g in range(VB):
                        dve.wait_ge(made, B + NG + b * VB + g + 1)
                        hb = BANK // hd
                        dve.tensor_tensor(
                            vc[:, b * heads + g * hb:b * heads + (g + 1) * hb, 0:hd],
                            psum[0:CTX, 4 + b * VB + g, :].rearrange("p (h d) -> p h d", d=hd),
                            bvr[:, g * BANK:(g + 1) * BANK].rearrange("p (h d) -> p h d", d=hd),
                            ALU.add).then_inc(read, 1)
                        k += 1
                if ctx_mask is not None:
                    dve.tensor_scalar(mrow[:, :, :], mi[:, :, :], 0.0, -BIG, ALU.is_equal, ALU.mult).then_inc(read, 1)
                    k += 1
                dve.wait_ge(read, k)
                dve.wait_ge(built, n)




def feed(nc, psum, consts, x, w1, b1, w2, b2, gain, shift, out):
    ident, half = consts
    T = 2
    CH = T * P
    ROUNDS = TOK // CH
    NF = FF // P
    NR = 4
    with ExitStack() as ctx:
        st = Stage(nc, ctx, "feed")
        wa, wb = st.halves("w1", [P, KC, FF]), st.halves("w2", [P, NF, D])
        split_weights(nc, "feed_w1", [(rows_of(w1)[:, j:j + 1, :], wa[0][:, j:j + 1, :], wa[1][:, j:j + 1, :])
                                      for j in range(KC)])
        split_weights(nc, "feed_w2", [(rows_of(w2)[:, j:j + 4, :], wb[0][:, j:j + 4, :], wb[1][:, j:j + 4, :])
                                      for j in range(0, NF, 4)])
        b1c = st.sb("b1", [P, NF])
        xn = st.sb("x", [P, T, D])
        xt = st.halves("xt", [P, KC, CH])
        hf = st.sb("hidden", [P, NR, CH])
        ht = st.halves("ht", [P, NF, CH])
        tail = Tail(st, T, x, out, b2, gain, shift, half)
        banks = st.banks(psum, [f"x{t}" for t in range(T)] + [f"h{o}" for o in range(NF)]
                         + [f"y{t}" for t in range(T)])
        b1_in, x_in, xt_hi = st.count("b1_in", 16), st.count("x_in", 16), st.count("xt_hi")
        h_hi, h_split = st.count("hidden_hi"), st.count("hidden_split", ahead=NR)
        with nc.Block() as block:

            @block.sync
            def _(sp):
                sp.dma_start(b1c[:, :], b1.rearrange("(c p) -> p c", p=P), allow_slow_non_contiguous=True).then_inc(b1_in.sem, 16)

                def load(r):
                    sp.wait_ge(banks.ready, banks.made_before(r, f"x{T - 1}"))
                    sp.dma_start(xn[:, :, :], tokens_of(x, r * CH, T)).then_inc(x_in.sem, 16)

                tail.run_sync(sp, ROUNDS, load)

            @block.tensor
            def _(pe):
                pe.sem_inc(banks.ready, len(banks.names))
                for sem in banks.read:
                    pe.sem_inc(sem, 1)
                with pe.Fori(0, ROUNDS) as r:
                    pe.wait_ge(x_in.sem, x_in.done(r))
                    for t in range(T):
                        pe.wait_ge(banks.read_of(f"x{t}"), banks.free(r, f"x{t}"))
                        for c in range(KC):
                            last = pe.transpose(banks.bank(f"x{t}")[:, c * P:(c + 1) * P],
                                                xn[:, t, c * P:(c + 1) * P], ident[:, :])
                        last.then_inc(banks.ready, 1)
                    for t in range(T):
                        pe.wait_ge(banks.read_of(f"x{t}"), banks.drained(r, f"x{t}"))
                    for o in range(NF):
                        pe.wait_ge(banks.read_of(f"h{o}"), banks.free(r, f"h{o}"))
                        for c in range(KC):
                            last = product(pe, banks.bank(f"h{o}")[:, 0:CH], [h[:, c, o * P:(o + 1) * P] for h in wa],
                                           [h[:, c, :] for h in xt], c == 0, c == KC - 1)
                        last.then_inc(banks.ready, 1)
                    for t in range(T):
                        pe.wait_ge(banks.read_of(f"y{t}"), banks.free(r, f"y{t}"))
                        for o in range(NF):
                            if t == 0:
                                pe.wait_ge(h_split.sem, h_split.done(r * NF + o))
                            last = product(pe, banks.bank(f"y{t}"), [h[:, o, t * P:(t + 1) * P] for h in ht],
                                           [h[:, o, :] for h in wb], o == 0, o == NF - 1)
                        last.then_inc(banks.ready, 1)

            @block.scalar
            def _(act):
                act.wait_ge(b1_in.sem, b1_in.done(0))
                with act.Fori(0, ROUNDS) as r:
                    for t in range(T):
                        act.wait_ge(banks.ready, banks.made(r, f"x{t}"))
                        act.activation(xt[0][:, :, t * P:(t + 1) * P],
                                                banks.bank(f"x{t}").rearrange("p (c q) -> p c q", q=P), ACT.Copy).then_inc(xt_hi.sem, 1)
                    for o in range(NF):
                        act.wait_ge(banks.ready, banks.made(r, f"h{o}"))
                        act.wait_ge(h_split.sem, h_split.room(r * NF + o, NR))
                        act.activation(hf[:, o % NR, :], banks.bank(f"h{o}")[:, 0:CH], ACT.Relu,
                                                     bias=b1c[:, o:o + 1]).then_inc(banks.read_of(f"h{o}"), 1)

            @block.vector
            def _(dve):
                tail.start_dve(dve)
                dve.sem_inc(h_split.sem, h_split.start)
                with dve.Fori(0, ROUNDS) as r:
                    for t in range(T):
                        dve.wait_ge(xt_hi.sem, xt_hi.done(r * T + t))
                        dve.tensor_tensor(
                            xt[1][:, :, t * P:(t + 1) * P], banks.bank(f"x{t}").rearrange("p (c q) -> p c q", q=P),
                            xt[0][:, :, t * P:(t + 1) * P].bitcast(F32), ALU.subtract).then_inc(banks.read_of(f"x{t}"), 1)
                    dve.wait_ge(banks.ready, banks.made_before(r, f"y{T - 1}"))
                    for o in range(NF):
                        dve.wait_ge(banks.read_of(f"h{o}"), banks.drained(r, f"h{o}"))
                        dve.tensor_copy(ht[0][:, o, :], hf[:, o % NR, :]).then_inc(h_hi.sem, 1)
                        dve.wait_ge(h_hi.sem, h_hi.done(r * NF + o))
                        dve.tensor_tensor(ht[1][:, o, :], hf[:, o % NR, :], ht[0][:, o, :].bitcast(F32),
                                                     ALU.subtract).then_inc(h_split.sem, 1)
                    for t in range(T):
                        tail.dve_sum(dve, r, t, banks, f"y{t}")
                        tail.dve_norm(dve, r, t)

            @block.gpsimd
            def _(pool):
                tail.start_pool(pool)
                with pool.Fori(0, ROUNDS) as r:
                    for t in range(T):
                        tail.pool_bias(pool, r, t)
                        tail.pool_rstd(pool, r, t)
                        tail.pool_finish(pool, r, t)




def build(nc, a, out):
    def scratch(name, shape, dt=F32):
        return nc.dram_tensor(name, shape, dt, kind="Internal").ap()

    halves = [scratch(f"{n}_halves", (2, B * D, S)) for n in "qk"]
    v_dram = scratch("v_ones", (TOK, H0 * (HD0 + 1)))
    bias_dram = scratch("mask_bias", (S, S), BF16)
    att_dram, sums_dram, inverse_dram = (scratch(n, (B * k, S)) for n, k in (
        ("attention", D), ("weight_sums", H0), ("inverse_sums", H0)))
    x1, x2, x3 = (scratch(f"x_{n}", (TOK, D)) for n in ("joined", "crossed", "fed"))
    x = a["x"].rearrange("b s d -> (b s) d")
    layer = {k[9:]: v for k, v in a.items() if k.startswith("L0_xattn_")}
    second = {k[9:]: v for k, v in a.items() if k.startswith("L1_xattn_")}

    with ExitStack() as ctx:
        psum = ctx.enter_context(nc.psum_tensor("psum", [P, 8, BANK], F32))
        ident, half, ones = make_constants(nc, ctx)
        consts = (ident, half)
        with ExitStack() as inner:
            st = Stage(nc, inner, "window")
            open_max = st.sb("open_max", [P, S // P, S // KEYS])
            choice = st.sb("choice", [1, 2], I32)
            project(nc, psum, ident, x, a["mask_SxS_ik1"], [layer[f"{n}_w"] for n in "qkv"],
                    [layer[f"{n}_b"] for n in "qkv"], halves, v_dram, bias_dram, open_max)
            choose_window(nc, psum, ones, open_max, choice)
            one_block = nc.values_load(choice[:, 0:1], min_val=0, max_val=1)
            block = nc.values_load(choice[:, 1:2], min_val=0, max_val=S // KEYS - 1)
            with nc.If(one_block):
                attend(nc, psum, ident, halves, v_dram, bias_dram, att_dram, sums_dram, 1, block)
            with nc.Else():
                attend(nc, psum, ident, halves, v_dram, bias_dram, att_dram, sums_dram,
                       S // KEYS, 0)
        invert_sums(nc, sums_dram, inverse_dram)
        join(nc, psum, consts, att_dram, inverse_dram, x, x1, layer["o_w"], layer["o_b"], layer["ln1_g"], layer["ln1_b"])
        cross(nc, psum, consts, "cross", H0, HD0, x1, a["ctx_1024"], None, layer["cq_w"], layer["cq_b"],
              layer["ck_w"], layer["ck_b"], layer["cv_w"], layer["cv_b"], layer["co_w"], layer["co_b"],
              layer["ln2_g"], layer["ln2_b"], x2)
        feed(nc, psum, consts, x2, layer["lin1_w"], layer["lin1_b"], layer["lin2_w"], layer["lin2_b"],
             layer["ln3_g"], layer["ln3_b"], x3)
        cross(nc, psum, consts, "second", H1, HD1, x3, a["ctx_1024"], a["mask_BxS2_ik0"], second["Wq"],
              second["bq"], second["Wk"], second["bk"], second["Wv"], second["bv"], second["Wo"], second["bo"],
              second["gamma"], second["beta"], out)


def kernel(**inputs):
    import numpy as np
    import concourse.bacc as bacc
    from concourse.bass_utils import run_bass_kernel_spmd

    nc = bacc.Bacc("TRN2", target_bir_lowering=False, num_devices=1)
    arrays = {f"in_{name}": np.ascontiguousarray(a) for name, a in inputs.items()}
    given = {name: nc.dram_tensor(f"in_{name}", arrays[f"in_{name}"].shape,
                                  mybir.dt.from_np(arrays[f"in_{name}"].dtype), kind="ExternalInput").ap()
             for name in inputs}
    out = nc.dram_tensor("out", (B, S, D), F32, kind="ExternalOutput").ap()
    build(nc, given, out.rearrange("b s d -> (b s) d"))
    result = run_bass_kernel_spmd(nc, [arrays], core_ids=[0])
    return result.results[0]["out"]
```

```python
from contextlib import ExitStack

import concourse.bass as bass
from concourse import mybir

F32 = mybir.dt.float32
F32R = mybir.dt.float32r
BF16 = mybir.dt.bfloat16
I32 = mybir.dt.int32
ALU = mybir.AluOpType
ACT = mybir.ActivationFunctionType
AX = mybir.AxisListType

P = 128
B, S, D = 2, 2048, 512
TOK = B * S
KC = D // P
H0, HD0 = 16, 32
H1, HD1 = 16, 64
CTX = 77
FF = 2048
EPS = 1e-5
BIG = 2.0 ** 126
BANK = 512
KEYS = 512


class Count:

    def __init__(self, sem, step=1, ahead=0):
        self.sem, self.step, self.ahead, self.start = sem, step, ahead, step * ahead

    def done(self, n):
        return n * self.step + self.step * (self.ahead + 1)

    def room(self, n, ring):
        assert ring <= self.ahead
        return n * self.step + self.step * (self.ahead + 1 - ring)


class Banks:

    def __init__(self, psum, ready, read, names):
        self.psum, self.ready, self.read, self.names = psum, ready, read, names
        self.at = {name: n for n, name in enumerate(names)}
        self.per_bank = [len(range(b, len(names), 8)) for b in range(8)]
        assert len(self.at) == len(names) >= 8

    def bank(self, name):
        return self.psum[:, self.at[name] % 8, :]

    def read_of(self, name):
        return self.read[self.at[name] % 8]

    def free(self, rnd, name):
        n = self.at[name]
        return rnd * self.per_bank[n % 8] + (n // 8 + 1)

    def drained(self, rnd, name):
        n = self.at[name]
        return rnd * self.per_bank[n % 8] + (n // 8 + 2)

    def made(self, rnd, name):
        return rnd * len(self.names) + (len(self.names) + self.at[name] + 1)

    def made_before(self, rnd, name):
        return rnd * len(self.names) + (self.at[name] + 1)


def skip(pe, banks, k, names):
    for name in names:
        pe.wait_ge(banks.ready, banks.made(k, name) - 1)
        pe.wait_ge(banks.read_of(name), banks.free(k, name))
        pe.sem_inc(banks.ready, 1)
        pe.sem_inc(banks.read_of(name), 1)


def product(pe, out, w, x, first, last):
    pe.matmul(out, w[1], x[0], start=first, stop=False)
    pe.matmul(out, w[0], x[1], start=False, stop=False)
    return pe.matmul(out, w[0], x[0], start=False, stop=last)


class Stage:

    def __init__(self, nc, ctx, name):
        self.nc, self.ctx, self.name, self.sems = nc, ctx, name, []
        ctx.push(self.clear)

    def clear(self, failed, *_):
        if failed:
            return
        with self.nc.Block() as block:

            @block.gpsimd
            def _(pool):
                self.nc.clear_and_free_semaphores(self.sems)

    def sb(self, name, shape, dt=F32):
        return self.ctx.enter_context(self.nc.sbuf_tensor(f"{self.name}_{name}", shape, dt))

    def halves(self, name, shape):
        return [self.sb(f"{name}_{h}", shape, F32R) for h in ("hi", "lo")]

    def sem(self, name):
        self.sems.append(self.nc.alloc_semaphore(f"{self.name}_{name}"))
        return self.sems[-1]

    def count(self, name, step=1, ahead=0):
        return Count(self.sem(name), step, ahead)

    def banks(self, psum, names):
        return Banks(psum, self.sem("ready"), [self.sem(f"read{b}") for b in range(8)], names)


def rows_of(m):
    return m.rearrange("(c p) n -> p c n", p=P)


def tokens_of(m, first, tiles):
    return m[bass.ds(first, tiles * P), :].rearrange("(t p) n -> p t n", p=P)


class Splitter:

    SLOTS = 6

    def __init__(self, st, jobs):
        self.jobs = jobs
        size = int(jobs[0][0].shape[1] * jobs[0][0].shape[2])
        self.raw = [st.sb(f"raw{s}", [P, size]) for s in range(self.SLOTS)]
        self.loaded = [st.count(f"raw{s}_loaded", 16) for s in range(self.SLOTS)]
        self.hi_done, self.split = st.count("raw_hi"), st.count("raw_split")

    def slot(self, n):
        return self.raw[n % self.SLOTS][:, :].rearrange("p (a b) -> p a b", b=self.jobs[n][0].shape[2])

    def sync(self, sp):
        for n, (src, _, _) in enumerate(self.jobs):
            if n >= self.SLOTS:
                sp.wait_ge(self.split.sem, self.split.done(n - self.SLOTS))
            sp.dma_start(self.slot(n), src).then_inc(self.loaded[n % self.SLOTS].sem, 16)

    def scalar(self, act):
        for n, (_, hi, _) in enumerate(self.jobs):
            loaded = self.loaded[n % self.SLOTS]
            act.wait_ge(loaded.sem, loaded.done(n // self.SLOTS))
            act.activation(hi, self.slot(n), ACT.Copy).then_inc(self.hi_done.sem, 1)

    def vector(self, dve):
        for n, (_, hi, lo) in enumerate(self.jobs):
            dve.wait_ge(self.hi_done.sem, self.hi_done.done(n))
            dve.tensor_tensor(lo, self.slot(n), hi.bitcast(F32), ALU.subtract).then_inc(self.split.sem, 1)
        dve.wait_ge(self.split.sem, self.split.done(len(self.jobs) - 1))


def split_weights(nc, name, jobs):
    with ExitStack() as ctx:
        splitter = Splitter(Stage(nc, ctx, name), jobs)
        with nc.Block() as block:

            @block.sync
            def _(sp):
                splitter.sync(sp)

            @block.scalar
            def _(act):
                splitter.scalar(act)

            @block.vector
            def _(dve):
                splitter.vector(dve)


def make_constants(nc, ctx):
    st = Stage(nc, ctx, "const")
    ident, half, ones = st.sb("ident", [P, P]), st.sb("minus_half", [P, 1]), st.sb("ones", [P, P])
    made = st.sem("made")
    with nc.Block() as block:

        @block.gpsimd
        def _(pool):
            pool.memset(ident[:, :], 0.0).then_inc(made, 1)
            pool.memset(half[:, :], -0.5).then_inc(made, 1)
            pool.memset(ones[:, :], 1.0).then_inc(made, 1)
            pool.wait_ge(made, 3)
            pool.affine_select(out=ident[:, :], in_=ident[:, :], compare_op=ALU.not_equal, fill=1.0,
                               base=0, pattern=[[-1, P]], channel_multiplier=1).then_inc(made, 1)
            pool.wait_ge(made, 4)

    return ident, half, ones


class Tail:

    def __init__(self, st, tiles, residual, out, bias, gain, shift, minus_half, depth=2, bias_in_product=False):
        assert tiles % depth == 0
        self.depth, self.bias_in_product = depth, bias_in_product
        self.tiles, self.residual, self.out, self.half = tiles, residual, out, minus_half
        self.rows_dram = (bias, gain, shift)
        self.rows = [st.sb(f"row_{n}", [P, D]) for n in ("bias", "gain", "shift")]
        self.res = [st.sb(f"residual{s}", [P, D]) for s in range(depth)]
        self.sum = [st.sb(f"sum{s}", [P, D]) for s in range(depth)]
        self.y = [st.sb(f"normed{s}", [P, D]) for s in range(depth)]
        self.stats = [st.sb(f"stats{s}", [P, 6]) for s in range(depth)]
        self.mean_var = [st.sb(f"mean_var{s}", [P, 2]) for s in range(depth)]
        self.var_eps = [st.sb(f"var_eps{s}", [P, 1]) for s in range(depth)]
        self.rstd = [st.sb(f"rstd{s}", [P, 1]) for s in range(depth)]
        self.rows_in = st.count("rows_in", 16)
        self.passed = st.sem("waits_passed")
        self.res_in = [st.count(f"residual_in{s}", 16) for s in range(depth)]
        self.biased = st.count("residual_biased")
        self.stats_done = st.count("stats_done")
        self.var_done = st.count("variance_done", ahead=depth)
        self.eps_added = st.count("eps_added")
        self.rstd_done = st.count("rstd_done")
        self.normed = st.count("normed")
        self.gained = st.count("gained", ahead=depth)
        self.finished = st.count("finished")
        self.stored = [st.count(f"stored{s}", 16, 1) for s in range(depth)]

    def tile(self, rnd, t):
        return rnd * self.tiles + t, rnd * (self.tiles // self.depth) + t // self.depth, t % self.depth

    def load_rows(self, sp):
        for row, src in zip(self.rows, self.rows_dram):
            sp.dma_start(row[:, :], src.partition_broadcast(P)).then_inc(self.rows_in.sem, 16)

    def load(self, sp, rnd, t):
        n, k, s = self.tile(rnd, t)
        sp.wait_ge(self.var_done.sem, self.var_done.room(n, self.depth))
        sp.dma_start(self.res[s][:, :], self.residual[bass.ds(n * P, P), :]).then_inc(self.res_in[s].sem, 16)

    def start_dve(self, dve):
        dve.sem_inc(self.var_done.sem, self.var_done.start)

    def store(self, sp, rnd, t):
        n, k, s = self.tile(rnd, t)
        sp.wait_ge(self.finished.sem, self.finished.done(n))
        sp.dma_start(self.out[bass.ds(n * P, P), :], self.y[s][:, :]).then_inc(self.stored[s].sem, 16)

    def run_sync(self, sp, rounds, load_x, parts=1, lead=0):
        def round_of(rnd, left):
            for t in range(self.tiles):
                if t % (self.tiles // parts) == 0:
                    p = t * parts // self.tiles + 1 + lead
                    if left is None or p < left * parts:
                        load_x(rnd * parts + p, p % parts)
                if left != 1 or t + self.depth < self.tiles:
                    self.load(sp, rnd, t + self.depth)
                self.store(sp, rnd, t)

        for c in self.stored:
            sp.sem_inc(c.sem, c.start)
        self.load_rows(sp)
        load_x(0, 0)
        for t in range(self.depth):
            self.load(sp, 0, t)
        for p in range(lead):
            load_x(p + 1, (p + 1) % parts)
        peeled = 1 + -(-lead // parts)
        with sp.Fori(0, rounds - peeled) as r:
            round_of(r, None)
        for left in range(peeled, 0, -1):
            round_of(rounds - left, left)
        for c in self.stored:
            sp.wait_ge(c.sem, c.done(rounds * (self.tiles // self.depth) - 1))

    def start_pool(self, pool):
        pool.sem_inc(self.gained.sem, self.gained.start)
        pool.wait_ge(self.rows_in.sem, self.rows_in.done(2))

    def pool_bias(self, pool, rnd, t):
        n, k, s = self.tile(rnd, t)
        pool.wait_ge(self.res_in[s].sem, self.res_in[s].done(k))
        pool.tensor_tensor(self.res[s][:, :], self.res[s][:, :], self.rows[0][:, :], ALU.add).then_inc(
            self.biased.sem, 1)

    def dve_sum(self, dve, rnd, t, banks, name, step=None):
        n, k, s = self.tile(rnd, t)
        step = rnd if step is None else step
        if self.bias_in_product:
            dve.wait_ge(self.res_in[s].sem, self.res_in[s].done(k))
        else:
            dve.wait_ge(self.biased.sem, self.biased.done(n))
        dve.wait_ge(self.gained.sem, self.gained.room(n, self.depth))
        dve.wait_ge(banks.ready, banks.made(step, name))
        dve.tensor_tensor(self.sum[s][:, :], banks.bank(name), self.res[s][:, :], ALU.add).then_inc(
            banks.read_of(name), 1)
        dve.wait_ge(banks.read_of(name), banks.drained(step, name))
        dve.bn_stats(self.stats[s][:, :], self.sum[s][:, :]).then_inc(self.stats_done.sem, 1)
        dve.wait_ge(self.stats_done.sem, self.stats_done.done(n))
        dve.sem_inc(self.passed, 1)
        dve.bn_aggr(self.mean_var[s][:, :], self.stats[s][:, :]).then_inc(self.var_done.sem, 1)

    def pool_rstd(self, pool, rnd, t):
        n, k, s = self.tile(rnd, t)
        pool.wait_ge(self.var_done.sem, self.var_done.done(n))
        pool.sem_inc(self.passed, 1)
        pool.tensor_scalar(self.var_eps[s][:, :], self.mean_var[s][:, 1:2], EPS, None, ALU.add).then_inc(
            self.eps_added.sem, 1)
        pool.wait_ge(self.eps_added.sem, self.eps_added.done(n))
        pool.tensor_tensor(self.rstd[s][:, :], self.var_eps[s][:, :], self.half[:, :], ALU.pow).then_inc(
            self.rstd_done.sem, 1)

    def dve_norm(self, dve, rnd, t):
        n, k, s = self.tile(rnd, t)
        dve.wait_ge(self.rstd_done.sem, self.rstd_done.done(n))
        dve.tensor_scalar(self.sum[s][:, :], self.sum[s][:, :], self.mean_var[s][:, 0:1], self.rstd[s][:, :],
                          ALU.subtract, ALU.mult).then_inc(self.normed.sem, 1)

    def pool_finish(self, pool, rnd, t):
        n, k, s = self.tile(rnd, t)
        pool.wait_ge(self.normed.sem, self.normed.done(n))
        pool.wait_ge(self.stored[s].sem, self.stored[s].room(k, 1))
        pool.tensor_tensor(self.y[s][:, :], self.sum[s][:, :], self.rows[1][:, :], ALU.mult).then_inc(
            self.gained.sem, 1)
        pool.wait_ge(self.gained.sem, self.gained.done(n))
        pool.tensor_tensor(self.y[s][:, :], self.y[s][:, :], self.rows[2][:, :], ALU.add).then_inc(self.finished.sem, 1)




def project(nc, psum, ident, x, mask, weights, biases, halves, v_dram, bias_dram, open_max):
    T = 4
    CH = T * P
    BR = S // CH
    ROUNDS = B * BR
    MT = S // P // ROUNDS
    with ExitStack() as ctx:
        st = Stage(nc, ctx, "project")
        w = [st.halves(f"w{n}", [P, KC, D]) for n in "qkv"]
        split_weights(nc, "project_w", [
            (rows_of(m)[:, j:j + 2, :], h[0][:, j:j + 2, :], h[1][:, j:j + 2, :])
            for m, h in zip(weights, w) for j in range(0, KC, 2)])
        bcol = [st.sb(f"b{n}", [P, KC]) for n in "qk"]
        brow = st.sb("bv", [P, D])
        xn = st.sb("x", [P, T, D])
        xt = st.halves("xt", [P, KC, CH])
        out = [st.halves(n, [P, KC, CH]) for n in "qk"]
        vo = st.sb("v", [P, T, H0, HD0 + 1])
        mi = [st.sb(f"mask{j}", [P, S], I32) for j in range(MT)]
        mb = [st.sb(f"bias{j}", [P, S], BF16) for j in range(MT)]

        banks = st.banks(psum, [f"xt{c}" for c in range(KC)] + [f"{n}{o}" for n in "qk" for o in range(KC)]
                         + [f"v{t}" for t in range(T)])
        biases_in = st.count("biases_in", 16)
        ones_set = st.count("ones_set")
        x_in = st.count("x_in", 16)
        mask_in = [st.count(f"mask_in{j}", 16) for j in range(MT)]
        xt_hi = st.count("xt_hi")
        out_hi = st.count("qk_hi")
        bias_made = st.count("bias_made", ahead=MT)
        open_made = st.count("open_made", ahead=MT)
        halves_out = [st.count(f"{n}_stored", 32, 1) for n in "qk"]
        v_out = st.count("v_stored", 16, 1)
        bias_out = [st.count(f"bias_stored{j}", 16, 1) for j in range(MT)]

        def rounds(eng, one):
            with eng.Fori(0, ROUNDS) as r:
                one(r)

        with nc.Block() as block:

            @block.sync
            def _(sp):
                for t, src in zip(bcol, biases[:2]):
                    sp.dma_start(t[:, :], src.rearrange("(c p) -> p c", p=P), allow_slow_non_contiguous=True).then_inc(
                        biases_in.sem, 16)
                sp.dma_start(brow[:, :], biases[2].partition_broadcast(P)).then_inc(biases_in.sem, 16)

                def load(r):
                    sp.wait_ge(banks.ready, banks.made_before(r, f"xt{KC - 1}"))
                    sp.dma_start(xn[:, :, :], tokens_of(x, r * CH, T)).then_inc(x_in.sem, 16)
                    for m in range(MT):
                        sp.wait_ge(bias_made.sem, bias_made.room(r * MT + m, MT))
                        sp.dma_start(mi[m][:, :], mask[bass.ds((r * MT + m) * P, P), :]).then_inc(mask_in[m].sem, 16)

                def store(r):
                    for m in range(MT):
                        sp.wait_ge(bias_made.sem, bias_made.done(r * MT + m))
                        sp.dma_start(bias_dram[bass.ds((r * MT + m) * P, P), :], mb[m][:, :]).then_inc(
                            bias_out[m].sem, 16)
                    for m, n in enumerate("qk"):
                        for o in range(KC):
                            sp.wait_ge(banks.read_of(f"{n}{o}"), banks.drained(r, f"{n}{o}"))
                        for h in range(2):
                            dst = halves[m][h].rearrange("(c p) s -> p c s", p=P)[
                                :, bass.ds(r // BR * KC, KC), bass.ds(r % BR * CH, CH)]
                            sp.dma_start(dst, out[m][h][:, :, :].bitcast(F32)).then_inc(halves_out[m].sem, 16)
                    for t in range(T):
                        sp.wait_ge(banks.read_of(f"v{t}"), banks.drained(r, f"v{t}"))
                    sp.dma_start(tokens_of(v_dram, r * CH, T),
                                          vo[:, :, :, :].rearrange("p t h d -> p t (h d)")).then_inc(v_out.sem, 16)

                stores = (*halves_out, v_out, *bias_out)
                for c in stores:
                    sp.sem_inc(c.sem, c.start)
                load(0)
                with sp.Fori(0, ROUNDS - 1) as r:
                    load(r + 1)
                    store(r)
                store(ROUNDS - 1)
                for c in stores:
                    sp.wait_ge(c.sem, c.done(ROUNDS - 1))

            @block.tensor
            def _(pe):
                pe.sem_inc(banks.ready, len(banks.names))
                for sem in banks.read:
                    pe.sem_inc(sem, 1)

                def one(r):
                    pe.wait_ge(x_in.sem, x_in.done(r))
                    for c in range(KC):
                        pe.wait_ge(banks.read_of(f"xt{c}"), banks.free(r, f"xt{c}"))
                        for t in range(T):
                            last = pe.transpose(banks.bank(f"xt{c}")[:, t * P:(t + 1) * P],
                                                xn[:, t, c * P:(c + 1) * P], ident[:, :])
                        last.then_inc(banks.ready, 1)
                    for m, n in enumerate("qk"):
                        for o in range(KC):
                            pe.wait_ge(banks.read_of(f"{n}{o}"), banks.free(r, f"{n}{o}"))
                            for c in range(KC):
                                if m == 0 and o == 0:
                                    pe.wait_ge(banks.read_of(f"xt{c}"), banks.drained(r, f"xt{c}"))
                                last = product(pe, banks.bank(f"{n}{o}"),
                                               [h[:, c, o * P:(o + 1) * P] for h in w[m]],
                                               [h[:, c, :] for h in xt], c == 0, c == KC - 1)
                            last.then_inc(banks.ready, 1)
                    for t in range(T):
                        pe.wait_ge(banks.read_of(f"v{t}"), banks.free(r, f"v{t}"))
                        for c in range(KC):
                            last = product(pe, banks.bank(f"v{t}"), [h[:, c, t * P:(t + 1) * P] for h in xt],
                                           [h[:, c, :] for h in w[2]], c == 0, c == KC - 1)
                        last.then_inc(banks.ready, 1)

                rounds(pe, one)

            @block.scalar
            def _(act):
                act.wait_ge(biases_in.sem, biases_in.done(2))

                def one(r):
                    for c in range(KC):
                        act.wait_ge(banks.ready, banks.made(r, f"xt{c}"))
                        act.wait_ge(banks.ready, banks.made_before(r, f"v{T - 1}"))
                        act.activation(xt[0][:, c, :], banks.bank(f"xt{c}"), ACT.Copy).then_inc(xt_hi.sem, 1)
                    for m, n in enumerate("qk"):
                        act.wait_ge(halves_out[m].sem, halves_out[m].room(r, 1))
                        for o in range(KC):
                            act.wait_ge(banks.ready, banks.made(r, f"{n}{o}"))
                            act.activation(out[m][0][:, o, :], banks.bank(f"{n}{o}"), ACT.Identity,
                                                     bias=bcol[m][:, o:o + 1]).then_inc(out_hi.sem, 1)

                rounds(act, one)

            @block.vector
            def _(dve):
                dve.sem_inc(bias_made.sem, bias_made.start)
                dve.sem_inc(open_made.sem, open_made.start)
                dve.memset(vo[:, :, :, HD0:], 1.0).then_inc(ones_set.sem, 1)
                dve.wait_ge(ones_set.sem, ones_set.done(0))
                dve.wait_ge(biases_in.sem, biases_in.done(2))

                def one(r):
                    for c in range(KC):
                        dve.wait_ge(xt_hi.sem, xt_hi.done(r * KC + c))
                        dve.tensor_tensor(xt[1][:, c, :], banks.bank(f"xt{c}"),
                                                        xt[0][:, c, :].bitcast(F32), ALU.subtract).then_inc(
                                                            banks.read_of(f"xt{c}"), 1)
                    for m in range(MT):
                        dve.wait_ge(mask_in[m].sem, mask_in[m].done(r))
                        dve.wait_ge(bias_out[m].sem, bias_out[m].room(r, 1))
                        dve.wait_ge(open_made.sem, open_made.room(r * MT + m, MT))
                        dve.tensor_scalar(mb[m][:, :], mi[m][:, :], 0.0, -BIG,
                                                       ALU.not_equal, ALU.mult).then_inc(bias_made.sem, 1)
                    for m, n in enumerate("qk"):
                        dve.wait_ge(halves_out[m].sem, halves_out[m].room(r, 1))
                        for o in range(KC):
                            dve.wait_ge(out_hi.sem, out_hi.done(r * 2 * KC + (m * KC + o)))
                            dve.scalar_tensor_tensor(
                                out[m][1][:, o, :], banks.bank(f"{n}{o}"), bcol[m][:, o:o + 1],
                                out[m][0][:, o, :].bitcast(F32), ALU.add, ALU.subtract).then_inc(
                                    banks.read_of(f"{n}{o}"), 1)
                        if m < MT:
                            dve.wait_ge(bias_made.sem, bias_made.done(r * MT + m))
                            dve.tensor_reduce(
                                open_max[:, bass.ds(r * MT + m, 1), :].rearrange("p o k -> p (o k)"),
                                mb[m][:, :].rearrange("p (k s) -> p k s", s=KEYS), AX.X, ALU.max).then_inc(
                                    open_made.sem, 1)
                    dve.wait_ge(v_out.sem, v_out.room(r, 1))
                    for t in range(T):
                        dve.wait_ge(banks.ready, banks.made(r, f"v{t}"))
                        dve.tensor_tensor(
                            vo[:, t, :, 0:HD0], banks.bank(f"v{t}").rearrange("p (h d) -> p h d", d=HD0),
                            brow[:, :].rearrange("p (h d) -> p h d", d=HD0), ALU.add).then_inc(
                                banks.read_of(f"v{t}"), 1)

                rounds(dve, one)




def choose_window(nc, psum, ones, open_max, choice):
    NB, NT = S // KEYS, S // P
    with ExitStack() as ctx:
        st = Stage(nc, ctx, "choose")
        is_open = st.sb("is_open", [P, NT * NB])
        rows = st.sb("rows", [P, NB])
        full, empty, which = st.sb("full", [P, NB]), st.sb("empty", [P, NB]), st.sb("which", [P, NB])
        votes, res = st.sb("votes", [P, NB]), st.sb("res", [P, 2])
        place = st.sb("place", [P, NB])
        yes = st.sb("yes", [P, 2])
        step, counted = st.sem("step"), st.sem("counted")
        with nc.Block() as block:

            @block.vector
            def _(dve):
                n = 0

                def link(ins):
                    nonlocal n
                    n += 1
                    ins.then_inc(step, 1)
                    dve.wait_ge(step, n)

                link(dve.tensor_scalar(is_open[:, :], open_max[:, :, :].rearrange("p t k -> p (t k)"), 0.0, None,
                                       ALU.is_equal))
                for k in range(NB):
                    link(dve.memset(place[:, k:k + 1], float(k)))
                dve.wait_ge(counted, 1)
                link(dve.tensor_reduce(rows[:, :], psum[:, 0, 0:NT * NB].rearrange("p (t k) -> p k t", k=NB),
                                       AX.X, ALU.add))
                link(dve.tensor_scalar(full[:, :], rows[:, :], float(S), None, ALU.is_equal))
                link(dve.tensor_scalar(empty[:, :], rows[:, :], 0.0, None, ALU.is_equal))
                link(dve.scalar_tensor_tensor(votes[:, :], full[:, :], float(NB), empty[:, :], ALU.mult, ALU.add))
                link(dve.tensor_reduce(res[:, 0:1], votes[:, :], AX.X, ALU.add))
                link(dve.tensor_scalar(yes[:, 0:1], res[:, 0:1], float(2 * NB - 1), None, ALU.is_equal))
                link(dve.tensor_tensor(which[:, :], full[:, :], place[:, :], ALU.mult))
                link(dve.tensor_reduce(res[:, 1:2], which[:, :], AX.X, ALU.add))
                link(dve.tensor_tensor(yes[:, 1:2], res[:, 1:2], yes[:, 0:1], ALU.mult))
                link(dve.tensor_copy(choice[:, :], yes[0:1, :]))

            @block.tensor
            def _(pe):
                pe.wait_ge(step, 1)
                pe.matmul(psum[:, 0, 0:NT * NB], ones[:, :], is_open[:, :], start=True, stop=True).then_inc(counted, 1)


def attend(nc, psum, ident, halves, v_dram, bias_dram, att_dram, sums_dram, blocks, first):
    NK = blocks * KEYS
    G = 4
    NT = S // P
    TG = G // blocks
    HU = 2 if blocks == 1 else 1
    KT = KEYS // P
    U = G * HU
    SETS = 2 if blocks == 1 else 1
    NS = HU * NT * blocks
    N = SETS * NS
    WS, HEADS = NS // U, SETS * HU
    ROUNDS = B * H0 // HEADS
    HV = HD0 + 1
    PLACES = 16 if blocks == 1 else 8
    QW = TG * P
    MV = 2 * HD0
    SCORE, EXP, TURN = (17, 12, 9) if blocks == 1 else (10, 6, 5)
    assert N % PLACES == 0 and N // G % 4 == 0 and N // U % 2 == 0
    SCALE = float(HD0) ** -0.5
    TOFS, OOFS = 4, 6
    with ExitStack() as ctx:
        st = Stage(nc, ctx, f"attend{blocks}")
        bias = st.sb("bias", [P, NT, NK], BF16)
        v = st.sb("v", [P, NK // P, B, H0 * HV])
        kst, qst = ([[st.sb(f"{n}{m}{u}", [P, width], F32R) for u in range(HU)] for m in range(SETS)]
                    for n, width in (("k", NK), ("q", S)))
        pr = st.sb("weights", [P, PLACES, KEYS])
        pt = [[st.sb(f"weights_t{s}{u}", [P, G, KEYS]) for u in range(HU)] for s in range(2)]
        mx = st.sb("max", [P, 4, G])
        gmx = st.sb("group_max", [P, 4])
        neg = st.sb("neg_max", [P, 4, G])
        vh = [[st.sb(f"v_of_head{m}{u}", [P, NK // P, MV]) for u in range(HU)] for m in range(SETS)]
        ao = [st.sb(f"out{m}", [HU * MV, S]) for m in range(SETS)]

        bias_in = [st.count(f"bias_in{m}", 16) for m in range(2)]
        v_in = st.count("v_in", 16)
        passed = st.sem("waits_passed")
        kq_in = [st.count(f"kq_in{m}", 16 * 8 * HU) for m in range(SETS)]
        scored = st.count("scored", ahead=N)
        masked = st.count("masked", ahead=4)
        group_max = st.count("group_max_done")
        shifted = st.count("shift_done")
        exped = st.count("exp_done")
        turned = st.count("transposed", ahead=PLACES)
        moved = st.count("transposed_moved", ahead=2)
        summed = st.count("summed", ahead=max(2 * G, N // U * G))
        ones_set = st.count("ones_set")
        v_here = [st.count(f"v_of_head{m}", HU) for m in range(SETS)]
        taken = st.count("sums_taken", ahead=2)
        stored = [st.count(f"stored{m}", 32 * HU, 1) for m in range(SETS)]

        def place(n):
            m, k = n // NS, n % NS
            return (m, k % U // G, k // U * G + k % G, 0) if blocks == 1 else (m, 0, k // G, k % G)

        with nc.Block() as block:

            @block.sync
            def _(sp):
                def load(i, m):
                    sp.wait_ge(scored.sem, scored.room(i * N + ((m + 1) * NS - 1), N))
                    for u in range(HU):
                        row = i * (HEADS * HD0) + (m * HU + u) * HD0
                        for part in range(4):
                            rows = slice(part * HD0, (part + 1) * HD0)
                            sp.dma_start(kst[m][u][rows, :].bitcast(F32), halves[1][part % 2][
                                bass.ds(row, HD0), bass.ds(first * KEYS, NK)]).then_inc(kq_in[m].sem, 16)
                            sp.dma_start(qst[m][u][rows, :].bitcast(F32), halves[0][part // 2][
                                bass.ds(row, HD0), :]).then_inc(kq_in[m].sem, 16)

                def store(i, m):
                    sp.wait_ge(taken.sem, taken.done(i * (N // U) + ((m + 1) * WS - 1)))
                    for u in range(HU):
                        head = i * HEADS + (m * HU + u)
                        sp.dma_start(att_dram[bass.ds(head * HD0, HD0), :],
                                     ao[m][u * MV:u * MV + HD0, :]).then_inc(stored[m].sem, 16)
                        sp.dma_start(sums_dram[bass.ds(head, 1), :],
                                     ao[m][u * MV + HD0:u * MV + HD0 + 1, :]).then_inc(stored[m].sem, 16)

                def load_bias(m, tiles):
                    sp.dma_start(bias[:, tiles, :], bias_dram.rearrange("(t p) s -> p t s", p=P)[
                        :, tiles, bass.ds(first * KEYS, NK)]).then_inc(bias_in[m].sem, 16)

                load_bias(0, slice(0, G))
                load(0, 0)
                load_bias(1, slice(G, NT))
                for b in range(B):
                    sp.dma_start(v[:, :, b, :], v_dram[bass.ds(first * KEYS + b * S, NK), :].rearrange(
                        "(t p) n -> p t n", p=P)).then_inc(v_in.sem, 16)
                for m in range(1, SETS):
                    load(0, m)
                with sp.Fori(0, ROUNDS - 1) as i:
                    for m in range(SETS):
                        load(i + 1, m)
                        store(i, m)
                for m in range(SETS):
                    store(ROUNDS - 1, m)
                for m in range(SETS):
                    sp.wait_ge(stored[m].sem, stored[m].done(ROUNDS - 1))

            @block.tensor
            def _(pe):
                pe.sem_inc(scored.sem, scored.start)
                pe.sem_inc(turned.sem, turned.start)
                pe.sem_inc(summed.sem, summed.start)

                def score(i, n):
                    m, u, qt, kb = place(n)
                    if n % NS == 0:
                        pe.wait_ge(kq_in[m].sem, kq_in[m].done(i))
                    pe.wait_ge(masked.sem, masked.room(i * N + n, 4))
                    pe.matmul(psum[:, n % 4, :], qst[m][u][:, qt * P:(qt + 1) * P],
                                        kst[m][u][:, kb * KEYS:(kb + 1) * KEYS], start=True, stop=True).then_inc(
                                            scored.sem, 1)

                def turn(i, n):
                    pe.wait_ge(exped.sem, exped.done(i * N + n))
                    pe.wait_ge(moved.sem, moved.room(i * N + n, 2))
                    for c in range(KT):
                        last = pe.transpose(psum[:, TOFS + n % 2, c * P:(c + 1) * P],
                                            pr[:, n % PLACES, c * P:(c + 1) * P], ident[:, :])
                    last.then_inc(turned.sem, 1)

                def weigh(i, n):
                    w, k, m = n // U, n % U, n // NS
                    if n % NS == 0:
                        pe.wait_ge(v_here[m].sem, v_here[m].done(i))
                    if k == 0:
                        pe.wait_ge(moved.sem, moved.done(i * N + n + (U - 1)))
                        pe.wait_ge(taken.sem, taken.room(i * (N // U) + w, 2))
                    if k % HU:
                        return
                    j = k // HU
                    tiles = 1 if blocks == 1 else KT
                    for c in range(tiles):
                        for u in range(HU):
                            last = pe.matmul(psum[u * MV:(u + 1) * MV, OOFS + w % 2, 0:QW],
                                             vh[m][u][:, j * tiles + c, :], pt[w % 2][u][:, j, c * P:c * P + QW],
                                             start=j == 0 and c == 0, stop=j == G - 1 and c == tiles - 1)
                    last.then_inc(summed.sem, 1)

                def one(i, more):
                    for n in range(N):
                        if n + SCORE < N or more:
                            score(i + (n + SCORE) // N, (n + SCORE) % N)
                        if n + TURN < N or more:
                            turn(i + (n + TURN) // N, (n + TURN) % N)
                        weigh(i, n)

                for n in range(SCORE):
                    score(0, n)
                for n in range(TURN):
                    turn(0, n)
                with pe.Fori(0, ROUNDS - 1) as i:
                    one(i, True)
                one(ROUNDS - 1, False)

            @block.scalar
            def _(act):
                act.sem_inc(moved.sem, moved.start)

                def exp(i, n):
                    j = n % G
                    act.wait_ge(shifted.sem, shifted.done(i * (N // G) + n // G))
                    bias_of = neg[:, n // G % 4, j:j + 1] if blocks == 1 else neg[:, n // G % 4, 0:1]
                    act.activation(pr[:, n % PLACES, :], pr[:, n % PLACES, :], ACT.Exp, bias=bias_of,
                                   scale=SCALE).then_inc(exped.sem, 1)

                def move(i, n):
                    j, w, u = n % G, n // U, n % U // G
                    act.wait_ge(turned.sem, turned.done(i * N + n))
                    act.wait_ge(summed.sem, summed.room(i * (N // U * G) + (w * G + (G - 1)), 2 * G))
                    res = psum[:, TOFS + n % 2, :]
                    if blocks == 1:
                        act.activation(pt[w % 2][u][:, :, j * P:(j + 1) * P], res.rearrange("p (c q) -> p c q", q=P),
                                       ACT.Copy).then_inc(moved.sem, 1)
                    else:
                        act.activation(pt[w % 2][u][:, j, :], res, ACT.Copy).then_inc(moved.sem, 1)

                def one(i, more):
                    for n in range(N):
                        if n + TURN < N or more:
                            move(i + (n + TURN) // N, (n + TURN) % N)
                        if n + EXP < N or more:
                            exp(i + (n + EXP) // N, (n + EXP) % N)

                for n in range(EXP):
                    exp(0, n)
                for n in range(TURN):
                    move(0, n)
                with act.Fori(0, ROUNDS - 1) as i:
                    one(i, True)
                one(ROUNDS - 1, False)

            @block.gpsimd
            def _(pool):
                for m in range(SETS):
                    pool.sem_inc(stored[m].sem, stored[m].start)
                    for u in range(HU):
                        pool.memset(vh[m][u][:, :, HD0:], 1.0).then_inc(ones_set.sem, 1)
                pool.wait_ge(ones_set.sem, ones_set.done(HEADS - 1))
                pool.wait_ge(v_in.sem, v_in.done(B - 1))
                with pool.Fori(0, ROUNDS) as i:
                    for m in range(SETS):
                        pool.wait_ge(summed.sem, summed.room(i * (N // U * G) + ((m + 1) * WS * G - 1), N // U * G))
                        pool.sem_inc(passed, 1)
                        for u in range(HU):
                            pool.tensor_copy(vh[m][u][:, :, 0:HD0], v[:, :, :, :].rearrange("p t b n -> p t (b n)")[
                                :, :, bass.ds(i * (HEADS * HV) + (m * HU + u) * HV, HD0)]).then_inc(v_here[m].sem, 1)

            @block.vector
            def _(dve):
                dve.sem_inc(masked.sem, masked.start)
                dve.sem_inc(taken.sem, taken.start)
                dve.wait_ge(bias_in[0].sem, bias_in[0].done(0))

                def mask(i, n):
                    _, _, qt, kb = place(n)
                    dve.wait_ge(scored.sem, scored.done(i * N + n))
                    dve.wait_ge(turned.sem, turned.room(i * N + n, PLACES))
                    dve.sem_inc(passed, 1)
                    dve.tensor_tensor_reduce(
                        pr[:, n % PLACES, :], psum[:, n % 4, :], bias[:, qt, kb * KEYS:(kb + 1) * KEYS], 1.0,
                        -3.0e38, ALU.add, ALU.max, mx[:, n // G % 4, n % G:n % G + 1]).then_inc(masked.sem, 1)
                    if n % G == G - 1:
                        g, p = i * (N // G) + n // G, n // G % 4
                        dve.wait_ge(masked.sem, masked.done(i * N + n))
                        if blocks == 1:
                            dve.tensor_scalar(neg[:, p, :], mx[:, p, :], -SCALE, None, ALU.mult).then_inc(
                                shifted.sem, 1)
                        else:
                            dve.tensor_reduce(gmx[:, p:p + 1], mx[:, p, :], AX.X, ALU.max).then_inc(group_max.sem, 1)
                            dve.wait_ge(group_max.sem, group_max.done(g))
                            dve.tensor_scalar(neg[:, p, 0:1], gmx[:, p:p + 1], -SCALE, None, ALU.mult).then_inc(
                                shifted.sem, 1)

                def take(i, n):
                    w, m = n // U, n // NS
                    if w % WS == 0:
                        dve.wait_ge(stored[m].sem, stored[m].room(i, 1))
                    dve.wait_ge(summed.sem, summed.done(i * (N // U * G) + (w * G + (G - 1))))
                    dve.tensor_copy(ao[m][:, w % WS * QW:(w % WS + 1) * QW], psum[0:HU * MV, OOFS + w % 2, 0:QW]).then_inc(
                        taken.sem, 1)

                def one(i, more):
                    for n in range(N):
                        if n + SCORE < N or more:
                            mask(i + (n + SCORE) // N, (n + SCORE) % N)
                        if n % U == U - 1:
                            take(i, n)

                for n in range(SCORE):
                    if place(n)[2] == G:
                        dve.wait_ge(bias_in[1].sem, bias_in[1].done(0))
                    mask(0, n)
                dve.wait_ge(bias_in[1].sem, bias_in[1].done(0))
                with dve.Fori(0, ROUNDS - 1) as i:
                    one(i, True)
                one(ROUNDS - 1, False)




def invert_sums(nc, sums_dram, inverse_dram, weight_jobs):
    with ExitStack() as ctx:
        st = Stage(nc, ctx, "invert")
        rows = st.sb("sums", [P, B * H0 * S // P])
        moved, inverted = st.count("moved", 16), st.count("inverted")
        splitter = Splitter(st, weight_jobs)
        assert len(weight_jobs) <= splitter.SLOTS

        def flat(m):
            return m.rearrange("h (c q) -> (h c) q", q=B * H0 * S // P)

        with nc.Block() as block:

            @block.sync
            def _(sp):
                sp.dma_start(rows[:, :], flat(sums_dram)).then_inc(moved.sem, 16)
                splitter.sync(sp)
                sp.wait_ge(inverted.sem, inverted.done(0))
                sp.dma_start(flat(inverse_dram), rows[:, :]).then_inc(moved.sem, 16)
                sp.wait_ge(moved.sem, moved.done(1))

            @block.scalar
            def _(act):
                splitter.scalar(act)

            @block.vector
            def _(dve):
                dve.wait_ge(moved.sem, moved.done(0))
                dve.reciprocal(rows[:, :], rows[:, :]).then_inc(inverted.sem, 1)
                splitter.vector(dve)


def join(nc, psum, consts, att_dram, sums_dram, inverse_dram, x, out, weight, bias, gain, shift):
    _, half = consts
    T = 4
    CH = T * P
    ROUNDS = TOK // CH
    HT = P // HD0
    with ExitStack() as ctx:
        st = Stage(nc, ctx, "join")
        w = st.halves("w", [P, KC, D])
        invert_sums(nc, sums_dram, inverse_dram, [
            (rows_of(weight)[:, j:j + 2, :], w[0][:, j:j + 2, :], w[1][:, j:j + 2, :])
                                     for j in range(0, KC, 2)])
        raw, inv = ([st.sb(f"{n}{u}", [P, KC, CH]) for u in range(2)] for n in ("att", "inverse"))
        quo = st.sb("quotient", [P, KC, CH])
        at = [st.halves(f"att_t{s}", [P, KC, CH]) for s in range(2)]
        tail = Tail(st, 2 * T, x, out, bias, gain, shift, half, depth=4, bias_in_product=True)
        one_row, bias_row = st.sb("one_row", [1, P], F32R), st.halves("bias_row", [1, D])
        bias_split, one_set = st.sem("bias_row_split"), st.sem("one_row_set")
        banks = st.banks(psum, [f"y{u}{t}" for u in range(2) for t in range(T)])
        a_in = [st.count(f"att_in{u}", 16 * (1 + HT)) for u in range(2)]
        divided = st.count("divided", ahead=2 * KC)
        at_hi = st.count("att_t_hi", ahead=KC)
        split = st.count("att_t_split", ahead=1)
        with nc.Block() as block:

            @block.sync
            def _(sp):
                RB = ROUNDS // B

                def load(r, u):
                    sp.wait_ge(divided.sem, divided.room(r * KC + (KC - 1), 2 * KC))
                    cols = bass.ds(r % RB * CH, CH)
                    sp.dma_start(raw[u][:, :, :], att_dram.rearrange("(c p) q -> p c q", p=P)[
                        :, bass.ds(r // RB * KC, KC), cols]).then_inc(a_in[u].sem, 16)
                    for h in range(HT):
                        sp.dma_start(inv[u][h * HD0:(h + 1) * HD0, :, :], inverse_dram.rearrange(
                            "(c h) q -> h c q", h=HT)[h, bass.ds(r // RB * KC, KC), cols].partition_broadcast(
                                HD0)).then_inc(a_in[u].sem, 16)

                tail.run_sync(sp, ROUNDS // 2, load, parts=2, lead=2)

            @block.tensor
            def _(pe):
                pe.sem_inc(banks.ready, len(banks.names))
                for sem in banks.read:
                    pe.sem_inc(sem, 1)
                pe.wait_ge(bias_split, 2)
                pe.wait_ge(one_set, 1)
                with pe.Fori(0, ROUNDS // 2) as k:
                    for u in range(2):
                        for t in range(T):
                            pe.wait_ge(banks.read_of(f"y{u}{t}"), banks.free(k, f"y{u}{t}"))
                            for n, h in enumerate(bias_row):
                                pe.matmul(banks.bank(f"y{u}{t}"), one_row[:, :], h[:, :], start=n == 0, stop=False)
                            for c in range(KC):
                                if t == 0:
                                    pe.wait_ge(split.sem, split.done(k * 2 * KC + (u * KC + c)))
                                last = product(pe, banks.bank(f"y{u}{t}"),
                                               [h[:, c, t * P:(t + 1) * P] for h in at[u]],
                                               [h[:, c, :] for h in w], False, c == KC - 1)
                            last.then_inc(banks.ready, 1)

            @block.scalar
            def _(act):
                act.sem_inc(at_hi.sem, at_hi.start)
                act.wait_ge(tail.rows_in.sem, tail.rows_in.done(2))
                act.activation(bias_row[0][:, :], tail.rows[0][0:1, :], ACT.Copy).then_inc(bias_split, 1)
                with act.Fori(0, ROUNDS // 2) as k:
                    for u in range(2):
                        act.wait_ge(banks.ready, banks.made_before(k, f"y{u}{T - 1}"))
                        for c in range(KC):
                            act.wait_ge(divided.sem, divided.done(k * 2 * KC + (u * KC + c)))
                            act.activation(at[u][0][:, c, :], quo[:, c, :], ACT.Copy).then_inc(at_hi.sem, 1)

            @block.vector
            def _(dve):
                tail.start_dve(dve)
                dve.sem_inc(divided.sem, divided.start)
                dve.sem_inc(split.sem, split.start)

                def ready(k, u):
                    dve.wait_ge(a_in[u].sem, a_in[u].done(k))
                    for c in range(KC):
                        n = k * 2 * KC + (u * KC + c)
                        dve.wait_ge(at_hi.sem, at_hi.room(n, KC))
                        if c == 0:
                            dve.wait_ge(split.sem, split.done(n - 1))
                        dve.tensor_tensor(quo[:, c, :], raw[u][:, c, :], inv[u][:, c, :], ALU.mult).then_inc(
                            divided.sem, 1)
                    for c in range(KC):
                        n = k * 2 * KC + (u * KC + c)
                        dve.wait_ge(at_hi.sem, at_hi.done(n))
                        dve.tensor_tensor(at[u][1][:, c, :], quo[:, c, :], at[u][0][:, c, :].bitcast(F32),
                                          ALU.subtract).then_inc(split.sem, 1)

                def tails(k, u):
                    for t in range(T):
                        tail.dve_sum(dve, k, u * T + t, banks, f"y{u}{t}")
                        if t > 0:
                            tail.dve_norm(dve, k, u * T + t - 1)
                    tail.dve_norm(dve, k, u * T + T - 1)

                dve.wait_ge(bias_split, 1)
                dve.tensor_tensor(bias_row[1][:, :], tail.rows[0][0:1, :], bias_row[0][:, :].bitcast(F32),
                                  ALU.subtract).then_inc(bias_split, 1)
                ready(0, 0)
                with dve.Fori(0, ROUNDS // 2 - 1) as k:
                    ready(k, 1)
                    tails(k, 0)
                    ready(k + 1, 0)
                    tails(k, 1)
                ready(ROUNDS // 2 - 1, 1)
                tails(ROUNDS // 2 - 1, 0)
                tails(ROUNDS // 2 - 1, 1)

            @block.gpsimd
            def _(pool):
                tail.start_pool(pool)
                pool.memset(one_row[:, :].bitcast(F32), 1.0).then_inc(one_set, 1)
                with pool.Fori(0, ROUNDS // 2) as k:
                    for t in range(2 * T):
                        tail.pool_rstd(pool, k, t)
                        if t > 0:
                            tail.pool_finish(pool, k, t - 1)
                    tail.pool_finish(pool, k, 2 * T - 1)




def cross(nc, psum, consts, name, heads, hd, x, context, ctx_mask, wq, bq, wk, bk, wv, bv, wo, bo, gain, shift,
          out):
    ident, half = consts
    T = 2
    CH = T * P
    ROUNDS = TOK // CH
    BR = ROUNDS // B
    W = heads * hd
    NG = W // P
    HG = P // hd
    SB, HB = 4, heads // 4
    GB = NG // SB
    NPART = T * SB
    SCALE = float(hd) ** -0.5
    masked = ctx_mask is not None
    parts = [(t, g) for t in range(T) for g in range(SB)]
    with ExitStack() as ctx:
        st = Stage(nc, ctx, name)
        w1, w2 = st.halves("wq", [P, KC, W]), st.halves("wo", [P, NG, D])
        bqc = st.sb("bq", [P, NG])
        kd = st.halves("k", [P, B * NG, HG * CTX])
        vc = st.sb("v", [CTX, B * heads, hd])
        mrow = st.sb("mask_row", [P, B, CTX])
        rows = 1024 // W
        cross_context(nc, psum, ident, name, heads, hd, context, ctx_mask, wk, bk, wv, bv, kd, vc, mrow, [
            *((rows_of(wq)[:, j:j + rows, :], w1[0][:, j:j + rows, :], w1[1][:, j:j + rows, :])
              for j in range(0, KC, rows)),
            *((rows_of(wo)[:, j:j + 2, :], w2[0][:, j:j + 2, :], w2[1][:, j:j + 2, :])
              for j in range(0, NG, 2))])

        xn = st.sb("x", [P, T, D])
        xt = st.halves("xt", [P, KC, CH])
        qt = st.halves("q", [P, NG, CH])
        sc = [st.sb(f"scores{t}", [P, heads, CTX]) for t in range(T)]
        mx = [st.sb(f"max{t}", [P, heads]) for t in range(T)]
        total = [st.sb(f"sum_of_weights{t}", [P, heads]) for t in range(T)]
        inv = [st.sb(f"inverse{t}", [P, heads]) for t in range(T)]
        pt = st.sb("weights_t", [CTX, heads, CH])
        vb = st.sb("v_of_batch", [CTX, heads, hd])
        at = st.halves("att_t", [P, NG, CH])
        tail = Tail(st, T, x, out, bo, gain, shift, half)

        names = [f"x{t}" for t in range(T)] + [f"s{t}{g}" for t, g in parts] + [f"y{t}" for t in range(T)]
        names += [f"q{o}" for o in range(NG)] + [f"p{t}{g}" for t, g in parts] + [f"o{o}" for o in range(NG)]
        banks = st.banks(psum, names)
        fixed_in = st.count("bq_in", 16)
        x_in = st.count("x_in", 16)
        xt_hi, q_hi, at_hi = st.count("xt_hi"), st.count("q_hi"), st.count("att_t_hi")
        maxed, shifted, exped = (st.count(n) for n in ("scores_max", "scores_shifted", "exp_done"))
        inverted, weighted = st.count("sum_inverted"), st.count("weights_normed")
        v_here = st.count("v_of_batch")
        def steps(eng, one):
            one(0, True, False, False)
            one(1, True, True, False)
            with eng.Fori(2, ROUNDS) as k:
                one(k, True, True, True)
            one(ROUNDS, False, True, True)
            one(ROUNDS + 1, False, False, True)

        with nc.Block() as block:

            @block.sync
            def _(sp):
                sp.dma_start(bqc[:, :], bq.rearrange("(c p) -> p c", p=P), allow_slow_non_contiguous=True).then_inc(
                    fixed_in.sem, 16)

                def load(r, _):
                    sp.wait_ge(banks.ready, banks.made_before(r, f"x{T - 1}"))
                    sp.dma_start(xn[:, :, :], tokens_of(x, r * CH, T)).then_inc(x_in.sem, 16)

                tail.run_sync(sp, ROUNDS, load, lead=2)

            @block.tensor
            def _(pe):
                pe.sem_inc(banks.ready, len(banks.names))
                for sem in banks.read:
                    pe.sem_inc(sem, 1)

                def transpose_x(k):
                    pe.wait_ge(x_in.sem, x_in.done(k))
                    for t in range(T):
                        pe.wait_ge(banks.read_of(f"x{t}"), banks.free(k, f"x{t}"))
                        for c in range(KC):
                            last = pe.transpose(banks.bank(f"x{t}")[:, c * P:(c + 1) * P],
                                                xn[:, t, c * P:(c + 1) * P], ident[:, :])
                        last.then_inc(banks.ready, 1)

                def make_q(k):
                    for t in range(T):
                        pe.wait_ge(banks.read_of(f"x{t}"), banks.drained(k, f"x{t}"))
                    for o in range(NG):
                        pe.wait_ge(banks.read_of(f"q{o}"), banks.free(k, f"q{o}"))
                        for c in range(KC):
                            last = product(pe, banks.bank(f"q{o}")[:, 0:CH], [h[:, c, o * P:(o + 1) * P] for h in w1],
                                           [h[:, c, :] for h in xt], c == 0, c == KC - 1)
                        last.then_inc(banks.ready, 1)

                def score(k):
                    b = (k - 1) // BR
                    for t, g in parts:
                        name = f"s{t}{g}"
                        pe.wait_ge(banks.read_of(name), banks.free(k, name))
                        for m in range(GB):
                            o = g * GB + m
                            if t == 0:
                                pe.wait_ge(banks.read_of(f"q{o}"), banks.drained(k - 1, f"q{o}"))
                            last = product(pe, banks.bank(name)[:, m * HG * CTX:(m + 1) * HG * CTX],
                                           [h[:, o, t * P:(t + 1) * P] for h in qt],
                                           [h[:, bass.ds(b * NG + o, 1), :].rearrange("p o n -> p (o n)")
                                            for h in kd], True, True)
                        last.then_inc(banks.ready, 1)

                def weigh(k):
                    for n, (t, g) in enumerate(parts):
                        name = f"p{t}{g}"
                        pe.wait_ge(banks.read_of(name), banks.free(k, name))
                        pe.wait_ge(weighted.sem, weighted.done((k - 1) * NPART + n))
                        for h in range(HB):
                            last = pe.transpose(banks.bank(name)[0:CTX, h * P:(h + 1) * P],
                                                sc[t][:, g * HB + h, :], ident[:, :])
                        last.then_inc(banks.ready, 1)
                    pe.wait_ge(v_here.sem, v_here.done(k - 1))
                    for o in range(NG):
                        pe.wait_ge(banks.read_of(f"o{o}"), banks.free(k, f"o{o}"))
                        for t in range(T):
                            name = f"p{t}{o * HG // HB}"
                            pe.wait_ge(banks.read_of(name), banks.drained(k, name))
                        for h in range(HG):
                            last = pe.matmul(banks.bank(f"o{o}")[h * hd:(h + 1) * hd, 0:CH], vb[:, o * HG + h, :],
                                             pt[:, o * HG + h, :], start=True, stop=True)
                        last.then_inc(banks.ready, 1)

                def project(k):
                    for t in range(T):
                        pe.wait_ge(banks.read_of(f"y{t}"), banks.free(k, f"y{t}"))
                        for o in range(NG):
                            if t == 0:
                                pe.wait_ge(banks.read_of(f"o{o}"), banks.drained(k - 1, f"o{o}"))
                            last = product(pe, banks.bank(f"y{t}"), [h[:, o, t * P:(t + 1) * P] for h in at],
                                           [h[:, o, :] for h in w2], o == 0, o == NG - 1)
                        last.then_inc(banks.ready, 1)

                def one(k, q, attention, output):
                    transpose_x(k) if q else skip(pe, banks, k, [f"x{t}" for t in range(T)])
                    score(k) if attention else skip(pe, banks, k, [f"s{t}{g}" for t, g in parts])
                    project(k) if output else skip(pe, banks, k, [f"y{t}" for t in range(T)])
                    make_q(k) if q else skip(pe, banks, k, [f"q{o}" for o in range(NG)])
                    if attention:
                        weigh(k)
                    else:
                        skip(pe, banks, k, [f"p{t}{g}" for t, g in parts] + [f"o{o}" for o in range(NG)])

                steps(pe, one)

            @block.scalar
            def _(act):
                act.wait_ge(fixed_in.sem, fixed_in.done(0))

                def one(k, q, attention, output):
                    if q:
                        for t in range(T):
                            act.wait_ge(banks.ready, banks.made(k, f"x{t}"))
                            act.activation(xt[0][:, :, t * P:(t + 1) * P],
                                           banks.bank(f"x{t}").rearrange("p (c q) -> p c q", q=P),
                                           ACT.Copy).then_inc(xt_hi.sem, 1)
                    if attention:
                        for n, (t, g) in enumerate(parts):
                            if masked:
                                act.wait_ge(shifted.sem, shifted.done((k - 1) * NPART + n))
                            else:
                                act.wait_ge(banks.read_of(f"s{t}{g}"), banks.drained(k, f"s{t}{g}"))
                            for h in range(g * HB, (g + 1) * HB):
                                last = act.activation(sc[t][:, h, :], sc[t][:, h, :], ACT.Exp, scale=SCALE,
                                                      accum_out=total[t][:, h:h + 1])
                            last.then_inc(exped.sem, 1)
                    if q:
                        for o in range(NG):
                            act.wait_ge(banks.ready, banks.made(k, f"q{o}"))
                            act.activation(qt[0][:, o, :], banks.bank(f"q{o}")[:, 0:CH], ACT.Identity,
                                           bias=bqc[:, o:o + 1]).then_inc(q_hi.sem, 1)
                    if attention:
                        for t, g in parts:
                            act.wait_ge(banks.ready, banks.made(k, f"p{t}{g}"))
                            act.activation(pt[:, g * HB:(g + 1) * HB, t * P:(t + 1) * P],
                                           banks.bank(f"p{t}{g}")[0:CTX, :].rearrange("p (h q) -> p h q", q=P),
                                           ACT.Copy).then_inc(banks.read_of(f"p{t}{g}"), 1)
                        for o in range(NG):
                            act.wait_ge(banks.ready, banks.made(k, f"o{o}"))
                            act.activation(at[0][:, o, :], banks.bank(f"o{o}")[:, 0:CH], ACT.Copy).then_inc(
                                at_hi.sem, 1)

                steps(act, one)

            @block.vector
            def _(dve):
                tail.start_dve(dve)

                def shift_scores(k, n):
                    t, g = parts[n]
                    name, m = f"s{t}{g}", (k - 1) * NPART + n
                    res = banks.bank(name)[:, 0:HB * CTX].rearrange("p (h k) -> p h k", k=CTX)
                    part = sc[t][:, g * HB:(g + 1) * HB, :]
                    top = mx[t][:, g * HB:(g + 1) * HB]
                    top_wide = top.unsqueeze(2).to_broadcast([P, HB, CTX])
                    dve.wait_ge(banks.ready, banks.made(k, name))
                    if masked:
                        b = (k - 1) // BR
                        dve.tensor_tensor(part, res, mrow[:, bass.ds(b, 1), :].to_broadcast([P, HB, CTX]),
                                          ALU.add).then_inc(banks.read_of(name), 1)
                        dve.wait_ge(banks.read_of(name), banks.drained(k, name))
                        dve.tensor_reduce(top, part, AX.X, ALU.max).then_inc(maxed.sem, 1)
                        dve.wait_ge(maxed.sem, maxed.done(m))
                        dve.tensor_tensor(part, part, top_wide, ALU.subtract).then_inc(shifted.sem, 1)
                    else:
                        dve.tensor_reduce(top, res, AX.X, ALU.max).then_inc(maxed.sem, 1)
                        dve.wait_ge(maxed.sem, maxed.done(m))
                        dve.tensor_tensor(part, res, top_wide, ALU.subtract).then_inc(banks.read_of(name), 1)

                def invert_sum(k, n):
                    t, g = parts[n]
                    m, hs = (k - 1) * NPART + n, slice(g * HB, (g + 1) * HB)
                    dve.wait_ge(exped.sem, exped.done(m))
                    dve.reciprocal(inv[t][:, hs], total[t][:, hs]).then_inc(inverted.sem, 1)

                def one(k, q, attention, output):
                    if q:
                        for t in range(T):
                            dve.wait_ge(xt_hi.sem, xt_hi.done(k * T + t))
                            dve.tensor_tensor(xt[1][:, :, t * P:(t + 1) * P],
                                              banks.bank(f"x{t}").rearrange("p (c q) -> p c q", q=P),
                                              xt[0][:, :, t * P:(t + 1) * P].bitcast(F32),
                                              ALU.subtract).then_inc(banks.read_of(f"x{t}"), 1)
                    if attention:
                        for n in range(NPART + 2):
                            if n < NPART:
                                shift_scores(k, n)
                            if n >= 2:
                                invert_sum(k, n - 2)
                    if output:
                        for t in range(T):
                            tail.dve_sum(dve, k - 2, t, banks, f"y{t}", k)
                    if q:
                        for o in range(NG):
                            dve.wait_ge(q_hi.sem, q_hi.done(k * NG + o))
                            dve.scalar_tensor_tensor(
                                qt[1][:, o, :], banks.bank(f"q{o}")[:, 0:CH], bqc[:, o:o + 1],
                                qt[0][:, o, :].bitcast(F32), ALU.add, ALU.subtract).then_inc(banks.read_of(f"q{o}"), 1)
                    if output:
                        for t in range(T):
                            tail.dve_norm(dve, k - 2, t)
                    if attention:
                        for o in range(NG):
                            dve.wait_ge(at_hi.sem, at_hi.done((k - 1) * NG + o))
                            dve.tensor_tensor(at[1][:, o, :], banks.bank(f"o{o}")[:, 0:CH],
                                              at[0][:, o, :].bitcast(F32), ALU.subtract).then_inc(
                                                  banks.read_of(f"o{o}"), 1)

                steps(dve, one)

            @block.gpsimd
            def _(pool):
                tail.start_pool(pool)

                def one(k, q, attention, output):
                    if output:
                        for t in range(T):
                            tail.pool_bias(pool, k - 2, t)
                    if attention:
                        pool.wait_ge(banks.ready, banks.made_before(k, f"o{NG - 1}"))
                        pool.sem_inc(tail.passed, 1)
                        pool.tensor_copy(vb[:, :, :], vc[:, bass.ds((k - 1) // BR * heads, heads), :]).then_inc(
                            v_here.sem, 1)
                        for n, (t, g) in enumerate(parts):
                            hs = slice(g * HB, (g + 1) * HB)
                            pool.wait_ge(inverted.sem, inverted.done((k - 1) * NPART + n))
                            pool.tensor_tensor(sc[t][:, hs, :], sc[t][:, hs, :],
                                               inv[t][:, hs].unsqueeze(2).to_broadcast([P, HB, CTX]),
                                               ALU.mult).then_inc(weighted.sem, 1)
                    if output:
                        for t in range(T):
                            tail.pool_rstd(pool, k - 2, t)
                        for t in range(T):
                            tail.pool_finish(pool, k - 2, t)

                steps(pool, one)


def cross_context(nc, psum, ident, name, heads, hd, context, ctx_mask, wk, bk, wv, bv, kd, vc, mrow,
                  weight_jobs):
    W = heads * hd
    NG, HG = W // P, P // hd
    VB = W // BANK
    with ExitStack() as ctx:
        st = Stage(nc, ctx, f"{name}_context")
        splitter = Splitter(st, weight_jobs)
        wks, wvs = st.sb("wk", [P, KC, W]), st.sb("wv", [P, KC, W])
        bkc, bvr = st.sb("bk", [P, NG]), st.sb("bv", [CTX, W])
        cn = st.sb("c", [CTX, B, D])
        ct = st.sb("ct", [P, KC, B, CTX])
        mi = st.sb("mask", [P, B, CTX], I32)
        k_loaded, v_loaded, zeroed = st.sem("k_loaded"), st.sem("v_loaded"), st.sem("zeroed")
        made, read, hi_done, built = st.sem("made"), st.sem("read"), st.sem("hi_done"), st.sem("built")
        k_loads = [(cn[:, :, :], context.rearrange("b s d -> s b d")), (bkc[:, :], bk.rearrange("(c p) -> p c", p=P)),
                   (wks[:, :, :], rows_of(wk))]
        v_loads = [(bvr[:, :], bv.partition_broadcast(CTX)), (wvs[:, :, :], rows_of(wv))]
        if ctx_mask is not None:
            v_loads.insert(0, (mi[:, :, :], ctx_mask.partition_broadcast(P)))
        with nc.Block() as block:

            @block.sync
            def _(sp):
                for dst, src in k_loads:
                    sp.dma_start(dst, src, allow_slow_non_contiguous=True).then_inc(k_loaded, 16)
                for dst, src in v_loads:
                    sp.dma_start(dst, src).then_inc(v_loaded, 16)
                splitter.sync(sp)

            @block.gpsimd
            def _(pool):
                for h in kd:
                    pool.memset(h[:, :, :].bitcast(F32), 0.0).then_inc(zeroed, 1)
                pool.wait_ge(zeroed, 2)

            @block.tensor
            def _(pe):
                pe.wait_ge(k_loaded, 16 * len(k_loads))
                for b in range(B):
                    for c in range(KC):
                        last = pe.transpose(psum[:, b, c * CTX:(c + 1) * CTX], cn[:, b, c * P:(c + 1) * P],
                                            ident[0:CTX, 0:CTX])
                    last.then_inc(made, 1)
                pe.wait_ge(read, B)
                for o in range(NG):
                    if o >= 2:
                        pe.wait_ge(built, (o - 1) * B * HG)
                    for c in range(KC):
                        last = pe.matmul(psum[:, 2 + o % 2, 0:B * CTX], wks[:, c, o * P:(o + 1) * P],
                                         ct[:, c, :, :].rearrange("p b s -> p (b s)"), start=c == 0,
                                         stop=c == KC - 1)
                    last.then_inc(made, 1)
                pe.wait_ge(v_loaded, 16 * len(v_loads))
                for b in range(B):
                    for g in range(VB):
                        for c in range(KC):
                            last = pe.matmul(psum[0:CTX, 4 + b * VB + g, :], ct[:, c, b, :],
                                             wvs[:, c, g * BANK:(g + 1) * BANK], start=c == 0, stop=c == KC - 1)
                        last.then_inc(made, 1)

            @block.scalar
            def _(act):
                act.wait_ge(zeroed, 2)
                act.wait_ge(k_loaded, 16 * len(k_loads))
                for o in range(NG):
                    act.wait_ge(made, B + o + 1)
                    for b in range(B):
                        for h in range(HG):
                            rows = slice(h * hd, (h + 1) * hd)
                            act.activation(kd[0][rows, b * NG + o, h * CTX:(h + 1) * CTX],
                                           psum[rows, 2 + o % 2, b * CTX:(b + 1) * CTX], ACT.Identity,
                                           bias=bkc[rows, o:o + 1]).then_inc(hi_done, 1)
                splitter.scalar(act)

            @block.vector
            def _(dve):
                dve.wait_ge(zeroed, 2)
                dve.wait_ge(k_loaded, 16 * len(k_loads))
                for b in range(B):
                    dve.wait_ge(made, b + 1)
                    dve.tensor_copy(ct[:, :, b, :], psum[:, b, 0:KC * CTX].rearrange(
                        "p (c s) -> p c s", s=CTX)).then_inc(read, 1)
                n = 0
                for o in range(NG):
                    dve.wait_ge(hi_done, (o + 1) * B * HG)
                    for b in range(B):
                        for h in range(HG):
                            rows = slice(h * hd, (h + 1) * hd)
                            n += 1
                            dst = kd[1][rows, b * NG + o, h * CTX:(h + 1) * CTX]
                            dve.scalar_tensor_tensor(
                                dst, psum[rows, 2 + o % 2, b * CTX:(b + 1) * CTX], bkc[rows, o:o + 1],
                                kd[0][rows, b * NG + o, h * CTX:(h + 1) * CTX].bitcast(F32),
                                ALU.add, ALU.subtract).then_inc(built, 1)
                k = B
                dve.wait_ge(v_loaded, 16 * len(v_loads))
                for b in range(B):
                    for g in range(VB):
                        dve.wait_ge(made, B + NG + b * VB + g + 1)
                        hb = BANK // hd
                        dve.tensor_tensor(
                            vc[:, b * heads + g * hb:b * heads + (g + 1) * hb, :],
                            psum[0:CTX, 4 + b * VB + g, :].rearrange("p (h d) -> p h d", d=hd),
                            bvr[:, g * BANK:(g + 1) * BANK].rearrange("p (h d) -> p h d", d=hd),
                            ALU.add).then_inc(read, 1)
                        k += 1
                if ctx_mask is not None:
                    dve.tensor_scalar(mrow[:, :, :], mi[:, :, :], 0.0, -BIG, ALU.is_equal, ALU.mult).then_inc(read, 1)
                    k += 1
                splitter.vector(dve)
                dve.wait_ge(read, k)
                dve.wait_ge(built, n)




def feed(nc, psum, consts, x, w1, b1, w2, b2, gain, shift, out):
    ident, half = consts
    T = 2
    CH = T * P
    ROUNDS = TOK // CH
    NF = FF // P
    NR = 4
    with ExitStack() as ctx:
        st = Stage(nc, ctx, "feed")
        wa, wb = st.halves("w1", [P, KC, FF]), st.halves("w2", [P, NF, D])
        split_weights(nc, "feed_w", [
            *((rows_of(w1)[:, j:j + 1, :], wa[0][:, j:j + 1, :], wa[1][:, j:j + 1, :]) for j in range(KC)),
            *((rows_of(w2)[:, j:j + 4, :], wb[0][:, j:j + 4, :], wb[1][:, j:j + 4, :]) for j in range(0, NF, 4))])
        b1c = st.sb("b1", [P, NF])
        xn = st.sb("x", [P, T, D])
        xt = st.halves("xt", [P, KC, CH])
        hf = st.sb("hidden", [P, NR, CH])
        ht = st.halves("ht", [P, NF, CH])
        tail = Tail(st, T, x, out, b2, gain, shift, half)
        banks = st.banks(psum, [f"h{o}" for o in range(NF)] + [f"x{t}" for t in range(T)]
                         + [f"y{t}" for t in range(T)])
        b1_in, x_in, xt_hi = st.count("b1_in", 16), st.count("x_in", 16), st.count("xt_hi")
        h_hi, h_split = st.count("hidden_hi"), st.count("hidden_split", ahead=NR)

        def steps(eng, one):
            one(0, True, False)
            with eng.Fori(1, ROUNDS) as k:
                one(k, True, True)
            one(ROUNDS, False, True)

        with nc.Block() as block:

            @block.sync
            def _(sp):
                sp.dma_start(b1c[:, :], b1.rearrange("(c p) -> p c", p=P), allow_slow_non_contiguous=True).then_inc(
                    b1_in.sem, 16)

                def load(r, _):
                    sp.wait_ge(banks.ready, banks.made_before(r, f"x{T - 1}"))
                    sp.dma_start(xn[:, :, :], tokens_of(x, r * CH, T)).then_inc(x_in.sem, 16)

                tail.run_sync(sp, ROUNDS, load, lead=1)

            @block.tensor
            def _(pe):
                pe.sem_inc(banks.ready, len(banks.names))
                for sem in banks.read:
                    pe.sem_inc(sem, 1)

                def one(k, x_t, layers):
                    if layers:
                        for t in range(T):
                            pe.wait_ge(banks.read_of(f"x{t}"), banks.drained(k - 1, f"x{t}"))
                        for o in range(NF):
                            pe.wait_ge(banks.read_of(f"h{o}"), banks.free(k, f"h{o}"))
                            for c in range(KC):
                                last = product(pe, banks.bank(f"h{o}")[:, 0:CH],
                                               [h[:, c, o * P:(o + 1) * P] for h in wa],
                                               [h[:, c, :] for h in xt], c == 0, c == KC - 1)
                            last.then_inc(banks.ready, 1)
                    else:
                        skip(pe, banks, k, [f"h{o}" for o in range(NF)])
                    if x_t:
                        pe.wait_ge(x_in.sem, x_in.done(k))
                        for t in range(T):
                            pe.wait_ge(banks.read_of(f"x{t}"), banks.free(k, f"x{t}"))
                            for c in range(KC):
                                last = pe.transpose(banks.bank(f"x{t}")[:, c * P:(c + 1) * P],
                                                    xn[:, t, c * P:(c + 1) * P], ident[:, :])
                            last.then_inc(banks.ready, 1)
                    else:
                        skip(pe, banks, k, [f"x{t}" for t in range(T)])
                    if layers:
                        for t in range(T):
                            pe.wait_ge(banks.read_of(f"y{t}"), banks.free(k, f"y{t}"))
                            for o in range(NF):
                                if t == 0:
                                    pe.wait_ge(h_split.sem, h_split.done((k - 1) * NF + o))
                                last = product(pe, banks.bank(f"y{t}"), [h[:, o, t * P:(t + 1) * P] for h in ht],
                                               [h[:, o, :] for h in wb], o == 0, o == NF - 1)
                            last.then_inc(banks.ready, 1)
                    else:
                        skip(pe, banks, k, [f"y{t}" for t in range(T)])

                steps(pe, one)

            @block.scalar
            def _(act):
                act.wait_ge(b1_in.sem, b1_in.done(0))

                def one(k, x_t, layers):
                    if layers:
                        for o in range(NF):
                            act.wait_ge(banks.ready, banks.made(k, f"h{o}"))
                            act.wait_ge(h_split.sem, h_split.room((k - 1) * NF + o, NR))
                            act.activation(hf[:, o % NR, :], banks.bank(f"h{o}")[:, 0:CH], ACT.Relu,
                                           bias=b1c[:, o:o + 1]).then_inc(banks.read_of(f"h{o}"), 1)
                    if x_t:
                        for t in range(T):
                            act.wait_ge(banks.ready, banks.made(k, f"x{t}"))
                            act.activation(xt[0][:, :, t * P:(t + 1) * P],
                                           banks.bank(f"x{t}").rearrange("p (c q) -> p c q", q=P),
                                           ACT.Copy).then_inc(xt_hi.sem, 1)

                steps(act, one)

            @block.vector
            def _(dve):
                tail.start_dve(dve)
                dve.sem_inc(h_split.sem, h_split.start)

                def one(k, x_t, layers):
                    if layers:
                        dve.wait_ge(banks.ready, banks.made_before(k, f"y{T - 1}"))
                        for o in range(NF):
                            dve.wait_ge(banks.read_of(f"h{o}"), banks.drained(k, f"h{o}"))
                            dve.tensor_copy(ht[0][:, o, :], hf[:, o % NR, :]).then_inc(h_hi.sem, 1)
                            dve.wait_ge(h_hi.sem, h_hi.done((k - 1) * NF + o))
                            dve.tensor_tensor(ht[1][:, o, :], hf[:, o % NR, :], ht[0][:, o, :].bitcast(F32),
                                              ALU.subtract).then_inc(h_split.sem, 1)
                    if x_t:
                        for t in range(T):
                            dve.wait_ge(xt_hi.sem, xt_hi.done(k * T + t))
                            dve.tensor_tensor(xt[1][:, :, t * P:(t + 1) * P],
                                              banks.bank(f"x{t}").rearrange("p (c q) -> p c q", q=P),
                                              xt[0][:, :, t * P:(t + 1) * P].bitcast(F32),
                                              ALU.subtract).then_inc(banks.read_of(f"x{t}"), 1)
                    if layers:
                        for t in range(T):
                            tail.dve_sum(dve, k - 1, t, banks, f"y{t}", k)
                        for t in range(T):
                            tail.dve_norm(dve, k - 1, t)

                steps(dve, one)

            @block.gpsimd
            def _(pool):
                tail.start_pool(pool)
                with pool.Fori(0, ROUNDS) as r:
                    for t in range(T):
                        tail.pool_bias(pool, r, t)
                    for t in range(T):
                        tail.pool_rstd(pool, r, t)
                    for t in range(T):
                        tail.pool_finish(pool, r, t)




def build(nc, a, out):
    def scratch(name, shape, dt=F32):
        return nc.dram_tensor(name, shape, dt, kind="Internal").ap()

    halves = [scratch(f"{n}_halves", (2, B * D, S)) for n in "qk"]
    v_dram = scratch("v_ones", (TOK, H0 * (HD0 + 1)))
    bias_dram = scratch("mask_bias", (S, S), BF16)
    att_dram, sums_dram, inverse_dram = (scratch(n, (B * k, S)) for n, k in (
        ("attention", D), ("weight_sums", H0), ("inverse_sums", H0)))
    x1, x2, x3 = (scratch(f"x_{n}", (TOK, D)) for n in ("joined", "crossed", "fed"))
    x = a["x"].rearrange("b s d -> (b s) d")
    layer = {k[9:]: v for k, v in a.items() if k.startswith("L0_xattn_")}
    second = {k[9:]: v for k, v in a.items() if k.startswith("L1_xattn_")}

    with ExitStack() as ctx:
        psum = ctx.enter_context(nc.psum_tensor("psum", [P, 8, BANK], F32))
        ident, half, ones = make_constants(nc, ctx)
        consts = (ident, half)
        with ExitStack() as inner:
            st = Stage(nc, inner, "window")
            open_max = st.sb("open_max", [P, S // P, S // KEYS])
            choice = st.sb("choice", [1, 2], I32)
            project(nc, psum, ident, x, a["mask_SxS_ik1"], [layer[f"{n}_w"] for n in "qkv"],
                    [layer[f"{n}_b"] for n in "qkv"], halves, v_dram, bias_dram, open_max)
            choose_window(nc, psum, ones, open_max, choice)
            one_block = nc.values_load(choice[:, 0:1], min_val=0, max_val=1)
            block = nc.values_load(choice[:, 1:2], min_val=0, max_val=S // KEYS - 1)
            with nc.If(one_block):
                attend(nc, psum, ident, halves, v_dram, bias_dram, att_dram, sums_dram, 1, block)
            with nc.Else():
                attend(nc, psum, ident, halves, v_dram, bias_dram, att_dram, sums_dram,
                       S // KEYS, 0)
        join(nc, psum, consts, att_dram, sums_dram, inverse_dram, x, x1, layer["o_w"], layer["o_b"],
             layer["ln1_g"], layer["ln1_b"])
        cross(nc, psum, consts, "cross", H0, HD0, x1, a["ctx_1024"], None, layer["cq_w"], layer["cq_b"],
              layer["ck_w"], layer["ck_b"], layer["cv_w"], layer["cv_b"], layer["co_w"], layer["co_b"],
              layer["ln2_g"], layer["ln2_b"], x2)
        feed(nc, psum, consts, x2, layer["lin1_w"], layer["lin1_b"], layer["lin2_w"], layer["lin2_b"],
             layer["ln3_g"], layer["ln3_b"], x3)
        cross(nc, psum, consts, "second", H1, HD1, x3, a["ctx_1024"], a["mask_BxS2_ik0"], second["Wq"],
              second["bq"], second["Wk"], second["bk"], second["Wv"], second["bv"], second["Wo"], second["bo"],
              second["gamma"], second["beta"], out)


def kernel(**inputs):
    import numpy as np
    import concourse.bacc as bacc
    from concourse.bass_utils import run_bass_kernel_spmd

    nc = bacc.Bacc("TRN2", target_bir_lowering=False, num_devices=1)
    arrays = {f"in_{name}": np.ascontiguousarray(a) for name, a in inputs.items()}
    given = {name: nc.dram_tensor(f"in_{name}", arrays[f"in_{name}"].shape,
                                  mybir.dt.from_np(arrays[f"in_{name}"].dtype), kind="ExternalInput").ap()
             for name in inputs}
    out = nc.dram_tensor("out", (B, S, D), F32, kind="ExternalOutput").ap()
    build(nc, given, out.rearrange("b s d -> (b s) d"))
    result = run_bass_kernel_spmd(nc, [arrays], core_ids=[0])
    return result.results[0]["out"]
```
